# Optimizing a Trainium2 kernel written in Bass

```python
import numpy as np
import jax
import jax.numpy as jnp

def _softmax(x, axis=-1):
    return jax.nn.softmax(x, axis=axis)

def _gelu(x):
    return jax.nn.gelu(x, approximate=True)

def _silu(x):
    return jax.nn.silu(x)

def _sigmoid(x):
    return jax.nn.sigmoid(x)

def _layernorm(x, axis=-1, eps=1e-05):
    m = jnp.mean(x, axis=axis, keepdims=True)
    v = jnp.var(x, axis=axis, keepdims=True)
    return (x - m) / jnp.sqrt(v + eps)

def _scatter_add(tgt, idx, src, axis=0):
    return tgt.at[idx].add(src)

def _segment_sum(src, seg, n):
    return jax.ops.segment_sum(src, seg, n)
kernel_name = 'mk_xattn_ffn_d2_seqx_r8_bf0592'

def setup_inputs(seed: int=0):
    np.random.seed(seed)
    _w = jnp.asarray

    def _rec_inputs():
        import jax
        import jax.numpy as jnp
        _rk = jax.random.key(seed)
        x = -0.0002928 + 1 * jax.random.normal(jax.random.fold_in(_rk, 1), (32, 64, 128), jnp.float32)
        _lenS = 64 - jax.random.randint(jax.random.fold_in(_rk, 7), (32,), 0, max(1, 64 // 4) + 1, jnp.int32)
        _lenS2 = 64 - jax.random.randint(jax.random.fold_in(_rk, 8), (32,), 0, max(1, 64 // 4) + 1, jnp.int32)
        _ctx_1024P = jax.random.normal(jax.random.fold_in(_rk, 11), (32, 16, 128), jnp.float32)
        _ctx_1024c = jax.random.dirichlet(jax.random.fold_in(_rk, 511), 0.3 * jnp.ones((16,), jnp.float32), (32, 64))
        _ctx_1024t = jnp.einsum('bsk,bkd->bsd', _ctx_1024c, _ctx_1024P)
        _ctx_1024t = _ctx_1024t * jax.lax.rsqrt(jnp.mean(jnp.square(_ctx_1024t)) + 1e-12) * 0.953939
        ctx_1024 = -1.39393e-06 + 0.999914 * (_ctx_1024t + 0.3 * jax.random.normal(jax.random.fold_in(_rk, 611), (32, 64, 128), jnp.float32))
        return (x, ctx_1024)
    x, ctx_1024 = _rec_inputs()

    def _L0_xattn_setup():
        import jax, jax.numpy as jnp
        import numpy as np
        import math
        EMBED_DIM = 128
        NUM_HEADS = 16
        HEAD_DIM = EMBED_DIM // NUM_HEADS
        BLOCK = 64
        SPARSITY = 0.05
        BATCH = 2
        SEQ = 256

        def _block_pattern(seq_len, block_size, sparsity_ratio, is_causal):
            nb = seq_len // block_size
            total = nb * nb
            keep = int(total * (1.0 - sparsity_ratio))
            idx = [(i, i) for i in range(nb)]
            band = max(1, int(math.sqrt(keep - nb) / 2))
            for i in range(nb):
                for o in range(1, band + 1):
                    if i + o < nb:
                        idx.append((i, i + o))
                        if not is_causal:
                            idx.append((i + o, i))
                    if not is_causal and i - o >= 0:
                        idx.append((i, i - o))
            for skip in (2, 4, 8, 16):
                if len(idx) >= keep:
                    break
                for i in range(0, nb - skip, skip):
                    if len(idx) < keep:
                        idx.append((i, i + skip))
                        if not is_causal and len(idx) < keep:
                            idx.append((i + skip, i))
            uniq = sorted(set(idx))
            if is_causal:
                uniq = [(r, c) for r, c in uniq if r >= c]
            uniq = uniq[:keep]
            rows = np.array([r for r, c in uniq], dtype=np.int32)
            cols = np.array([c for r, c in uniq], dtype=np.int32)
            return (rows, cols)
        ROWS, COLS = _block_pattern(SEQ, BLOCK, SPARSITY, is_causal=False)
        rng = jax.random.key(seed)
        ks = jax.random.split(rng, 7)
        wscale = EMBED_DIM ** (-0.5)
        return {'query': jax.random.normal(ks[0], (BATCH, SEQ, EMBED_DIM), jnp.float32), 'key': jax.random.normal(ks[1], (BATCH, SEQ, EMBED_DIM), jnp.float32), 'value': jax.random.normal(ks[2], (BATCH, SEQ, EMBED_DIM), jnp.float32), 'Wq': jax.random.normal(ks[3], (EMBED_DIM, EMBED_DIM), jnp.float32) * wscale, 'Wk': jax.random.normal(ks[4], (EMBED_DIM, EMBED_DIM), jnp.float32) * wscale, 'Wv': jax.random.normal(ks[5], (EMBED_DIM, EMBED_DIM), jnp.float32) * wscale, 'Wo': jax.random.normal(ks[6], (EMBED_DIM, EMBED_DIM), jnp.float32) * wscale}
    _L0_xattn_all = _L0_xattn_setup()
    _L0_xattn_in = {k: v for k, v in _L0_xattn_all.items() if k in ('Wq', 'Wk', 'Wv', 'Wo')}
    del _L0_xattn_all

    def _L0_ffn_setup():
        import jax, jax.numpy as jnp
        import numpy as np
        HIDDEN_SIZE = 128
        NUM_EXPERTS = 8
        MOE_INTERMEDIATE_SIZE = 176
        NUM_EXPERTS_PER_TOK = 2
        SHARED_EXPERT_INTERMEDIATE_SIZE = 352
        B, T = (2, 128)
        W_SCALE = 0.02
        key = jax.random.key(seed)
        ks = jax.random.split(key, 8)
        H, E, I, SI = (HIDDEN_SIZE, NUM_EXPERTS, MOE_INTERMEDIATE_SIZE, SHARED_EXPERT_INTERMEDIATE_SIZE)
        return {'x': jax.random.normal(ks[0], (B, T, H), jnp.float32), 'gate_w': jax.random.normal(ks[1], (E, H), jnp.float32) * W_SCALE, 'experts_gate_up': jax.random.normal(ks[2], (E, 2 * I, H), jnp.float32) * W_SCALE, 'experts_down': jax.random.normal(ks[3], (E, H, I), jnp.float32) * W_SCALE, 'shared_gate_w': jax.random.normal(ks[4], (SI, H), jnp.float32) * W_SCALE, 'shared_up_w': jax.random.normal(ks[5], (SI, H), jnp.float32) * W_SCALE, 'shared_down_w': jax.random.normal(ks[6], (H, SI), jnp.float32) * W_SCALE, 'shared_expert_gate_w': jax.random.normal(ks[7], (1, H), jnp.float32) * W_SCALE}
    _L0_ffn_all = _L0_ffn_setup()
    _L0_ffn_in = {k: v for k, v in _L0_ffn_all.items() if k in ('gate_w', 'experts_gate_up', 'experts_down', 'shared_gate_w', 'shared_up_w', 'shared_down_w', 'shared_expert_gate_w')}
    del _L0_ffn_all

    def _L1_xattn_setup():
        import jax, jax.numpy as jnp
        import numpy as np
        B, SQ, SK, D = (4, 256, 256, 128)
        key = jax.random.key(seed)
        ks = jax.random.split(key, 8)
        s = 1.0 / np.sqrt(D)
        return {'input_seq': jax.random.normal(ks[0], (B, SQ, D), jnp.float32), 'condition_seq': jax.random.normal(ks[1], (B, SK, D), jnp.float32), 'Wq': jax.random.normal(ks[2], (D, D), jnp.float32) * s, 'bq': jnp.zeros((D,), jnp.float32), 'Wk': jax.random.normal(ks[3], (D, D), jnp.float32) * s, 'bk': jnp.zeros((D,), jnp.float32), 'Wv': jax.random.normal(ks[4], (D, D), jnp.float32) * s, 'bv': jnp.zeros((D,), jnp.float32)}
    _L1_xattn_all = _L1_xattn_setup()
    _L1_xattn_in = {k: v for k, v in _L1_xattn_all.items() if k in ('Wq', 'bq', 'Wk', 'bk', 'Wv', 'bv')}
    del _L1_xattn_all

    def _L1_ffn_setup():
        import jax, jax.numpy as jnp
        import numpy as np
        MANT_BITS = 8
        _PWL_X = jnp.linspace(-4.0, 4.0, 33, dtype=jnp.float32)
        _PWL_Y = 0.5 * _PWL_X * (1.0 + jax.lax.erf(_PWL_X / jnp.sqrt(jnp.float32(2.0))))

        def float2fix(x, mantissa_bits):
            s = jnp.float32(2.0 ** mantissa_bits)
            q = jnp.round(x * s) / s
            return x + jax.lax.stop_gradient(q - x)

        def pwlin_gelu_basic(x, mantissa_bits_in, mantissa_bits_out):
            xq = float2fix(x, mantissa_bits_in)
            y = jnp.interp(xq, _PWL_X, _PWL_Y)
            y = jnp.where(xq > 4.0, xq, jnp.where(xq < -4.0, jnp.float32(0.0), y))
            return float2fix(y, mantissa_bits_out)
        key = jax.random.key(seed)
        k_x, k_w1, k_b1, k_w2, k_b2 = jax.random.split(key, 5)
        dim, ff_dim = (128, 512)
        B, S = (32, 64)
        sc1 = 1.0 / np.sqrt(dim)
        sc2 = 1.0 / np.sqrt(ff_dim)
        return {'x': jax.random.normal(k_x, (B, S, dim), dtype=jnp.float32), 'w1': jax.random.uniform(k_w1, (dim, ff_dim), jnp.float32, -sc1, sc1), 'b1': jax.random.uniform(k_b1, (ff_dim,), jnp.float32, -sc1, sc1), 'w2': jax.random.uniform(k_w2, (ff_dim, dim), jnp.float32, -sc2, sc2), 'b2': jax.random.uniform(k_b2, (dim,), jnp.float32, -sc2, sc2)}
    _L1_ffn_all = _L1_ffn_setup()
    _L1_ffn_in = {k: v for k, v in _L1_ffn_all.items() if k in ('w1', 'b1', 'w2', 'b2')}
    del _L1_ffn_all
    return {'x': x, 'ctx_1024': ctx_1024, 'L0_xattn_Wq': _L0_xattn_in['Wq'], 'L0_xattn_Wk': _L0_xattn_in['Wk'], 'L0_xattn_Wv': _L0_xattn_in['Wv'], 'L0_xattn_Wo': _L0_xattn_in['Wo'], 'L0_ffn_gate_w': _L0_ffn_in['gate_w'], 'L0_ffn_experts_gate_up': _L0_ffn_in['experts_gate_up'], 'L0_ffn_experts_down': _L0_ffn_in['experts_down'], 'L0_ffn_shared_gate_w': _L0_ffn_in['shared_gate_w'], 'L0_ffn_shared_up_w': _L0_ffn_in['shared_up_w'], 'L0_ffn_shared_down_w': _L0_ffn_in['shared_down_w'], 'L0_ffn_shared_expert_gate_w': _L0_ffn_in['shared_expert_gate_w'], 'L1_xattn_Wq': _L1_xattn_in['Wq'], 'L1_xattn_bq': _L1_xattn_in['bq'], 'L1_xattn_Wk': _L1_xattn_in['Wk'], 'L1_xattn_bk': _L1_xattn_in['bk'], 'L1_xattn_Wv': _L1_xattn_in['Wv'], 'L1_xattn_bv': _L1_xattn_in['bv'], 'L1_ffn_w1': _L1_ffn_in['w1'], 'L1_ffn_b1': _L1_ffn_in['b1'], 'L1_ffn_w2': _L1_ffn_in['w2'], 'L1_ffn_b2': _L1_ffn_in['b2']}

def reference(x, ctx_1024, L0_xattn_Wq, L0_xattn_Wk, L0_xattn_Wv, L0_xattn_Wo, L0_ffn_gate_w, L0_ffn_experts_gate_up, L0_ffn_experts_down, L0_ffn_shared_gate_w, L0_ffn_shared_up_w, L0_ffn_shared_down_w, L0_ffn_shared_expert_gate_w, L1_xattn_Wq, L1_xattn_bq, L1_xattn_Wk, L1_xattn_bk, L1_xattn_Wv, L1_xattn_bv, L1_ffn_w1, L1_ffn_b1, L1_ffn_w2, L1_ffn_b2):
    import jax
    import jax.numpy as jnp

    def _L0_xattn_ref(query, key, value, Wq, Wk, Wv, Wo):
        import jax, jax.numpy as jnp
        import numpy as np
        import math
        EMBED_DIM = 128
        NUM_HEADS = 16
        HEAD_DIM = EMBED_DIM // NUM_HEADS
        BLOCK = 64
        SPARSITY = 0.05
        BATCH = 2
        SEQ = 256

        def _block_pattern(seq_len, block_size, sparsity_ratio, is_causal):
            nb = seq_len // block_size
            total = nb * nb
            keep = int(total * (1.0 - sparsity_ratio))
            idx = [(i, i) for i in range(nb)]
            band = max(1, int(math.sqrt(keep - nb) / 2))
            for i in range(nb):
                for o in range(1, band + 1):
                    if i + o < nb:
                        idx.append((i, i + o))
                        if not is_causal:
                            idx.append((i + o, i))
                    if not is_causal and i - o >= 0:
                        idx.append((i, i - o))
            for skip in (2, 4, 8, 16):
                if len(idx) >= keep:
                    break
                for i in range(0, nb - skip, skip):
                    if len(idx) < keep:
                        idx.append((i, i + skip))
                        if not is_causal and len(idx) < keep:
                            idx.append((i + skip, i))
            uniq = sorted(set(idx))
            if is_causal:
                uniq = [(r, c) for r, c in uniq if r >= c]
            uniq = uniq[:keep]
            rows = np.array([r for r, c in uniq], dtype=np.int32)
            cols = np.array([c for r, c in uniq], dtype=np.int32)
            return (rows, cols)
        ROWS, COLS = _block_pattern(SEQ, BLOCK, SPARSITY, is_causal=False)
        B, S, E = query.shape
        nb = S // BLOCK
        scale = HEAD_DIM ** (-0.5)

        def proj_blocks(x, W):
            h = (x @ W.T).reshape(B, S, NUM_HEADS, HEAD_DIM).transpose(0, 2, 1, 3)
            return h.reshape(B, NUM_HEADS, nb, BLOCK, HEAD_DIM)
        qb = proj_blocks(query, Wq)
        kb = proj_blocks(key, Wk)
        vb = proj_blocks(value, Wv)
        rows = jnp.asarray(ROWS)
        cols = jnp.asarray(COLS)
        qg = qb[:, :, rows]
        kg = kb[:, :, cols]
        vg = vb[:, :, cols]
        scores = jnp.einsum('bhpqd,bhpkd->bhpqk', qg, kg) * scale
        attn = jax.nn.softmax(scores, axis=-1)
        ob = jnp.einsum('bhpqk,bhpkd->bhpqd', attn, vg)
        acc = jax.ops.segment_sum(ob.transpose(2, 0, 1, 3, 4), rows, num_segments=nb)
        out = acc.transpose(1, 2, 0, 3, 4).reshape(B, NUM_HEADS, S, HEAD_DIM)
        out = out.transpose(0, 2, 1, 3).reshape(B, S, E)
        return out @ Wo.T

    def _L0_ffn_ref(x, gate_w, experts_gate_up, experts_down, shared_gate_w, shared_up_w, shared_down_w, shared_expert_gate_w):
        import jax, jax.numpy as jnp
        import numpy as np
        HIDDEN_SIZE = 128
        NUM_EXPERTS = 8
        MOE_INTERMEDIATE_SIZE = 176
        NUM_EXPERTS_PER_TOK = 2
        SHARED_EXPERT_INTERMEDIATE_SIZE = 352
        B, T = (2, 128)
        W_SCALE = 0.02
        Bx, Tx, H = x.shape
        E = gate_w.shape[0]
        I = experts_down.shape[2]
        x_flat = x.reshape(Bx * Tx, H)
        logits = x_flat @ gate_w.T
        scores = jax.nn.softmax(logits, axis=-1)
        _, topk_ids = jax.lax.top_k(scores, NUM_EXPERTS_PER_TOK)
        in_topk = jax.nn.one_hot(topk_ids, E, dtype=x.dtype).sum(axis=1)
        w = scores * in_topk
        gu = jnp.einsum('nh,eih->nei', x_flat, experts_gate_up)
        g, u = (gu[..., :I], gu[..., I:])
        h = jax.nn.silu(g) * u
        expert_out = jnp.einsum('nei,ehi->neh', h, experts_down)
        out = jnp.einsum('neh,ne->nh', expert_out, w)
        shared = jax.nn.silu(x_flat @ shared_gate_w.T) * (x_flat @ shared_up_w.T) @ shared_down_w.T
        shared_weight = jax.nn.sigmoid(x_flat @ shared_expert_gate_w.T)
        out = out + shared_weight * shared
        return out.reshape(Bx, Tx, H)

    def _L1_xattn_ref(input_seq, condition_seq, Wq, bq, Wk, bk, Wv, bv):
        import jax, jax.numpy as jnp
        import numpy as np
        B, SQ, SK, D = (4, 256, 256, 128)
        q = jnp.einsum('bsd,ed->bse', input_seq, Wq) + bq
        k = jnp.einsum('btd,ed->bte', condition_seq, Wk) + bk
        v = jnp.einsum('btd,ed->bte', condition_seq, Wv) + bv
        scores = jnp.einsum('bse,bte->bst', q, k)
        attn = jax.nn.softmax(scores, axis=-1)
        attended = jnp.einsum('bst,bte->bse', attn, v)
        return attended

    def _L1_ffn_ref(x, w1, b1, w2, b2):
        import jax, jax.numpy as jnp
        import numpy as np
        MANT_BITS = 8
        _PWL_X = jnp.linspace(-4.0, 4.0, 33, dtype=jnp.float32)
        _PWL_Y = 0.5 * _PWL_X * (1.0 + jax.lax.erf(_PWL_X / jnp.sqrt(jnp.float32(2.0))))

        def float2fix(x, mantissa_bits):
            s = jnp.float32(2.0 ** mantissa_bits)
            q = jnp.round(x * s) / s
            return x + jax.lax.stop_gradient(q - x)

        def pwlin_gelu_basic(x, mantissa_bits_in, mantissa_bits_out):
            xq = float2fix(x, mantissa_bits_in)
            y = jnp.interp(xq, _PWL_X, _PWL_Y)
            y = jnp.where(xq > 4.0, xq, jnp.where(xq < -4.0, jnp.float32(0.0), y))
            return float2fix(y, mantissa_bits_out)
        h = jnp.einsum('bsd,df->bsf', x, w1) + b1
        h = float2fix(h, MANT_BITS)
        h = pwlin_gelu_basic(h, MANT_BITS, MANT_BITS)
        h = float2fix(h, MANT_BITS)
        out = jnp.einsum('bsf,fd->bsd', h, w2) + b2
        return float2fix(out, MANT_BITS)
    x = x + _L0_xattn_ref(_layernorm(x, axis=-1), ctx_1024, ctx_1024, L0_xattn_Wq, L0_xattn_Wk, L0_xattn_Wv, L0_xattn_Wo)
    x = x + _L0_ffn_ref(_layernorm(x, axis=-1), L0_ffn_gate_w, L0_ffn_experts_gate_up, L0_ffn_experts_down, L0_ffn_shared_gate_w, L0_ffn_shared_up_w, L0_ffn_shared_down_w, L0_ffn_shared_expert_gate_w)
    x = x + _L1_xattn_ref(_layernorm(x, axis=-1), ctx_1024, L1_xattn_Wq, L1_xattn_bq, L1_xattn_Wk, L1_xattn_bk, L1_xattn_Wv, L1_xattn_bv)
    x = x + _L1_ffn_ref(_layernorm(x, axis=-1), L1_ffn_w1, L1_ffn_b1, L1_ffn_w2, L1_ffn_b2)
    return x

_drawn_inputs = setup_inputs


def setup_inputs(seed=0):
    import zlib

    import numpy as np

    out = dict(_drawn_inputs(seed))
    spreads = {'L1_xattn_bq': (0.0, 0.1), 'L1_xattn_bk': (0.0, 2.0), 'L1_xattn_bv': (0.0, 0.436)}
    factors = {'L0_ffn_gate_w': 8.0,
     'L0_ffn_experts_gate_up': 8.0,
     'L0_ffn_experts_down': 8.0,
     'L0_ffn_shared_gate_w': 8.0,
     'L0_ffn_shared_up_w': 8.0,
     'L0_ffn_shared_down_w': 8.0,
     'L0_ffn_shared_expert_gate_w': 8.0,
     'L1_ffn_b1': 7.278,
     'L1_ffn_b2': 4.881}
    for name, (base, spread) in spreads.items():
        noise = np.random.default_rng([zlib.crc32(name.encode()), seed]).standard_normal(out[name].shape)
        drawn = base * np.exp(spread * noise) if base else spread * noise
        out[name] = jnp.asarray(drawn.astype(out[name].dtype))
    for name, factor in factors.items():
        out[name] = (out[name] * factor).astype(out[name].dtype)
    return out
```

```python
from contextlib import ExitStack

import numpy as np

import concourse.bass as bass
from concourse import mybir

F32 = mybir.dt.float32
F32R = mybir.dt.float32r
I32 = mybir.dt.int32
ALU = mybir.AluOpType
ACT = mybir.ActivationFunctionType
AX_X = mybir.AxisListType.X

P = 128
BATCH, SEQ = 32, 64
NT = BATCH * SEQ // P
NPAIR = NT // 2
PW = 2 * P
HEADS, HD = 16, 8
NEXP, TOPK = 8, 2
INTER = 176
SHARED = 352
UNITS = NEXP + SHARED // INTER
UW = 2 * INTER
HC = -(-UNITS * INTER // P)
HPAD = HC * P
FF = 512
FC = FF // P
EPS = 1e-5
SCALE0 = HD ** -0.5
REPEAT0 = 3
QUANT = 256.0
KNOT = 64

W_Q0, W_K0, W_K1, W_Q1, W_V, W_UP = 0, 128, 256, 384, 512, 768
W_DOWN = W_UP + FF
W_GATE = W_DOWN + FF
NGATE = 10
W_COLS = W_GATE + NGATE
C_ID, C_WO, C_BV, C_MASK, C_TRI, C_ONES = 0, 128, 256, 384, 388, 452
C_BQ = C_ONES + 64
C_BK, C_B1 = C_BQ + 1, C_BQ + 2
C_COLS = C_B1 + FC + 1
ROUTE_STEPS = 14


def pair(g):
    return bass.ds(g * PW, PW)


def one(t):
    return bass.ds(t, 1)


def after(step, n):
    return not isinstance(step, int) or step >= n


def bank_of(i, u):
    return (i * UNITS + u) % 4


def silu_of(i, v):
    return (i * (UNITS // 2) + v) % 2


class Steps:

    def __init__(self, eng, sem, base=0):
        self.eng, self.sem, self.n = eng, sem, base

    def did(self, ins):
        ins.then_inc(self.sem, 1)
        self.n = self.n + 1

    def wait(self):
        self.eng.wait_ge(self.sem, self.n)


def two_layers(nc, x_d, ctx_d, w_d, gu_d, down_d, const_d, out_d):
    with ExitStack() as ctx:
        def sb(name, shape, dt=F32):
            return ctx.enter_context(nc.sbuf_tensor(name, shape, dt))

        def sem(name):
            return ctx.enter_context(nc.semaphore(name))

        x = sb("x", [P, NT, P])
        const = sb("const", [P, C_COLS])
        w_hi = sb("w_hi", [P, W_COLS], F32R)
        w_lo = sb("w_lo", [P, W_COLS], F32R)
        gu_hi = sb("gu_hi", [P, UNITS * UW], F32R)
        gu_lo = sb("gu_lo", [P, UNITS * UW], F32R)
        down_hi = sb("down_hi", [P, HC * P], F32R)
        down_lo = sb("down_lo", [P, HC * P], F32R)
        k1T = sb("k1T", [P, NT * P])
        v1 = sb("v1", [P, NT, P])
        moments = sb("moments", [P, 2, 6])
        meanvar = sb("meanvar", [P, 2, 2])
        veps = sb("veps", [P, 2])
        mean = sb("mean", [P, NT])
        rstd = sb("rstd", [P, NT])
        minus_half = sb("minus_half", [P, 1])
        xn = sb("xn", [P, 2, 2, P])
        xT_hi = sb("xT_hi", [P, 2, PW], F32R)
        xT_lo = sb("xT_lo", [P, 2, PW], F32R)

        AR = 2 * HC * PW
        arena_r = sb("arena_r", [P, AR], F32R)
        AF = 20864
        arena_f = sb("arena_f", [P, AF])

        def carve(arena, sizes):
            at, out = 0, []
            for n in sizes:
                out.append(arena[:, at:at + n])
                at += n
            assert at <= arena.shape[1]
            return out

        (k0T, q0T, v0dup, gu_raw, down_raw, kexp_, q_st_, vblk_, prob_, probT_, rden, oT_, ctxT_) = carve(
            arena_f, [NT * P, NT * P, 2 * NT * P, UNITS * UW, HC * P, 2 * 512, 2 * P, 2 * 512, 2 * 1024,
                      2 * 1024, P, 2 * P, 2 * PW])
        v0dup = v0dup.rearrange("p (b f) -> p b f", f=P)
        kexp = kexp_.rearrange("p (s b j k) -> p s b j k", s=2, b=2, j=4)
        q_st = q_st_.rearrange("p (s n) -> p s n", s=2)
        vblk = vblk_.rearrange("p (s b c n) -> p s b c n", s=2, b=2, c=8)
        prob = prob_.rearrange("p (s n) -> p s n", s=2)
        probT = probT_.rearrange("p (s c n) -> p s c n", s=2, c=8)
        oT = oT_.rearrange("p (s n) -> p s n", s=2)
        ctxT = ctxT_.rearrange("p (s n) -> p s n", s=2)
        wraw = prob_[:, 0:W_COLS]
        ctx_hi_, ctx_lo_ = carve(arena_r, [4 * PW, 4 * PW])
        ctx_hi = ctx_hi_.rearrange("p (s b r n) -> p s b r n", s=2, b=4, r=2)
        ctx_lo = ctx_lo_.rearrange("p (s b r n) -> p s b r n", s=2, b=4, r=2)
        rowmax = sb("rowmax", [P, 2, 4, 4])

        hT_hi, hT_lo = (a.rearrange("p (c n) -> p c n", c=HC) for a in carve(arena_r, [HC * PW] * 2))
        hid_, act_, yT, lgT = carve(arena_f, [2 * HPAD, 2 * 2 * INTER, PW, PW])
        hid = hid_.rearrange("p (s n) -> p s n", s=2)
        silu = act_.rearrange("p (s u n) -> p s u n", s=2, u=2)
        gl = sb("gl", [P, 2, 16])
        gd = sb("gd", [P, 2, 12])
        ge = sb("ge", [P, 2, 12])
        gp = sb("gp", [P, 2, 8])
        beats = sb("beats", [P, 2, 8, 8])
        ties = sb("ties", [P, 2, 8, 8])
        rank = sb("rank", [P, 2, 8])
        wexp = sb("wexp", [P, 2, 2, UNITS])

        q1T_, k1s_, pd_, pblk_, pT_ = carve(arena_f[:, 5120:], [2 * PW, 2 * PW, 2 * P, 2 * PW, 2 * PW])
        q1T = q1T_.rearrange("p (s n) -> p s n", s=2)
        k1s = k1s_.rearrange("p (s n) -> p s n", s=2)
        pdiff = pd_.rearrange("p (s t k) -> p s t k", s=2, t=2)
        pblk = pblk_.rearrange("p (s t k) -> p s t k", s=2, t=2)
        p1T = pT_.rearrange("p (s t k) -> p s t k", s=2, t=2)
        stat1 = sb("stat1", [P, 2, 3, 2])

        n_, base_, frac_, g0_, g1_, y_, oq_ = carve(arena_f[:, 7680:], [2 * 1024] * 6 + [2 * PW])
        (n_i, base_i, frac_i) = (a.bitcast(I32).rearrange("p (s n) -> p s n", s=2) for a in (n_, base_, frac_))
        g_lo = g0_.rearrange("p (s n) -> p s n", s=2)
        g_hi = g1_.rearrange("p (s n) -> p s n", s=2)
        y_i = y_.bitcast(I32).rearrange("p (s n) -> p s n", s=2)
        oq = oq_.rearrange("p (s n) -> p s n", s=2)
        oq_i = oq_.bitcast(I32).rearrange("p (s n) -> p s n", s=2)
        yq_hi_, yq_lo_ = carve(arena_r, [2 * 1024] * 2)
        yq_hi = yq_hi_.rearrange("p (s c n) -> p s c n", s=2, c=FC)
        yq_lo = yq_lo_.rearrange("p (s c n) -> p s c n", s=2, c=FC)
        b_q = sb("b_q", [P, FC + 1])
        quarter = sb("quarter", [P, 1])

        ident = const[:, C_ID:C_ID + P]
        woT = const[:, C_WO:C_WO + P]
        bv_rows = const[:, C_BV:C_BV + P]
        tri = const[:, C_TRI:C_TRI + 64].rearrange("p (i j) -> p i j", i=8)
        ones32 = const[:, C_ONES:C_ONES + 64].rearrange("p (a n) -> p a n", a=2)

        ps = ctx.enter_context(nc.psum_tensor("ps", [P, 8, 512], F32))

        S = {}
        for name in """
            ctx_in0 ctx_in1 w_in const_in x_in gu_in down_in out_done
            held consts_set b_scaled w_split ctx_split moments0 stats0 veps0 rstd0 xn_ready
            xT_done xT_hi_ready xT_lo_ready k0_done k0_kept k1_done k1_kept v_done v0_kept v1_kept q_done q_kept
            vblk_zero kq_staged vblk_staged scores_done rowmax_ready diff_ready exp_done probT_done probT_kept
            pv_done rden_ready oT_ready wo_done x1_ready w_high w_low moments1 stats1 veps1 rstd1
            hid_zero gxn_ready gxT_done gxT_hi gxT_lo glT_done glT_kept gl_done gl_diff gexp_done route_steps
            unit_done silu_done hid_ready hT_done hT_hi_ready hT_lo_ready down_done yT_kept y_done x2_ready
            moments2 stats2 veps2 rstd2
            pblk_zero axn_ready axT_done axT_hi axT_lo aq_done aq_kept ak_staged as_done adiff aexp_done apT_done
            apT_kept ao_done astat x3_ready moments3 stats3 veps3 rstd3
            fxn_ready fxT_done fxT_hi fxT_lo up_done n_ready base_ready frac_ready glo_done ghi_done slope_ready
            rise_ready y_ready yq_hi_ready yq_lo_ready fd_done oq_int oq_ready fo_done x4_ready
        """.split():
            S[name] = sem(name)

        def hold(eng, name, value):
            eng.wait_ge(S[name], value)
            eng.sem_inc(S["held"], 1)

        def split3(pe, out, w, m_hi, m_lo, n=P, first=True):
            pe.matmul(out, w_hi[:, w:w + n], m_hi, start=first, stop=False)
            pe.matmul(out, w_lo[:, w:w + n], m_hi, start=False, stop=False)
            return pe.matmul(out, w_hi[:, w:w + n], m_lo, start=False, stop=True)

        block = ctx.enter_context(nc.Block())

        @block.sync
        def _(sp):
            sp.dma_start(wraw[:], w_d).then_inc(S["w_in"], 16)
            sp.dma_start(const[:], const_d).then_inc(S["const_in"], 16)
            for s in range(2):
                sp.dma_start(ctxT[:, s], ctx_d[:, pair(s)]).then_inc(S[f"ctx_in{s}"], 16)
            sp.dma_start(x[:], x_d).then_inc(S["x_in"], 16)
            sp.dma_start(gu_raw, gu_d).then_inc(S["gu_in"], 16)
            sp.dma_start(down_raw, down_d).then_inc(S["down_in"], 16)
            for g in range(2, NPAIR):
                sp.wait_ge(S["ctx_split"], 2 * (g - 1))
                sp.dma_start(ctxT[:, g % 2], ctx_d[:, pair(g)]).then_inc(S[f"ctx_in{g % 2}"], 16)
            for g in range(NPAIR):
                sp.wait_ge(S["x4_ready"], 2 * g + 2)
                sp.dma_start(out_d[:, 2 * g:2 * g + 2, :], x[:, 2 * g:2 * g + 2, :]).then_inc(S["out_done"], 16)
            sp.wait_ge(S["out_done"], 16 * NPAIR)

        @block.tensor
        def _(pe):
            pe.wait_ge(S["w_split"], 2)
            pe.wait_ge(S["const_in"], 16)

            def project(g, s):
                pe.wait_ge(S["xn_ready"], g + 1)
                pe.wait_ge(S["xT_lo_ready"], g + 1)
                pe.wait_ge(S["xT_hi_ready"], g + 1)
                for i in range(2):
                    mm = pe.transpose(ps[:, 0, i * P:(i + 1) * P], xn[:, s, i, :], ident)
                mm.then_inc(S["xT_done"], 1)
                pe.wait_ge(S["ctx_split"], 2 * g + 2)
                pe.wait_ge(S["k0_kept"], g + 1)
                split3(pe, ps[:, 2, 0:PW], W_K0, ctx_hi[:, s, :, 0], ctx_lo[:, s, :, 0]).then_inc(S["k0_done"], 1)
                pe.wait_ge(S["k1_kept"], g + 1)
                split3(pe, ps[:, 3, 0:PW], W_K1, ctx_hi[:, s, :, 0], ctx_lo[:, s, :, 0]).then_inc(S["k1_done"], 1)
                pe.wait_ge(S["v0_kept"], 2 * g + 2)
                pe.wait_ge(S["v1_kept"], 2 * g + 2)
                for i in range(2):
                    for b in range(2):
                        at = (s * 4 + 2 * i + b) * P
                        hi, lo = ctx_hi_[:, at:at + P], ctx_lo_[:, at:at + P]
                        o = ps[:, 4 + 2 * s + i, b * PW:(b + 1) * PW]
                        pe.matmul(o, hi, w_hi[:, W_V:W_V + PW], start=True, stop=False)
                        pe.matmul(o, hi, w_lo[:, W_V:W_V + PW], start=False, stop=False)
                        mm = pe.matmul(o, lo, w_hi[:, W_V:W_V + PW], start=False, stop=True)
                    mm.then_inc(S["v_done"], 1)
                pe.wait_ge(S["xT_lo_ready"], g + 2)
                pe.wait_ge(S["xT_hi_ready"], g + 2)
                pe.wait_ge(S["q_kept"], g + 1)
                split3(pe, ps[:, 1, 0:PW], W_Q0, xT_hi[:, s], xT_lo[:, s]).then_inc(S["q_done"], 1)

            with pe.Fori(0, NPAIR // 2) as r:
                for s in range(2):
                    project(r * 2 + s, s)

            def scores(t, s):
                pe.wait_ge(S["kq_staged"], 2 * t + 2)
                if after(t, 1):
                    pe.wait_ge(S["diff_ready"], t)
                for h4 in range(4):
                    rows = slice(32 * h4, 32 * h4 + 32)
                    for b in range(2):
                        mm = pe.matmul(ps[b * SEQ:(b + 1) * SEQ, h4, 0:256],
                                       q_st[rows, s, b * SEQ:(b + 1) * SEQ],
                                       kexp_[rows, (2 * s + b) * 256:(2 * s + b + 1) * 256], start=True, stop=True)
                mm.then_inc(S["scores_done"], 1)

            def turn(t, s):
                pe.wait_ge(S["exp_done"], t + 1)
                for half in range(2):
                    if after(t, 1):
                        pe.wait_ge(S["probT_kept"], 2 * t - 1 + half)
                    for c in range(4):
                        cc = 4 * half + c
                        mm = pe.transpose(ps[:, 4 + half, c * P:(c + 1) * P],
                                          prob[:, s, cc * P:(cc + 1) * P], ident)
                    mm.then_inc(S["probT_done"], 1)

            def values(t, s):
                pe.wait_ge(S["probT_kept"], 2 * t + 2)
                pe.wait_ge(S["vblk_staged"], 2 * t + 2)
                if after(t, 1):
                    pe.wait_ge(S["oT_ready"], t)
                for b in range(2):
                    q = slice(b * SEQ, (b + 1) * SEQ)
                    for kind in range(2):
                        for par in range(2):
                            for j in range(4):
                                w = vblk[:, s, b, 2 * j + par] if kind == 0 else ones32[:, par]
                                at = kind * P + b * SEQ
                                mm = pe.matmul(ps[32 * j:32 * j + 32, 6, at:at + SEQ], w,
                                               probT[:, s, 2 * j + par, q], start=(par == 0), stop=(par == 1))
                mm.then_inc(S["pv_done"], 1)

            def out_proj(t, s):
                pe.wait_ge(S["oT_ready"], t + 1)
                if after(t, 1):
                    pe.wait_ge(S["x1_ready"], t)
                pe.matmul(ps[:, 7, 0:P], oT[:, s], woT, start=True, stop=True).then_inc(S["wo_done"], 1)

            def attend(t, s):
                scores(t, s)
                turn(t - 1, 1 - s)
                values(t - 2, s)
                out_proj(t - 3, 1 - s)

            for name, n in (("xT_hi_ready", NPAIR + 1), ("xT_lo_ready", NPAIR + 1), ("k0_kept", NPAIR + 1),
                            ("k1_kept", NPAIR + 1), ("v0_kept", NT + 4), ("v1_kept", NT + 4), ("q_kept", NPAIR + 1)):
                pe.wait_ge(S[name], n)
            scores(0, 0)
            scores(1, 1)
            turn(0, 0)
            scores(2, 0)
            turn(1, 1)
            values(0, 0)
            scores(3, 1)
            turn(2, 0)
            values(1, 1)
            out_proj(0, 0)
            with pe.Fori(2, NT // 2) as r:
                for s in range(2):
                    attend(r * 2 + s, s)
            turn(NT - 1, 1)
            values(NT - 2, 0)
            out_proj(NT - 3, 1)
            values(NT - 1, 1)
            out_proj(NT - 2, 0)
            out_proj(NT - 1, 1)

            def route_turn(g, s):
                pe.wait_ge(S["gxn_ready"], g + 1)
                if after(g, 1):
                    pe.wait_ge(S["gl_diff"], 2 * g)
                for i in range(2):
                    mm = pe.transpose(ps[:, 7, i * P:(i + 1) * P], xn[:, s, i, :], ident)
                mm.then_inc(S["gxT_done"], 1)

            def route_logits(g, s):
                pe.wait_ge(S["gxT_hi"], g + 1)
                pe.wait_ge(S["gxT_lo"], g + 1)
                split3(pe, ps[0:NGATE, 7, PW:2 * PW], W_GATE, xT_hi[:, s], xT_lo[:, s], NGATE).then_inc(S["glT_done"], 1)

            def route_back(g):
                hold(pe, "glT_kept", g + 1)
                for i in range(2):
                    mm = pe.transpose(ps[:, 7, i * 16:i * 16 + NGATE], lgT[0:NGATE, i * P:(i + 1) * P],
                                      const[0:NGATE, C_ID:C_ID + NGATE])
                mm.then_inc(S["gl_done"], 1)

            def unit(t, s, i, u):
                n = t * UNITS + u
                if after(t, 1) or u >= 4:
                    pe.wait_ge(S["hid_ready"], n - 3)
                for k, (a, b) in enumerate(((xT_hi, gu_hi), (xT_hi, gu_lo), (xT_lo, gu_hi))):
                    mm = pe.matmul(ps[:, bank_of(i, u), 0:UW], a[:, s, i * P:(i + 1) * P], b[:, u * UW:(u + 1) * UW],
                                   start=(k == 0), stop=(k == 2))
                mm.then_inc(S["unit_done"], 1)

            def hid_turn(t, i, q):
                if q == 0:
                    pe.wait_ge(S["hid_ready"], (t + 1) * UNITS)
                m = t * 4 + q
                if after(t, 1) or q >= 2:
                    pe.wait_ge(S["hT_lo_ready"], m - 1)
                for c in range(4 * q, min(4 * q + 4, HC)):
                    mm = pe.transpose(ps[:, 4 + q % 2, (c % 4) * P:(c % 4 + 1) * P], hid[:, i, c * P:(c + 1) * P], ident)
                mm.then_inc(S["hT_done"], 1)

            def down(g):
                pe.wait_ge(S["hT_lo_ready"], (g + 1) * 8)
                pe.wait_ge(S["hT_hi_ready"], (g + 1) * 8)
                for c in range(HC):
                    cols = slice(c * P, (c + 1) * P)
                    o = ps[:, 6, 0:PW]
                    pe.matmul(o, down_hi[:, cols], hT_hi[:, c], start=(c == 0), stop=False)
                    pe.matmul(o, down_lo[:, cols], hT_hi[:, c], start=False, stop=False)
                    mm = pe.matmul(o, down_hi[:, cols], hT_lo[:, c], start=False, stop=(c == HC - 1))
                mm.then_inc(S["down_done"], 1)

            def down_back(g):
                pe.wait_ge(S["yT_kept"], g + 1)
                for i in range(2):
                    mm = pe.transpose(ps[:, 6, PW + i * P:PW + (i + 1) * P], yT[:, i * P:(i + 1) * P], ident)
                mm.then_inc(S["y_done"], 1)

            def moe(g, s, first=False, last=False):
                for u in range(UNITS):
                    unit(g * 2, s, 0, u)
                    if u % 2 == 1 and u < 9 and not first:
                        hid_turn(g * 2 - 1, 1, u // 2)
                if not first:
                    down(g - 1)
                for u in range(UNITS):
                    unit(g * 2 + 1, s, 1, u)
                    if u % 2 == 1 and u < 9:
                        hid_turn(g * 2, 0, u // 2)
                    if not last:
                        if u == 0:
                            route_turn(g + 1, 1 - s)
                        if u == 3:
                            route_logits(g + 1, 1 - s)
                        if u == 6:
                            route_back(g + 1)
                    if u == 2 and not first:
                        down_back(g - 1)

            pe.wait_ge(S["x1_ready"], NT)
            pe.wait_ge(S["w_low"], 2 * NT)
            route_turn(0, 0)
            route_logits(0, 0)
            route_back(0)
            moe(0, 0, first=True)
            with pe.Fori(0, NPAIR // 2 - 1) as r:
                for s in range(2):
                    moe(r * 2 + 1 + s, (1 + s) % 2)
            moe(NPAIR - 1, 1, last=True)
            for q in range(4):
                hid_turn(NT - 1, 1, q)
            down(NPAIR - 1)
            down_back(NPAIR - 1)

            def q1_proj(g, s):
                pe.wait_ge(S["axn_ready"], g + 1)
                if after(g, 2):
                    pe.wait_ge(S["adiff"], g - 1)
                    pe.wait_ge(S["apT_kept"], g - 1)
                for i in range(2):
                    mm = pe.transpose(ps[:, s, i * P:(i + 1) * P], xn[:, s, i, :], ident)
                mm.then_inc(S["axT_done"], 1)
                pe.wait_ge(S["axT_hi"], g + 1)
                pe.wait_ge(S["axT_lo"], g + 1)
                split3(pe, ps[:, 2 + s, 0:PW], W_Q1, xT_hi[:, s], xT_lo[:, s]).then_inc(S["aq_done"], 1)

            def scores1(g, s):
                pe.wait_ge(S["aq_kept"], g + 1)
                pe.wait_ge(S["ak_staged"], g + 1)
                for i in range(2):
                    for b in range(2):
                        tok = slice(i * P + b * SEQ, i * P + (b + 1) * SEQ)
                        mm = pe.matmul(ps[b * SEQ:(b + 1) * SEQ, s, PW + i * SEQ:PW + (i + 1) * SEQ],
                                       q1T[:, s, tok], k1s[:, s, tok], start=True, stop=True)
                mm.then_inc(S["as_done"], 1)

            def values1(g, s):
                pe.wait_ge(S["aexp_done"], g + 1)
                for i in range(2):
                    mm = pe.transpose(ps[:, 2 + s, PW + i * P:PW + (i + 1) * P], pblk[:, s, i], ident)
                mm.then_inc(S["apT_done"], 1)
                pe.wait_ge(S["apT_kept"], g + 1)
                if after(g, 2):
                    pe.wait_ge(S["x3_ready"], 2 * (g - 1))
                for i in range(2):
                    mm = pe.matmul(ps[:, 4 + s, i * P:(i + 1) * P], p1T[:, s, i], v1[:, g * 2 + i], start=True, stop=True)
                mm.then_inc(S["ao_done"], 1)

            pe.wait_ge(S["x2_ready"], NT)
            q1_proj(0, 0)
            scores1(0, 0)
            def attend1(g, s):
                q1_proj(g + 1, 1 - s)
                values1(g, s)
                scores1(g + 1, 1 - s)

            attend1(0, 0)
            attend1(1, 1)
            with pe.Fori(1, NPAIR // 2 - 1) as r:
                for s in range(2):
                    attend1(r * 2 + s, s)
            q1_proj(NPAIR - 1, 1)
            values1(NPAIR - 2, 0)
            scores1(NPAIR - 1, 1)
            values1(NPAIR - 1, 1)

            def ff_up(g, s):
                pe.wait_ge(S["fxn_ready"], g + 1)
                if after(g, 1):
                    pe.wait_ge(S["fxT_hi"], g)
                    pe.wait_ge(S["fxT_lo"], g)
                for i in range(2):
                    mm = pe.transpose(ps[:, 4, i * P:(i + 1) * P], xn[:, s, i, :], ident)
                mm.then_inc(S["fxT_done"], 1)
                pe.wait_ge(S["fxT_hi"], g + 1)
                pe.wait_ge(S["fxT_lo"], g + 1)
                if after(g, 2):
                    pe.wait_ge(S["n_ready"], 4 * (g - 1))
                for c in range(FC):
                    split3(pe, ps[:, 2 * s + c // 2, (c % 2) * PW:(c % 2 + 1) * PW], W_UP + c * P,
                           xT_hi[:, s], xT_lo[:, s]).then_inc(S["up_done"], 1)

            def ff_down(g, s):
                pe.wait_ge(S["yq_hi_ready"], g + 1)
                pe.wait_ge(S["yq_lo_ready"], g + 1)
                if after(g, 2):
                    pe.wait_ge(S["oq_int"], g - 1)
                    pe.wait_ge(S["x4_ready"], 2 * (g - 1))
                for c in range(FC):
                    w = W_DOWN + c * P
                    o = ps[:, 5 + s, 0:PW]
                    pe.matmul(o, w_hi[:, w:w + P], yq_hi[:, s, c], start=(c == 0), stop=False)
                    pe.matmul(o, w_lo[:, w:w + P], yq_hi[:, s, c], start=False, stop=False)
                    mm = pe.matmul(o, w_hi[:, w:w + P], yq_lo[:, s, c], start=False, stop=(c == FC - 1))
                mm.then_inc(S["fd_done"], 1)

            def ff_back(g, s):
                pe.wait_ge(S["oq_ready"], g + 1)
                for i in range(2):
                    mm = pe.transpose(ps[:, 5 + s, PW + i * P:PW + (i + 1) * P], oq[:, s, i * P:(i + 1) * P], ident)
                mm.then_inc(S["fo_done"], 1)

            pe.wait_ge(S["x3_ready"], NT)
            pe.wait_ge(S["adiff"], NPAIR)
            ff_up(0, 0)
            ff_up(1, 1)
            ff_down(0, 0)
            def feed(g, s):
                ff_up(g, s)
                ff_down(g - 1, 1 - s)
                ff_back(g - 2, s)

            feed(2, 0)
            feed(3, 1)
            with pe.Fori(2, NPAIR // 2) as r:
                for s in range(2):
                    feed(r * 2 + s, s)
            ff_down(NPAIR - 1, 1)
            ff_back(NPAIR - 2, 0)
            ff_back(NPAIR - 1, 1)

        @block.scalar
        def _(act):
            act.sem_inc(S["xT_hi_ready"], 1)
            act.sem_inc(S["k0_kept"], 1)
            act.sem_inc(S["k1_kept"], 1)
            act.sem_inc(S["v0_kept"], 4)
            act.sem_inc(S["q_kept"], 1)
            act.wait_ge(S["const_in"], 16)

            def keep_projections(g, s):
                act.wait_ge(S["xT_done"], g + 1)
                act.copy(xT_hi[:, s], ps[:, 0, 0:PW]).then_inc(S["xT_hi_ready"], 1)
                act.wait_ge(S["k0_done"], g + 1)
                act.copy(k0T[:, pair(g)], ps[:, 2, 0:PW]).then_inc(S["k0_kept"], 1)
                act.wait_ge(S["k1_done"], g + 1)
                act.activation(k1T[:, pair(g)], ps[:, 3, 0:PW], ACT.Identity,
                               bias=const[:, C_BK:C_BK + 1]).then_inc(S["k1_kept"], 1)
                for i in range(2):
                    act.wait_ge(S["v_done"], 2 * g + i + 1)
                    src = ps[:, 4 + 2 * s + i, :].rearrange("p (b n) -> p b n", b=2)[:, :, 0:P]
                    act.copy(v0dup[:, bass.ds(g * 4 + 2 * i, 2), :], src).then_inc(S["v0_kept"], 1)
                act.wait_ge(S["q_done"], g + 1)
                act.copy(q0T[:, pair(g)], ps[:, 1, 0:PW]).then_inc(S["q_kept"], 1)

            with act.Fori(0, NPAIR // 2) as r:
                for s in range(2):
                    keep_projections(r * 2 + s, s)

            def keep_turned(t, s):
                for half in range(2):
                    act.wait_ge(S["probT_done"], 2 * t + half + 1)
                    if half == 0 and after(t, 2):
                        act.wait_ge(S["pv_done"], t - 1)
                    act.copy(probT[:, s, 4 * half:4 * half + 4].rearrange("p c n -> p (c n)"),
                             ps[:, 4 + half, :]).then_inc(S["probT_kept"], 1)

            def exps(t, s):
                act.wait_ge(S["diff_ready"], t + 1)
                act.activation(prob[:, s], prob[:, s], ACT.Exp, scale=SCALE0).then_inc(S["exp_done"], 1)

            def split_high(t):
                n, m = UNITS * UW // NT, HC * P // NT
                act.copy(gu_hi[:, bass.ds(t * n, n)], gu_raw[:, bass.ds(t * n, n)])
                act.copy(down_hi[:, bass.ds(t * m, m)], down_raw[:, bass.ds(t * m, m)]).then_inc(S["w_high"], 1)

            act.wait_ge(S["gu_in"], 16)
            act.wait_ge(S["down_in"], 16)
            exps(0, 0)
            split_high(0)
            keep_turned(0, 0)
            exps(1, 1)
            split_high(1)
            with act.Fori(1, NT // 2) as r:
                for s in range(2):
                    t = r * 2 + s
                    keep_turned(t - 1, 1 - s)
                    exps(t, s)
                    split_high(t)
            keep_turned(NT - 1, 1)

            def route_high(g, s):
                act.wait_ge(S["gxT_done"], g + 1)
                act.copy(xT_hi[:, s], ps[:, 7, 0:PW]).then_inc(S["gxT_hi"], 1)

            def route_keep(g):
                act.wait_ge(S["glT_done"], g + 1)
                act.copy(lgT[0:NGATE, :], ps[0:NGATE, 7, PW:2 * PW]).then_inc(S["glT_kept"], 1)

            def route_exp(g):
                act.wait_ge(S["gl_diff"], 2 * g + 2)
                act.activation(ge[:, :, 0:10], gd[:, :, 0:10], ACT.Exp).then_inc(S["gexp_done"], 1)

            def silus(t, i, v):
                act.wait_ge(S["unit_done"], t * UNITS + 2 * v + 2)
                m = t * (UNITS // 2) + v
                if after(t, 1) or v >= 2:
                    act.wait_ge(S["hid_ready"], 2 * m - 2)
                b = bank_of(i, 2 * v)
                act.activation(silu[:, silu_of(i, v)], ps[:, b:b + 2, 0:INTER], ACT.Silu).then_inc(S["silu_done"], 1)

            def keep_high(t, i, q):
                act.wait_ge(S["hT_done"], t * 4 + q + 1)
                n = min(4, HC - 4 * q)
                act.copy(hT_hi[:, 4 * q:4 * q + n, i * P:(i + 1) * P],
                         ps[:, 4 + q % 2, 0:n * P].rearrange("p (c n) -> p c n", c=n)).then_inc(S["hT_hi_ready"], 1)

            def keep_y(g):
                act.wait_ge(S["down_done"], g + 1)
                act.copy(yT, ps[:, 6, 0:PW]).then_inc(S["yT_kept"], 1)

            def moe(g, s, first=False, last=False):
                for v in range(UNITS // 2):
                    silus(g * 2, 0, v)
                    if v < 4 and not first:
                        keep_high(g * 2 - 1, 1, v)
                if not first:
                    keep_y(g - 1)
                for v in range(UNITS // 2):
                    silus(g * 2 + 1, 1, v)
                    if v < 4:
                        if v == 0 and not first:
                            act.wait_ge(S["down_done"], g)
                        keep_high(g * 2, 0, v)
                    if not last:
                        if v == 1:
                            route_high(g + 1, 1 - s)
                        if v == 2:
                            route_keep(g + 1)
                if not last:
                    route_exp(g + 1)

            route_high(0, 0)
            route_keep(0)
            route_exp(0)
            moe(0, 0, first=True)
            with act.Fori(0, NPAIR // 2 - 1) as r:
                for s in range(2):
                    moe(r * 2 + 1 + s, (1 + s) % 2)
            moe(NPAIR - 1, 1, last=True)
            for q in range(4):
                keep_high(NT - 1, 1, q)
            keep_y(NPAIR - 1)

            def q1_keep(g, s):
                act.wait_ge(S["axT_done"], g + 1)
                act.copy(xT_hi[:, s], ps[:, s, 0:PW]).then_inc(S["axT_hi"], 1)
                act.wait_ge(S["aq_done"], g + 1)
                act.activation(q1T[:, s], ps[:, 2 + s, 0:PW], ACT.Identity,
                               bias=const[:, C_BQ:C_BQ + 1]).then_inc(S["aq_kept"], 1)

            def exps1(g, s):
                act.wait_ge(S["adiff"], g + 1)
                act.wait_ge(S["pblk_zero"], 1)
                for b in range(2):
                    rows = slice(b * SEQ, (b + 1) * SEQ)
                    e = act.activation(pblk[rows, s, :, b * SEQ:(b + 1) * SEQ], pdiff[rows, s], ACT.Exp)
                e.then_inc(S["aexp_done"], 1)

            def keep_p1T(g, s):
                act.wait_ge(S["apT_done"], g + 1)
                act.copy(p1T[:, s].rearrange("p t k -> p (t k)"), ps[:, 2 + s, PW:2 * PW]).then_inc(S["apT_kept"], 1)

            q1_keep(0, 0)
            exps1(0, 0)
            def attend1(g, s):
                q1_keep(g + 1, 1 - s)
                keep_p1T(g, s)
                exps1(g + 1, 1 - s)

            attend1(0, 0)
            attend1(1, 1)
            with act.Fori(1, NPAIR // 2 - 1) as r:
                for s in range(2):
                    attend1(r * 2 + s, s)
            q1_keep(NPAIR - 1, 1)
            keep_p1T(NPAIR - 2, 0)
            exps1(NPAIR - 1, 1)
            keep_p1T(NPAIR - 1, 1)

            act.wait_ge(S["b_scaled"], 1)

            def ff_n(g, s):
                act.wait_ge(S["fxT_done"], g + 1)
                act.copy(xT_hi[:, s], ps[:, 4, 0:PW]).then_inc(S["fxT_hi"], 1)
                for c in range(FC):
                    if c % 2 == 0:
                        act.wait_ge(S["up_done"], g * 4 + c + 2)
                    if c == 0 and after(g, 2):
                        act.wait_ge(S["frac_ready"], g - 1)
                    act.activation(n_i[:, s, c * PW:(c + 1) * PW], ps[:, 2 * s + c // 2, (c % 2) * PW:(c % 2 + 1) * PW],
                                   ACT.Identity, bias=b_q[:, c:c + 1], scale=QUANT).then_inc(S["n_ready"], 1)

            def ff_gelu(g, s):
                act.wait_ge(S["base_ready"], g + 1)
                if after(g, 2):
                    act.wait_ge(S["y_ready"], g - 1)
                act.activation(g_lo[:, s], base_i[:, s], ACT.Gelu, scale=1 / QUANT).then_inc(S["glo_done"], 1)
                act.activation(g_hi[:, s], base_i[:, s], ACT.Gelu, scale=1 / QUANT,
                               bias=quarter[:]).then_inc(S["ghi_done"], 1)

            def ff_yhigh(g, s):
                act.wait_ge(S["y_ready"], g + 1)
                if after(g, 2):
                    act.wait_ge(S["fd_done"], g - 1)
                act.copy(yq_hi[:, s].rearrange("p c n -> p (c n)"), y_i[:, s]).then_inc(S["yq_hi_ready"], 1)

            def ff_out(g, s):
                act.wait_ge(S["fd_done"], g + 1)
                if after(g, 2):
                    act.wait_ge(S["fo_done"], g - 1)
                act.activation(oq_i[:, s], ps[:, 5 + s, 0:PW], ACT.Identity,
                               bias=b_q[:, FC:FC + 1]).then_inc(S["oq_int"], 1)

            ff_n(0, 0)
            ff_gelu(0, 0)
            ff_n(1, 1)
            ff_gelu(1, 1)
            ff_yhigh(0, 0)
            def feed(g, s):
                ff_n(g, s)
                ff_gelu(g, s)
                ff_yhigh(g - 1, 1 - s)
                ff_out(g - 2, s)

            feed(2, 0)
            feed(3, 1)
            with act.Fori(2, NPAIR // 2) as r:
                for s in range(2):
                    feed(r * 2 + s, s)
            ff_yhigh(NPAIR - 1, 1)
            ff_out(NPAIR - 2, 0)
            ff_out(NPAIR - 1, 1)

        @block.vector
        def _(dve):
            dve.sem_inc(S["xT_lo_ready"], 1)
            dve.sem_inc(S["v1_kept"], 4)
            dve.memset(quarter[:], 0.25)
            dve.memset(minus_half[:], -0.5).then_inc(S["consts_set"], 1)
            dve.wait_ge(S["w_in"], 16)
            dve.tensor_copy(w_hi[:], wraw).then_inc(S["w_split"], 1)
            dve.wait_ge(S["w_split"], 1)
            dve.tensor_tensor(w_lo[:], wraw, w_hi[:].bitcast(F32), ALU.subtract).then_inc(S["w_split"], 1)
            dve.wait_ge(S["const_in"], 16)
            dve.tensor_scalar(b_q[:], const[:, C_B1:C_B1 + FC + 1], QUANT, None, ALU.mult).then_inc(S["b_scaled"], 1)
            dve.wait_ge(S["x_in"], 16)

            def stats(t, slot, norm):
                dve.bn_stats(moments[:, slot], x[:, t, :]).then_inc(S[f"moments{norm}"], 1)
                hold(dve, f"rstd{norm}", t + 1)
                hold(dve, f"moments{norm}", t + 1)
                dve.bn_aggr(meanvar[:, slot], moments[:, slot]).then_inc(S[f"stats{norm}"], 1)

            def normalise(g, s, ready, rstd_name):
                dve.wait_ge(S[rstd_name], 2 * g + 4)
                for i in range(2):
                    t = g * 2 + i
                    n = dve.tensor_scalar(xn[:, s, i], x[:, t, :], mean[:, one(t)], rstd[:, one(t)],
                                          ALU.subtract, ALU.mult)
                n.then_inc(S[ready], 1)

            def low_part(out, src, high, done):
                return dve.tensor_tensor(out, src, high.bitcast(F32), ALU.subtract).then_inc(S[done], 1)

            def keep_projections(g, s, last=False):
                if not last:
                    for i in range(2):
                        stats(g * 2 + 2 + i, i, 0)
                if after(g, 2):
                    dve.wait_ge(S["xT_done"], g - 1)
                normalise(g, s, "xn_ready", "rstd0")
                dve.wait_ge(S["xT_hi_ready"], g + 2)
                if after(g, 2):
                    dve.wait_ge(S["q_done"], g - 1)
                low_part(xT_lo[:, s], ps[:, 0, 0:PW], xT_hi[:, s], "xT_lo_ready")
                for i in range(2):
                    dve.wait_ge(S["v0_kept"], 2 * g + i + 5)
                    for b in range(2):
                        rows = slice(b * SEQ, (b + 1) * SEQ)
                        o = dve.tensor_tensor(v1[rows, g * 2 + i, :],
                                              ps[rows, 4 + 2 * s + i, b * PW + P:(b + 1) * PW],
                                              bv_rows[rows], ALU.add)
                    o.then_inc(S["v1_kept"], 1)

            stats(0, 0, 0)
            stats(1, 1, 0)
            keep_projections(0, 0)
            keep_projections(1, 1)
            with dve.Fori(1, NPAIR // 2 - 1) as r:
                for s in range(2):
                    keep_projections(r * 2 + s, s)
            keep_projections(NPAIR - 2, 0)
            keep_projections(NPAIR - 1, 1, last=True)

            def diffs(t, s):
                dve.wait_ge(S["scores_done"], t + 1)
                sc = ps[:, 0:4, 0:256].rearrange("p a (j k) -> p a j k", k=SEQ)
                dve.tensor_reduce(rowmax[:, s], sc, AX_X, ALU.max).then_inc(S["rowmax_ready"], 1)
                dve.wait_ge(S["rowmax_ready"], t + 1)
                if after(t, 2):
                    dve.wait_ge(S["probT_done"], 2 * t - 2)
                m = rowmax[:, s].unsqueeze(3).broadcast_to([P, 4, 4, SEQ])
                d = prob[:, s].rearrange("p (a j k) -> p a j k", a=4, j=4)
                dve.tensor_tensor(d, sc, m, ALU.subtract).then_inc(S["diff_ready"], 1)

            def heads_out(t, s):
                dve.wait_ge(S["pv_done"], t + 1)
                dve.reciprocal(rden, ps[:, 6, P:2 * P]).then_inc(S["rden_ready"], 1)
                dve.wait_ge(S["rden_ready"], t + 1)
                if after(t, 2):
                    dve.wait_ge(S["wo_done"], t - 1)
                dve.scalar_tensor_tensor(out=oT[:, s], in0=ps[:, 6, 0:P], scalar=float(REPEAT0),
                                         in1=rden, op0=ALU.mult, op1=ALU.mult).then_inc(S["oT_ready"], 1)

            def add_x(t, s):
                dve.wait_ge(S["wo_done"], t + 1)
                dve.tensor_tensor(x[:, t, :], ps[:, 7, 0:P], x[:, t, :], ALU.add).then_inc(S["x1_ready"], 1)
                hold(dve, "x1_ready", t + 1)
                stats(t, s, 1)

            def attend(t, s):
                diffs(t, s)
                heads_out(t - 2, s)
                add_x(t - 3, 1 - s)

            diffs(0, 0)
            diffs(1, 1)
            diffs(2, 0)
            heads_out(0, 0)
            diffs(3, 1)
            heads_out(1, 1)
            add_x(0, 0)
            with dve.Fori(2, NT // 2) as r:
                for s in range(2):
                    attend(r * 2 + s, s)
            heads_out(NT - 2, 0)
            add_x(NT - 3, 1)
            heads_out(NT - 1, 1)
            add_x(NT - 2, 0)
            add_x(NT - 1, 1)

            own = Steps(dve, S["route_steps"])

            def route_norm(g, s):
                normalise(g, s, "gxn_ready", "rstd1")

            def route_low(g, s):
                dve.wait_ge(S["gxT_hi"], g + 1)
                low_part(xT_lo[:, s], ps[:, 7, 0:PW], xT_hi[:, s], "gxT_lo")

            def route_diff(g):
                own.n = g * ROUTE_STEPS
                dve.wait_ge(S["gl_done"], g + 1)
                lg = ps[:, 7, 0:32].rearrange("p (t n) -> p t n", t=2)
                own.did(dve.tensor_reduce(gl[:, :, 0], lg[:, :, 0:NEXP], AX_X, ALU.max))
                dve.tensor_scalar(gd[:, :, 8:10], lg[:, :, 8:10], -1.0, None, ALU.mult).then_inc(S["gl_diff"], 1)
                own.wait()
                dve.tensor_tensor(gd[:, :, 0:NEXP], lg[:, :, 0:NEXP],
                                  gl[:, :, 0:1].broadcast_to([P, 2, NEXP]), ALU.subtract).then_inc(S["gl_diff"], 1)

            def route_weights(g, s):
                own.n = g * ROUTE_STEPS + 1
                dve.wait_ge(S["gexp_done"], g + 1)
                own.did(dve.tensor_reduce(gl[:, :, 1], ge[:, :, 0:NEXP], AX_X, ALU.add))
                own.did(dve.tensor_scalar(gl[:, :, 2:3], ge[:, :, 8:9], 1.0, None, ALU.add))
                own.wait()
                own.did(dve.reciprocal(gl[:, :, 4:6], gl[:, :, 1:3]))
                own.wait()
                own.did(dve.tensor_tensor(gp[:], ge[:, :, 0:NEXP], gl[:, :, 4:5].broadcast_to([P, 2, NEXP]), ALU.mult))
                own.wait()
                for i in range(2):
                    mine = gp[:, i].unsqueeze(2).broadcast_to([P, NEXP, NEXP])
                    other = gp[:, i].unsqueeze(1).broadcast_to([P, NEXP, NEXP])
                    own.did(dve.tensor_tensor(beats[:, i], other, mine, ALU.is_gt))
                    own.did(dve.tensor_tensor(ties[:, i], other, mine, ALU.is_equal))
                own.wait()
                own.did(dve.tensor_tensor(ties[:], ties[:], tri.unsqueeze(1).broadcast_to([P, 2, 8, 8]), ALU.mult))
                own.wait()
                own.did(dve.tensor_tensor(beats[:], beats[:], ties[:], ALU.add))
                own.wait()
                own.did(dve.tensor_reduce(rank[:], beats[:], AX_X, ALU.add))
                own.wait()
                own.did(dve.scalar_tensor_tensor(out=wexp[:, s, :, 0:NEXP], in0=rank[:], scalar=float(TOPK) - 0.5,
                                                 in1=gp[:], op0=ALU.is_lt, op1=ALU.mult))
                own.did(dve.tensor_copy(wexp[:, s, :, NEXP:UNITS], gl[:, :, 5:6].broadcast_to([P, 2, 2])))
                own.wait()

            def products(t, s, i, u):
                if u % 2 == 0:
                    dve.wait_ge(S["silu_done"], t * (UNITS // 2) + u // 2 + 1)
                if u == 0 and after(t, 2):
                    dve.wait_ge(S["hT_done"], (t - 1) * 4)
                dve.scalar_tensor_tensor(out=hid[:, i, u * INTER:(u + 1) * INTER], in0=silu[:, silu_of(i, u // 2), u % 2],
                                         scalar=wexp[:, s, i, u:u + 1], in1=ps[:, bank_of(i, u), INTER:UW],
                                         op0=ALU.mult, op1=ALU.mult).then_inc(S["hid_ready"], 1)

            def keep_low(t, i, q):
                dve.wait_ge(S["hT_hi_ready"], t * 4 + q + 1)
                n = min(4, HC - 4 * q)
                dve.tensor_tensor(hT_lo[:, 4 * q:4 * q + n, i * P:(i + 1) * P],
                                  ps[:, 4 + q % 2, 0:n * P].rearrange("p (c n) -> p c n", c=n),
                                  hT_hi[:, 4 * q:4 * q + n, i * P:(i + 1) * P].bitcast(F32),
                                  ALU.subtract).then_inc(S["hT_lo_ready"], 1)

            def add_y(g, i):
                t = g * 2 + i
                dve.wait_ge(S["y_done"], g + 1)
                dve.tensor_tensor(x[:, t, :], ps[:, 6, PW + i * P:PW + (i + 1) * P], x[:, t, :],
                                  ALU.add).then_inc(S["x2_ready"], 1)
                hold(dve, "x2_ready", t + 1)
                stats(t, i, 2)

            def moe(g, s, first=False, last=False):
                for u in range(UNITS):
                    products(g * 2, s, 0, u)
                    if u % 2 == 1 and u < 9 and not first:
                        keep_low(g * 2 - 1, 1, u // 2)
                if not last:
                    route_norm(g + 1, 1 - s)
                for u in range(UNITS):
                    products(g * 2 + 1, s, 1, u)
                    if u % 2 == 1 and u < 9:
                        keep_low(g * 2, 0, u // 2)
                    if u == 3 and not last:
                        route_low(g + 1, 1 - s)
                    if u == 4 and not first:
                        add_y(g - 1, 0)
                    if u == 6 and not first:
                        add_y(g - 1, 1)
                if not last:
                    route_diff(g + 1)
                    route_weights(g + 1, 1 - s)

            dve.wait_ge(S["kq_staged"], 2 * NT)
            dve.wait_ge(S["vblk_staged"], 2 * NT)
            dve.memset(hid[:, :, UNITS * INTER:HPAD], 0.0).then_inc(S["hid_zero"], 1)
            dve.wait_ge(S["hid_zero"], 1)
            route_norm(0, 0)
            route_low(0, 0)
            route_diff(0)
            route_weights(0, 0)
            moe(0, 0, first=True)
            with dve.Fori(0, NPAIR // 2 - 1) as r:
                for s in range(2):
                    moe(r * 2 + 1 + s, (1 + s) % 2)
            moe(NPAIR - 1, 1, last=True)
            for q in range(4):
                keep_low(NT - 1, 1, q)
            add_y(NPAIR - 1, 0)
            add_y(NPAIR - 1, 1)

            def q1_in(g, s):
                normalise(g, s, "axn_ready", "rstd2")
                dve.wait_ge(S["axT_hi"], g + 1)
                low_part(xT_lo[:, s], ps[:, s, 0:PW], xT_hi[:, s], "axT_lo")

            def diffs1(g, s):
                dve.wait_ge(S["as_done"], g + 1)
                sc = ps[:, s, PW:PW + 2 * SEQ].rearrange("p (t k) -> p t k", t=2)
                dve.tensor_reduce(stat1[:, s, 0, :], sc, AX_X, ALU.max).then_inc(S["astat"], 1)
                dve.wait_ge(S["astat"], 3 * g + 1)
                dve.tensor_tensor(pdiff[:, s], sc, stat1[:, s, 0, :].unsqueeze(2).broadcast_to([P, 2, SEQ]),
                                  ALU.subtract).then_inc(S["adiff"], 1)

            def sums1(g, s):
                dve.wait_ge(S["aexp_done"], g + 1)
                dve.tensor_reduce(stat1[:, s, 1, :], pblk[:, s], AX_X, ALU.add).then_inc(S["astat"], 1)
                dve.wait_ge(S["astat"], 3 * g + 2)
                dve.reciprocal(stat1[:, s, 2, :], stat1[:, s, 1, :]).then_inc(S["astat"], 1)
                dve.wait_ge(S["astat"], 3 * g + 3)

            def add_v(g, s):
                dve.wait_ge(S["ao_done"], g + 1)
                for i in range(2):
                    t = g * 2 + i
                    dve.scalar_tensor_tensor(out=x[:, t, :], in0=ps[:, 4 + s, i * P:(i + 1) * P],
                                             scalar=stat1[:, s, 2, i:i + 1], in1=x[:, t, :],
                                             op0=ALU.mult, op1=ALU.add).then_inc(S["x3_ready"], 1)
                    hold(dve, "x3_ready", t + 1)
                    stats(t, i, 3)

            dve.memset(pblk_, 0.0).then_inc(S["pblk_zero"], 1)
            q1_in(0, 0)
            diffs1(0, 0)
            sums1(0, 0)
            def attend1(g, s):
                q1_in(g + 1, 1 - s)
                add_v(g, s)
                diffs1(g + 1, 1 - s)
                sums1(g + 1, 1 - s)

            attend1(0, 0)
            attend1(1, 1)
            with dve.Fori(1, NPAIR // 2 - 1) as r:
                for s in range(2):
                    attend1(r * 2 + s, s)
            q1_in(NPAIR - 1, 1)
            add_v(NPAIR - 2, 0)
            diffs1(NPAIR - 1, 1)
            sums1(NPAIR - 1, 1)
            add_v(NPAIR - 1, 1)

            def ff_in(g, s):
                normalise(g, s, "fxn_ready", "rstd3")
                dve.wait_ge(S["fxT_hi"], g + 1)
                low_part(xT_lo[:, s], ps[:, 4, 0:PW], xT_hi[:, s], "fxT_lo")

            def ff_knots(g, s):
                dve.wait_ge(S["n_ready"], 4 * g + 4)
                if after(g, 2):
                    dve.wait_ge(S["ghi_done"], g - 1)
                dve.tensor_scalar(base_i[:, s], n_i[:, s], -KNOT, None, ALU.bitwise_and).then_inc(S["base_ready"], 1)
                dve.tensor_scalar(frac_i[:, s], n_i[:, s], KNOT - 1, None, ALU.bitwise_and).then_inc(S["frac_ready"], 1)

            def ff_lerp(g, s):
                dve.wait_ge(S["slope_ready"], g + 1)
                dve.scalar_tensor_tensor(out=g_hi[:, s], in0=frac_i[:, s], scalar=QUANT / KNOT, in1=g_hi[:, s],
                                         op0=ALU.mult, op1=ALU.mult).then_inc(S["rise_ready"], 1)
                dve.wait_ge(S["rise_ready"], g + 1)
                if after(g, 2):
                    dve.wait_ge(S["yq_lo_ready"], g - 1)
                dve.scalar_tensor_tensor(out=y_i[:, s], in0=g_lo[:, s], scalar=QUANT, in1=g_hi[:, s],
                                         op0=ALU.mult, op1=ALU.add).then_inc(S["y_ready"], 1)

            def ff_ylow(g, s):
                dve.wait_ge(S["yq_hi_ready"], g + 1)
                dve.tensor_tensor(yq_lo[:, s].rearrange("p c n -> p (c n)"), y_i[:, s],
                                  yq_hi[:, s].rearrange("p c n -> p (c n)").bitcast(F32),
                                  ALU.subtract).then_inc(S["yq_lo_ready"], 1)

            def ff_scale(g, s):
                dve.wait_ge(S["oq_int"], g + 1)
                dve.tensor_scalar(oq[:, s], oq_i[:, s], 1 / QUANT, None, ALU.mult).then_inc(S["oq_ready"], 1)

            def ff_add(g, s):
                dve.wait_ge(S["fo_done"], g + 1)
                for i in range(2):
                    t = g * 2 + i
                    dve.tensor_tensor(x[:, t, :], ps[:, 5 + s, PW + i * P:PW + (i + 1) * P], x[:, t, :],
                                      ALU.add).then_inc(S["x4_ready"], 1)

            ff_in(0, 0)
            ff_knots(0, 0)
            ff_in(1, 1)
            ff_lerp(0, 0)
            ff_knots(1, 1)
            ff_ylow(0, 0)
            def feed(g, s):
                ff_in(g, s)
                ff_lerp(g - 1, 1 - s)
                ff_knots(g, s)
                ff_ylow(g - 1, 1 - s)
                ff_scale(g - 2, s)
                ff_add(g - 2, s)

            feed(2, 0)
            feed(3, 1)
            with dve.Fori(2, NPAIR // 2) as r:
                for s in range(2):
                    feed(r * 2 + s, s)
            ff_lerp(NPAIR - 1, 1)
            ff_ylow(NPAIR - 1, 1)
            ff_scale(NPAIR - 2, 0)
            ff_add(NPAIR - 2, 0)
            ff_scale(NPAIR - 1, 1)
            ff_add(NPAIR - 1, 1)

        @block.gpsimd
        def _(pool):
            pool.wait_ge(S["consts_set"], 1)
            pool.sem_inc(S["rstd0"], 2)

            def free_slots(norm):
                pool.wait_ge(S[f"rstd{norm - 1}"], NT + 2)
                pool.sem_inc(S[f"rstd{norm}"], 2)

            def rstds(t, slot, norm):
                hold(pool, f"stats{norm}", t + 1)
                pool.tensor_copy(mean[:, one(t)], meanvar[:, slot, 0:1]).then_inc(S[f"veps{norm}"], 1)
                pool.tensor_scalar(veps[:, slot:slot + 1], meanvar[:, slot, 1:2], EPS, 1.0, ALU.add,
                                   ALU.mult).then_inc(S[f"veps{norm}"], 1)
                hold(pool, f"veps{norm}", 2 * t + 2)
                pool.tensor_tensor(rstd[:, one(t)], veps[:, slot:slot + 1], minus_half[:],
                                   ALU.pow).then_inc(S[f"rstd{norm}"], 1)

            def split_context(g, s, half):
                hold(pool, f"ctx_in{s}", 16 * (half + 1))
                if after(g, 2):
                    hold(pool, "v_done", 2 * (g - 1))
                src = ctxT[:, s].rearrange("p (b n) -> p b n", b=4).unsqueeze(2).broadcast_to([P, 4, 2, SEQ])
                pool.tensor_copy(ctx_hi[:, s], src).then_inc(S["ctx_split"], 1)
                hold(pool, "ctx_split", 2 * g + 1)
                pool.tensor_tensor(ctx_lo[:, s], src, ctx_hi[:, s].bitcast(F32),
                                   ALU.subtract).then_inc(S["ctx_split"], 1)

            def context_and_stats(g, s, half):
                split_context(g, s, half)
                for i in range(2):
                    rstds(g * 2 + i, i, 0)

            context_and_stats(0, 0, 0)
            context_and_stats(1, 1, 0)
            with pool.Fori(1, NPAIR // 2) as r:
                for s in range(2):
                    context_and_stats(r * 2 + s, s, r)
            pool.memset(vblk_, 0.0).then_inc(S["vblk_zero"], 1)
            pool.wait_ge(S["vblk_zero"], 1)

            def stage_kq(t, s):
                if after(t, 2):
                    hold(pool, "scores_done", t - 1)
                src = k0T[:, bass.ds(t * P, P)].rearrange("p (b k) -> p b k", b=2)
                msk = const[:, C_MASK:C_MASK + 4]
                pool.tensor_tensor(kexp[:, s], src.unsqueeze(2).broadcast_to([P, 2, 4, SEQ]),
                                   msk.unsqueeze(1).unsqueeze(3).broadcast_to([P, 2, 4, SEQ]),
                                   ALU.mult).then_inc(S["kq_staged"], 1)
                pool.tensor_copy(q_st[:, s], q0T[:, bass.ds(t * P, P)]).then_inc(S["kq_staged"], 1)

            def stage_v(t, s):
                if after(t, 2):
                    hold(pool, "pv_done", t - 1)
                src = v0dup[:, bass.ds(t * 2, 2), :].rearrange("p b (j a m) -> p (b j) a m", j=4, a=2)
                dst = vblk[:, s].rearrange("p b (j a) n -> p (b j) a n", a=2)
                for par in range(2):
                    cols = slice(par * 16, par * 16 + 16)
                    own = ones32[:, par, cols].unsqueeze(1).broadcast_to([P, 8, 16])
                    pool.tensor_tensor(dst[:, :, par, cols], src[:, :, par], own,
                                       ALU.mult).then_inc(S["vblk_staged"], 1)

            def split_low(t):
                n, m = UNITS * UW // NT, HC * P // NT
                hold(pool, "w_high", t + 1)
                pool.tensor_tensor(gu_lo[:, bass.ds(t * n, n)], gu_raw[:, bass.ds(t * n, n)],
                                   gu_hi[:, bass.ds(t * n, n)].bitcast(F32), ALU.subtract).then_inc(S["w_low"], 1)
                pool.tensor_tensor(down_lo[:, bass.ds(t * m, m)], down_raw[:, bass.ds(t * m, m)],
                                   down_hi[:, bass.ds(t * m, m)].bitcast(F32), ALU.subtract).then_inc(S["w_low"], 1)

            def attend(t, s):
                stage_kq(t, s)
                if after(t, 1):
                    stage_v(t - 1, 1 - s)
                split_low(t)
                if after(t, 4):
                    rstds(t - 4, s, 1)

            free_slots(1)
            pool.wait_ge(S["k0_kept"], NPAIR + 1)
            pool.wait_ge(S["q_kept"], NPAIR + 1)
            pool.wait_ge(S["v0_kept"], NT + 4)
            for t in range(4):
                attend(t, t % 2)
            with pool.Fori(2, NT // 2) as r:
                for s in range(2):
                    attend(r * 2 + s, s)
            stage_v(NT - 1, 1)
            for t in range(NT - 4, NT):
                rstds(t, t % 2, 1)

            free_slots(2)
            with pool.Fori(0, NPAIR) as g:
                for i in range(2):
                    rstds(g * 2 + i, i, 2)

            def stage_k1(g, s):
                if after(g, 2):
                    hold(pool, "as_done", g - 1)
                pool.tensor_copy(k1s[:, s], k1T[:, pair(g)]).then_inc(S["ak_staged"], 1)

            def stats_of(g):
                for i in range(2):
                    rstds(g * 2 + i, i, 3)

            free_slots(3)
            stage_k1(0, 0)
            stage_k1(1, 1)
            with pool.Fori(1, NPAIR // 2) as r:
                for s in range(2):
                    stage_k1(r * 2 + s, s)
                    stats_of(r * 2 + s - 2)
            stats_of(NPAIR - 2)
            stats_of(NPAIR - 1)

            def ff_slope(g, s):
                pool.wait_ge(S["glo_done"], g + 1)
                pool.wait_ge(S["ghi_done"], g + 1)
                pool.tensor_tensor(g_hi[:, s], g_hi[:, s], g_lo[:, s], ALU.subtract).then_inc(S["slope_ready"], 1)

            with pool.Fori(0, NPAIR // 2) as r:
                for s in range(2):
                    ff_slope(r * 2 + s, s)


def kernel(**inputs):
    import concourse.bacc as bacc
    from concourse.bass_utils import run_bass_kernel_spmd

    a = {k: np.asarray(v) for k, v in inputs.items()}

    def tokens_on_partitions(v):
        return v.reshape(NT, P, P).transpose(1, 0, 2)

    def chunks(v):
        return v.reshape(-1, P, v.shape[1]).transpose(1, 0, 2).reshape(P, -1)

    gate = np.concatenate([a["L0_ffn_gate_w"], a["L0_ffn_shared_expert_gate_w"],
                           np.zeros((NGATE - NEXP - 1, P), np.float32)])
    w = np.concatenate([a["L0_xattn_Wq"].T, a["L0_xattn_Wk"].T, a["L1_xattn_Wk"].T, a["L1_xattn_Wq"].T,
                        a["L0_xattn_Wv"].T, a["L1_xattn_Wv"].T, a["L1_ffn_w1"], chunks(a["L1_ffn_w2"]), gate.T], axis=1)
    sg, su = (a[f"L0_ffn_shared_{n}_w"].reshape(-1, INTER, P) for n in ("gate", "up"))
    gu = np.concatenate([a["L0_ffn_experts_gate_up"], np.concatenate([sg, su], axis=1)]).reshape(UNITS * UW, P).T
    down = np.concatenate([a["L0_ffn_experts_down"].transpose(0, 2, 1).reshape(NEXP * INTER, P),
                           a["L0_ffn_shared_down_w"].T, np.zeros((HPAD - UNITS * INTER, P), np.float32)])
    p = np.arange(P)
    mask = (p[:, None] // HD % 4 == np.arange(4)).astype(np.float32)
    tri = np.broadcast_to((np.arange(8)[None, :] < np.arange(8)[:, None]).astype(np.float32).reshape(1, 64), (P, 64))
    ones = (np.arange(64)[None, :] % 32 // HD == 2 * (np.arange(64)[None, :] // 32) + p[:, None] // SEQ).astype(np.float32)
    const = np.concatenate([np.eye(P, dtype=np.float32), a["L0_xattn_Wo"].T,
                            np.broadcast_to(a["L1_xattn_bv"], (P, P)), mask, tri, ones,
                            a["L1_xattn_bq"][:, None], a["L1_xattn_bk"][:, None],
                            a["L1_ffn_b1"].reshape(FC, P).T, a["L1_ffn_b2"][:, None]], axis=1)
    arrays = {
        "in_x": tokens_on_partitions(a["x"]), "in_ctx": a["ctx_1024"].reshape(NT * P, P).T, "in_w": w, "in_gu": gu,
        "in_down": chunks(down), "in_const": const,
    }
    arrays = {k: np.ascontiguousarray(v) for k, v in arrays.items()}
    nc = bacc.Bacc("TRN2", target_bir_lowering=False, num_devices=1)
    args = [nc.dram_tensor(k, v.shape, F32, kind="ExternalInput").ap() for k, v in arrays.items()]
    out = nc.dram_tensor("out_0", (P, NT, P), F32, kind="ExternalOutput").ap()
    two_layers(nc, *args, out)
    r = run_bass_kernel_spmd(nc, [arrays], core_ids=[0])
    return np.ascontiguousarray(r.results[0]["out_0"].transpose(1, 0, 2)).reshape(BATCH, SEQ, P)
```

```python
from contextlib import ExitStack

import numpy as np

import concourse.bass as bass
from concourse import mybir

F32 = mybir.dt.float32
F32R = mybir.dt.float32r
I32 = mybir.dt.int32
ALU = mybir.AluOpType
ACT = mybir.ActivationFunctionType
AX_X = mybir.AxisListType.X

P = 128
BATCH, SEQ = 32, 64
NT = BATCH * SEQ // P
NPAIR = NT // 2
PW = 2 * P
HEADS, HD = 16, 8
NEXP, TOPK = 8, 2
INTER = 176
SHARED = 352
UNITS = NEXP + SHARED // INTER
UW = 2 * INTER
HC = -(-UNITS * INTER // P)
HPAD = HC * P
FF = 512
FC = FF // P
EPS = 1e-5
SCALE0 = HD ** -0.5
REPEAT0 = 3
QUANT = 256.0
KNOT = 64

W_Q0, W_K0, W_K1, W_Q1, W_V, W_UP = 0, 128, 256, 384, 512, 768
W_DOWN = W_UP + FF
W_GATE = W_DOWN + FF
W_EARLY = W_UP
NGATE = 10
W_COLS = W_GATE + NGATE
C_ID, C_WO, C_BV, C_MASK, C_TRI, C_ONES = 0, 128, 256, 384, 388, 452
C_BQ = C_ONES + 64
C_BK, C_B1 = C_BQ + 1, C_BQ + 2
C_COLS = C_B1 + FC + 1
ROUTE_STEPS = 14


def pair(g):
    return bass.ds(g * PW, PW)


def one(t):
    return bass.ds(t, 1)


def after(step, n):
    return not isinstance(step, int) or step >= n


def inside(step, n):
    return not isinstance(step, int) or 0 <= step < n


def steps(eng, first, lo, hi, stop, step):
    for k in range(first, lo):
        step(k, k % 2, k // 2)
    with eng.Fori(lo // 2, hi // 2) as r:
        for s in range(2):
            step(r * 2 + s, s, r)
    for k in range(hi, stop):
        step(k, k % 2, k // 2)


def bank_of(i, u):
    return (i * UNITS + u) % 4


def silu_of(i, v):
    return (i * (UNITS // 2) + v) % 2


class Steps:

    def __init__(self, eng, sem, base=0):
        self.eng, self.sem, self.n = eng, sem, base

    def did(self, ins):
        ins.then_inc(self.sem, 1)
        self.n = self.n + 1

    def wait(self):
        self.eng.wait_ge(self.sem, self.n)


def two_layers(nc, x_d, ctx_d, w_d, gu_d, down_d, const_d, out_d):
    with ExitStack() as ctx:
        def sb(name, shape, dt=F32):
            return ctx.enter_context(nc.sbuf_tensor(name, shape, dt))

        def sem(name):
            return ctx.enter_context(nc.semaphore(name))

        x = sb("x", [P, NT, P])
        const = sb("const", [P, C_COLS])
        w_hi = sb("w_hi", [P, W_COLS], F32R)
        w_lo = sb("w_lo", [P, W_COLS], F32R)
        gu_hi = sb("gu_hi", [P, UNITS * UW], F32R)
        gu_lo = sb("gu_lo", [P, UNITS * UW], F32R)
        down_hi = sb("down_hi", [P, HC * P], F32R)
        down_lo = sb("down_lo", [P, HC * P], F32R)
        k1T = sb("k1T", [P, NT * P])
        v1 = sb("v1", [P, NT, P])
        moments = sb("moments", [P, 2, 6])
        meanvar = sb("meanvar", [P, 2, 2])
        veps = sb("veps", [P, 2])
        mean = sb("mean", [P, NT])
        rstd = sb("rstd", [P, NT])
        minus_half = sb("minus_half", [P, 2])
        xn = sb("xn", [P, 2, 2, P])
        xT_hi = sb("xT_hi", [P, 2, PW], F32R)
        xT_lo = sb("xT_lo", [P, 2, PW], F32R)

        AR = 2 * HC * PW
        arena_r = sb("arena_r", [P, AR], F32R)
        AF = 20864
        arena_f = sb("arena_f", [P, AF])

        def carve(arena, sizes):
            at, out = 0, []
            for n in sizes:
                out.append(arena[:, at:at + n])
                at += n
            assert at <= arena.shape[1]
            return out

        (k0T, q0T, v0dup, gu_raw, down_raw, kexp_, q_st_, vblk_, prob_, probT_, rden, oT_, ctxT_) = carve(
            arena_f, [NT * P, NT * P, 2 * NT * P, UNITS * UW, HC * P, 2 * 512, 2 * P, 2 * 512, 2 * 1024,
                      2 * 1024, P, 2 * P, 2 * PW])
        v0dup = v0dup.rearrange("p (b f) -> p b f", f=P)
        kexp = kexp_.rearrange("p (s b j k) -> p s b j k", s=2, b=2, j=4)
        q_st = q_st_.rearrange("p (s n) -> p s n", s=2)
        vblk = vblk_.rearrange("p (s b c n) -> p s b c n", s=2, b=2, c=8)
        prob = prob_.rearrange("p (s n) -> p s n", s=2)
        probT = probT_.rearrange("p (s c n) -> p s c n", s=2, c=8)
        oT = oT_.rearrange("p (s n) -> p s n", s=2)
        ctxT = ctxT_.rearrange("p (s n) -> p s n", s=2)
        wraw = prob_[:, 0:W_COLS]
        ctx_hi_, ctx_lo_ = carve(arena_r, [4 * PW, 4 * PW])
        ctx_hi = ctx_hi_.rearrange("p (s b r n) -> p s b r n", s=2, b=4, r=2)
        ctx_lo = ctx_lo_.rearrange("p (s b r n) -> p s b r n", s=2, b=4, r=2)
        rowmax = sb("rowmax", [P, 2, 4, 4])

        hT_hi, hT_lo = (a.rearrange("p (c n) -> p c n", c=HC) for a in carve(arena_r, [HC * PW] * 2))
        hid_, act_, yT, lgT = carve(arena_f, [2 * HPAD, 2 * 2 * INTER, PW, PW])
        hid = hid_.rearrange("p (s n) -> p s n", s=2)
        silu = act_.rearrange("p (s u n) -> p s u n", s=2, u=2)
        gl = sb("gl", [P, 2, 16])
        gd = sb("gd", [P, 2, 12])
        ge = sb("ge", [P, 2, 12])
        gp = sb("gp", [P, 2, 8])
        beats = sb("beats", [P, 2, 8, 8])
        ties = sb("ties", [P, 2, 8, 8])
        rank = sb("rank", [P, 2, 8])
        wexp = sb("wexp", [P, 2, 2, UNITS])

        q1T_, k1s_, pd_, pblk_, pT_ = carve(arena_f[:, 5120:], [2 * PW, 2 * PW, 2 * P, 2 * PW, 2 * PW])
        q1T = q1T_.rearrange("p (s n) -> p s n", s=2)
        k1s = k1s_.rearrange("p (s n) -> p s n", s=2)
        pdiff = pd_.rearrange("p (s t k) -> p s t k", s=2, t=2)
        pblk = pblk_.rearrange("p (s t k) -> p s t k", s=2, t=2)
        p1T = pT_.rearrange("p (s t k) -> p s t k", s=2, t=2)
        stat1 = sb("stat1", [P, 2, 3, 2])

        n_, base_, frac_, g0_, g1_, y_, oq_ = carve(arena_f[:, 7680:], [2 * 1024] * 6 + [2 * PW])
        (n_i, base_i, frac_i) = (a.bitcast(I32).rearrange("p (s n) -> p s n", s=2) for a in (n_, base_, frac_))
        g_lo = g0_.rearrange("p (s n) -> p s n", s=2)
        g_hi = g1_.rearrange("p (s n) -> p s n", s=2)
        y_i = y_.bitcast(I32).rearrange("p (s n) -> p s n", s=2)
        oq = oq_.rearrange("p (s n) -> p s n", s=2)
        oq_i = oq_.bitcast(I32).rearrange("p (s n) -> p s n", s=2)
        yq_hi_, yq_lo_ = carve(arena_r, [2 * 1024] * 2)
        yq_hi = yq_hi_.rearrange("p (s c n) -> p s c n", s=2, c=FC)
        yq_lo = yq_lo_.rearrange("p (s c n) -> p s c n", s=2, c=FC)
        b_q = sb("b_q", [P, FC + 1])
        quarter = sb("quarter", [P, 1])

        ident = const[:, C_ID:C_ID + P]
        woT = const[:, C_WO:C_WO + P]
        bv_rows = const[:, C_BV:C_BV + P]
        tri = const[:, C_TRI:C_TRI + 64].rearrange("p (i j) -> p i j", i=8)
        ones32 = const[:, C_ONES:C_ONES + 64].rearrange("p (a n) -> p a n", a=2)

        ps = ctx.enter_context(nc.psum_tensor("ps", [P, 8, 512], F32))

        S = {}
        for name in """
            ctx_in0 ctx_in1 w_in w_rest_in const_in x_in x_rest_in gu_in down_in out_done
            held consts_set b_scaled w_hi_ready w_lo_ready ctx_hi_ready ctx_lo_ready moments0 stats0 veps0 rstd0 xn_ready
            xT_done xT_hi_ready xT_lo_ready k0_done k0_kept k1_done k1_kept v_done v0_kept v1_kept q_done q_kept
            vblk_zero k_staged q_staged vblk_staged scores_done rowmax_ready diff_ready exp_done probT_done probT_kept
            pv_done rden_ready oT_ready wo_done x1_ready w_high w_low moments1 stats1 veps1 rstd1
            hid_zero gxn_ready gxT_done gxT_hi gxT_lo glT_done glT_kept gl_done gl_diff gexp_done route_steps
            unit_done silu_done hid_ready hT_done hT_hi_ready hT_lo_ready down_done yT_kept y_done x2_ready
            moments2 stats2 veps2 rstd2
            pblk_zero axn_ready axT_done axT_hi axT_lo aq_done aq_kept ak_staged as_done amax adiff aexp_done apT_done
            apT_kept ao_done astat x3_ready moments3 stats3 veps3 rstd3
            fxn_ready fxT_done fxT_hi fxT_lo up_done n_ready base_ready frac_ready glo_done ghi_done slope_ready
            rise_ready y_ready yq_hi_ready yq_lo_ready fd_done oq_int oq_ready fo_done x4_ready
        """.split():
            S[name] = sem(name)

        def hold(eng, name, value):
            eng.wait_ge(S[name], value)
            eng.sem_inc(S["held"], 1)

        def split3(pe, out, w, m_hi, m_lo, n=P, first=True):
            pe.matmul(out, w_hi[:, w:w + n], m_hi, start=first, stop=False)
            pe.matmul(out, w_lo[:, w:w + n], m_hi, start=False, stop=False)
            return pe.matmul(out, w_hi[:, w:w + n], m_lo, start=False, stop=True)

        block = ctx.enter_context(nc.Block())

        @block.sync
        def _(sp):
            sp.dma_start(wraw[:, 0:W_EARLY], w_d[:, 0:W_EARLY]).then_inc(S["w_in"], 16)
            sp.dma_start(x[:, 0:4], x_d[:, 0:4]).then_inc(S["x_in"], 16)
            sp.dma_start(ctxT[:, 0], ctx_d[:, pair(0)]).then_inc(S["ctx_in0"], 16)
            sp.dma_start(const[:], const_d).then_inc(S["const_in"], 16)
            sp.dma_start(ctxT[:, 1], ctx_d[:, pair(1)]).then_inc(S["ctx_in1"], 16)
            sp.dma_start(x[:, 4:NT], x_d[:, 4:NT]).then_inc(S["x_rest_in"], 16)
            sp.dma_start(wraw[:, W_EARLY:W_COLS], w_d[:, W_EARLY:W_COLS]).then_inc(S["w_rest_in"], 16)
            sp.dma_start(gu_raw, gu_d).then_inc(S["gu_in"], 16)
            sp.dma_start(down_raw, down_d).then_inc(S["down_in"], 16)
            for g in range(2, NPAIR):
                sp.wait_ge(S["ctx_lo_ready"], g - 1)
                sp.dma_start(ctxT[:, g % 2], ctx_d[:, pair(g)]).then_inc(S[f"ctx_in{g % 2}"], 16)
            for g in range(NPAIR):
                sp.wait_ge(S["x4_ready"], 2 * g + 6)
                sp.dma_start(out_d[:, 2 * g:2 * g + 2, :], x[:, 2 * g:2 * g + 2, :]).then_inc(S["out_done"], 16)
            sp.wait_ge(S["out_done"], 16 * NPAIR)

        @block.tensor
        def _(pe):
            pe.wait_ge(S["w_hi_ready"], 1)
            pe.wait_ge(S["w_lo_ready"], 1)
            pe.wait_ge(S["const_in"], 16)

            def project(g, s):
                pe.wait_ge(S["xn_ready"], g + 1)
                pe.wait_ge(S["xT_lo_ready"], g + 1)
                pe.wait_ge(S["xT_hi_ready"], g + 1)
                for i in range(2):
                    mm = pe.transpose(ps[:, 0, i * P:(i + 1) * P], xn[:, s, i, :], ident)
                mm.then_inc(S["xT_done"], 1)
                pe.wait_ge(S["ctx_hi_ready"], g + 1)
                pe.wait_ge(S["ctx_lo_ready"], g + 1)
                pe.wait_ge(S["k0_kept"], g + 1)
                split3(pe, ps[:, 2, 0:PW], W_K0, ctx_hi[:, s, :, 0], ctx_lo[:, s, :, 0]).then_inc(S["k0_done"], 1)
                pe.wait_ge(S["k1_kept"], g + 1)
                split3(pe, ps[:, 3, 0:PW], W_K1, ctx_hi[:, s, :, 0], ctx_lo[:, s, :, 0]).then_inc(S["k1_done"], 1)
                pe.wait_ge(S["v0_kept"], 2 * g + 2)
                pe.wait_ge(S["v1_kept"], 2 * g + 2)
                for i in range(2):
                    for b in range(2):
                        at = (s * 4 + 2 * i + b) * P
                        hi, lo = ctx_hi_[:, at:at + P], ctx_lo_[:, at:at + P]
                        o = ps[:, 4 + 2 * s + i, b * PW:(b + 1) * PW]
                        pe.matmul(o, hi, w_hi[:, W_V:W_V + PW], start=True, stop=False)
                        pe.matmul(o, hi, w_lo[:, W_V:W_V + PW], start=False, stop=False)
                        mm = pe.matmul(o, lo, w_hi[:, W_V:W_V + PW], start=False, stop=True)
                    mm.then_inc(S["v_done"], 1)
                pe.wait_ge(S["xT_lo_ready"], g + 2)
                pe.wait_ge(S["xT_hi_ready"], g + 2)
                pe.wait_ge(S["q_kept"], g + 1)
                split3(pe, ps[:, 1, 0:PW], W_Q0, xT_hi[:, s], xT_lo[:, s]).then_inc(S["q_done"], 1)

            with pe.Fori(0, NPAIR // 2) as r:
                for s in range(2):
                    project(r * 2 + s, s)

            def scores(t, s):
                pe.wait_ge(S["k_staged"], t + 1)
                pe.wait_ge(S["q_staged"], t + 1)
                if after(t, 1):
                    pe.wait_ge(S["diff_ready"], t)
                for h4 in range(4):
                    rows = slice(32 * h4, 32 * h4 + 32)
                    for b in range(2):
                        mm = pe.matmul(ps[b * SEQ:(b + 1) * SEQ, h4, 0:256],
                                       q_st[rows, s, b * SEQ:(b + 1) * SEQ],
                                       kexp_[rows, (2 * s + b) * 256:(2 * s + b + 1) * 256], start=True, stop=True)
                mm.then_inc(S["scores_done"], 1)

            def turn(t, s):
                pe.wait_ge(S["exp_done"], t + 1)
                for half in range(2):
                    if after(t, 1):
                        pe.wait_ge(S["probT_kept"], 2 * t - 1 + half)
                    for c in range(4):
                        cc = 4 * half + c
                        mm = pe.transpose(ps[:, 4 + half, c * P:(c + 1) * P],
                                          prob[:, s, cc * P:(cc + 1) * P], ident)
                    mm.then_inc(S["probT_done"], 1)

            def values(t, s):
                pe.wait_ge(S["probT_kept"], 2 * t + 2)
                pe.wait_ge(S["vblk_staged"], 2 * t + 2)
                if after(t, 1):
                    pe.wait_ge(S["oT_ready"], t)
                for b in range(2):
                    q = slice(b * SEQ, (b + 1) * SEQ)
                    for kind in range(2):
                        for par in range(2):
                            for j in range(4):
                                w = vblk[:, s, b, 2 * j + par] if kind == 0 else ones32[:, par]
                                at = kind * P + b * SEQ
                                mm = pe.matmul(ps[32 * j:32 * j + 32, 6, at:at + SEQ], w,
                                               probT[:, s, 2 * j + par, q], start=(par == 0), stop=(par == 1))
                mm.then_inc(S["pv_done"], 1)

            def out_proj(t, s):
                pe.wait_ge(S["oT_ready"], t + 1)
                if after(t, 1):
                    pe.wait_ge(S["x1_ready"], t)
                pe.matmul(ps[:, 7, 0:P], oT[:, s], woT, start=True, stop=True).then_inc(S["wo_done"], 1)

            def attend(t, s, _):
                if inside(t, NT):
                    scores(t, s)
                if inside(t - 1, NT):
                    turn(t - 1, 1 - s)
                if inside(t - 2, NT):
                    values(t - 2, s)
                if inside(t - 3, NT):
                    out_proj(t - 3, 1 - s)

            for name, n in (("xT_hi_ready", NPAIR + 1), ("xT_lo_ready", NPAIR + 1), ("k0_kept", NPAIR + 1),
                            ("k1_kept", NPAIR + 1), ("v0_kept", NT + 4), ("v1_kept", NT + 4), ("q_kept", NPAIR + 1)):
                pe.wait_ge(S[name], n)
            steps(pe, 0, 4, NT, NT + 3, attend)

            def route_turn(g, s):
                pe.wait_ge(S["gxn_ready"], g + 1)
                if after(g, 1):
                    pe.wait_ge(S["gl_diff"], 2 * g)
                for i in range(2):
                    mm = pe.transpose(ps[:, 7, i * P:(i + 1) * P], xn[:, s, i, :], ident)
                mm.then_inc(S["gxT_done"], 1)

            def route_logits(g, s):
                pe.wait_ge(S["gxT_hi"], g + 1)
                pe.wait_ge(S["gxT_lo"], g + 1)
                split3(pe, ps[0:NGATE, 7, PW:2 * PW], W_GATE, xT_hi[:, s], xT_lo[:, s], NGATE).then_inc(S["glT_done"], 1)

            def route_back(g):
                hold(pe, "glT_kept", g + 1)
                for i in range(2):
                    mm = pe.transpose(ps[:, 7, i * 16:i * 16 + NGATE], lgT[0:NGATE, i * P:(i + 1) * P],
                                      const[0:NGATE, C_ID:C_ID + NGATE])
                mm.then_inc(S["gl_done"], 1)

            def unit(t, s, i, u):
                n = t * UNITS + u
                if after(t, 1) or u >= 4:
                    pe.wait_ge(S["hid_ready"], n - 3)
                for k, (a, b) in enumerate(((xT_hi, gu_hi), (xT_hi, gu_lo), (xT_lo, gu_hi))):
                    mm = pe.matmul(ps[:, bank_of(i, u), 0:UW], a[:, s, i * P:(i + 1) * P], b[:, u * UW:(u + 1) * UW],
                                   start=(k == 0), stop=(k == 2))
                mm.then_inc(S["unit_done"], 1)

            def hid_turn(t, i, q):
                if q == 0:
                    pe.wait_ge(S["hid_ready"], (t + 1) * UNITS)
                m = t * 4 + q
                if after(t, 1) or q >= 2:
                    pe.wait_ge(S["hT_lo_ready"], m - 1)
                for c in range(4 * q, min(4 * q + 4, HC)):
                    mm = pe.transpose(ps[:, 4 + q % 2, (c % 4) * P:(c % 4 + 1) * P], hid[:, i, c * P:(c + 1) * P], ident)
                mm.then_inc(S["hT_done"], 1)

            def down(g):
                pe.wait_ge(S["hT_lo_ready"], (g + 1) * 8)
                pe.wait_ge(S["hT_hi_ready"], (g + 1) * 8)
                for c in range(HC):
                    cols = slice(c * P, (c + 1) * P)
                    o = ps[:, 6, 0:PW]
                    pe.matmul(o, down_hi[:, cols], hT_hi[:, c], start=(c == 0), stop=False)
                    pe.matmul(o, down_lo[:, cols], hT_hi[:, c], start=False, stop=False)
                    mm = pe.matmul(o, down_hi[:, cols], hT_lo[:, c], start=False, stop=(c == HC - 1))
                mm.then_inc(S["down_done"], 1)

            def down_back(g):
                pe.wait_ge(S["yT_kept"], g + 1)
                for i in range(2):
                    mm = pe.transpose(ps[:, 6, PW + i * P:PW + (i + 1) * P], yT[:, i * P:(i + 1) * P], ident)
                mm.then_inc(S["y_done"], 1)

            def moe(g, s, _):
                last = not inside(g + 1, NPAIR)
                for u in range(UNITS):
                    unit(g * 2, s, 0, u)
                    if u % 2 == 1 and u < 9 and after(g, 1):
                        hid_turn(g * 2 - 1, 1, u // 2)
                    if u == 0 and not last:
                        route_turn(g + 1, 1 - s)
                    if u == 5 and not last:
                        route_logits(g + 1, 1 - s)
                if not last:
                    route_back(g + 1)
                if after(g, 1):
                    down(g - 1)
                for u in range(UNITS):
                    unit(g * 2 + 1, s, 1, u)
                    if u % 2 == 1 and u < 9:
                        hid_turn(g * 2, 0, u // 2)
                    if u == 2 and after(g, 1):
                        down_back(g - 1)

            pe.wait_ge(S["x1_ready"], NT)
            pe.wait_ge(S["w_low"], 2 * NT)
            pe.wait_ge(S["w_hi_ready"], 2)
            pe.wait_ge(S["w_lo_ready"], 2)
            route_turn(0, 0)
            route_logits(0, 0)
            route_back(0)
            steps(pe, 0, 2, NPAIR - 2, NPAIR, moe)
            for q in range(4):
                hid_turn(NT - 1, 1, q)
            down(NPAIR - 1)
            down_back(NPAIR - 1)

            def q1_turn(g, s):
                pe.wait_ge(S["axn_ready"], g + 1)
                if after(g, 2):
                    pe.wait_ge(S["axT_lo"], g - 1)
                for i in range(2):
                    mm = pe.transpose(ps[:, s, i * P:(i + 1) * P], xn[:, s, i, :], ident)
                mm.then_inc(S["axT_done"], 1)

            def q1_proj(g, s):
                pe.wait_ge(S["axT_hi"], g + 1)
                pe.wait_ge(S["axT_lo"], g + 1)
                if after(g, 1):
                    pe.wait_ge(S["aq_kept"], g)
                split3(pe, ps[:, 4, 0:PW], W_Q1, xT_hi[:, s], xT_lo[:, s]).then_inc(S["aq_done"], 1)

            def scores1(g, s):
                pe.wait_ge(S["aq_kept"], g + 1)
                pe.wait_ge(S["ak_staged"], g + 1)
                if after(g, 2):
                    pe.wait_ge(S["adiff"], g - 1)
                for i in range(2):
                    for b in range(2):
                        tok = slice(i * P + b * SEQ, i * P + (b + 1) * SEQ)
                        mm = pe.matmul(ps[b * SEQ:(b + 1) * SEQ, 2 + s, i * SEQ:(i + 1) * SEQ],
                                       q1T[:, s, tok], k1s[:, s, tok], start=True, stop=True)
                mm.then_inc(S["as_done"], 1)

            def p1_turn(g, s):
                pe.wait_ge(S["aexp_done"], g + 1)
                if after(g, 1):
                    pe.wait_ge(S["apT_kept"], g)
                for i in range(2):
                    mm = pe.transpose(ps[:, 5, i * P:(i + 1) * P], pblk[:, s, i], ident)
                mm.then_inc(S["apT_done"], 1)

            def values1(g, s):
                pe.wait_ge(S["apT_kept"], g + 1)
                if after(g, 2):
                    pe.wait_ge(S["x3_ready"], 2 * (g - 1))
                for i in range(2):
                    mm = pe.matmul(ps[:, 6 + s, i * P:(i + 1) * P], p1T[:, s, i], v1[:, g * 2 + i], start=True, stop=True)
                mm.then_inc(S["ao_done"], 1)

            def attend1(g, s, _):
                if inside(g + 1, NPAIR):
                    scores1(g + 1, 1 - s)
                if inside(g + 2, NPAIR):
                    q1_turn(g + 2, s)
                if inside(g, NPAIR):
                    p1_turn(g, s)
                if inside(g + 2, NPAIR):
                    q1_proj(g + 2, s)
                if inside(g, NPAIR):
                    values1(g, s)

            pe.wait_ge(S["x2_ready"], NT)
            steps(pe, -2, 2, NPAIR - 2, NPAIR, attend1)

            def ff_up(g, s):
                pe.wait_ge(S["fxn_ready"], g + 1)
                if after(g, 1):
                    pe.wait_ge(S["fxT_hi"], g)
                    pe.wait_ge(S["fxT_lo"], g)
                for i in range(2):
                    mm = pe.transpose(ps[:, 4, i * P:(i + 1) * P], xn[:, s, i, :], ident)
                mm.then_inc(S["fxT_done"], 1)
                pe.wait_ge(S["fxT_hi"], g + 1)
                pe.wait_ge(S["fxT_lo"], g + 1)
                if after(g, 2):
                    pe.wait_ge(S["n_ready"], 4 * (g - 1))
                for c in range(FC):
                    split3(pe, ps[:, 2 * s + c // 2, (c % 2) * PW:(c % 2 + 1) * PW], W_UP + c * P,
                           xT_hi[:, s], xT_lo[:, s]).then_inc(S["up_done"], 1)

            def ff_down(g, s):
                pe.wait_ge(S["yq_hi_ready"], g + 1)
                pe.wait_ge(S["yq_lo_ready"], g + 1)
                pe.wait_ge(S["oq_int"], g + 1)
                pe.wait_ge(S["x4_ready"], 2 * g + 2)
                for c in range(FC):
                    w = W_DOWN + c * P
                    o = ps[:, 5 + s, 0:PW]
                    pe.matmul(o, w_hi[:, w:w + P], yq_hi[:, s, c], start=(c == 0), stop=False)
                    pe.matmul(o, w_lo[:, w:w + P], yq_hi[:, s, c], start=False, stop=False)
                    mm = pe.matmul(o, w_hi[:, w:w + P], yq_lo[:, s, c], start=False, stop=(c == FC - 1))
                mm.then_inc(S["fd_done"], 1)

            def ff_back(g, s):
                pe.wait_ge(S["oq_ready"], g + 1)
                for i in range(2):
                    mm = pe.transpose(ps[:, 5 + s, PW + i * P:PW + (i + 1) * P], oq[:, s, i * P:(i + 1) * P], ident)
                mm.then_inc(S["fo_done"], 1)

            def feed(g, s, _):
                if inside(g - 2, NPAIR):
                    ff_back(g - 2, s)
                if inside(g + 2, NPAIR):
                    ff_up(g + 2, s)
                if inside(g - 1, NPAIR):
                    ff_down(g - 1, 1 - s)

            pe.sem_inc(S["fo_done"], 2)
            pe.wait_ge(S["x3_ready"], NT)
            pe.wait_ge(S["adiff"], NPAIR)
            pe.wait_ge(S["apT_kept"], NPAIR)
            steps(pe, -2, 2, NPAIR - 2, NPAIR + 2, feed)

        @block.scalar
        def _(act):
            act.sem_inc(S["xT_hi_ready"], 1)
            act.sem_inc(S["k0_kept"], 1)
            act.sem_inc(S["k1_kept"], 1)
            act.sem_inc(S["v0_kept"], 4)
            act.sem_inc(S["q_kept"], 1)
            act.sem_inc(S["oq_int"], 2)
            act.wait_ge(S["w_in"], 16)
            act.copy(w_hi[:, 0:W_EARLY], wraw[:, 0:W_EARLY]).then_inc(S["w_hi_ready"], 1)

            def context_high(g, s, half):
                act.wait_ge(S[f"ctx_in{s}"], 16 * (half + 1))
                if after(g, 2):
                    act.wait_ge(S["v_done"], 2 * (g - 1))
                src = ctxT[:, s].rearrange("p (b n) -> p b n", b=4).unsqueeze(2).broadcast_to([P, 4, 2, SEQ])
                act.copy(ctx_hi[:, s], src).then_inc(S["ctx_hi_ready"], 1)

            def keep_projections(g, s, half):
                act.wait_ge(S["xT_done"], g + 1)
                act.copy(xT_hi[:, s], ps[:, 0, 0:PW]).then_inc(S["xT_hi_ready"], 1)
                act.wait_ge(S["k0_done"], g + 1)
                act.copy(k0T[:, pair(g)], ps[:, 2, 0:PW]).then_inc(S["k0_kept"], 1)
                if inside(g + 1, NPAIR):
                    context_high(g + 1, 1 - s, half + s)
                act.wait_ge(S["k1_done"], g + 1)
                act.activation(k1T[:, pair(g)], ps[:, 3, 0:PW], ACT.Identity,
                               bias=const[:, C_BK:C_BK + 1]).then_inc(S["k1_kept"], 1)
                for i in range(2):
                    act.wait_ge(S["v_done"], 2 * g + i + 1)
                    src = ps[:, 4 + 2 * s + i, :].rearrange("p (b n) -> p b n", b=2)[:, :, 0:P]
                    act.copy(v0dup[:, bass.ds(g * 4 + 2 * i, 2), :], src).then_inc(S["v0_kept"], 1)
                act.wait_ge(S["q_done"], g + 1)
                act.copy(q0T[:, pair(g)], ps[:, 1, 0:PW]).then_inc(S["q_kept"], 1)

            context_high(0, 0, 0)
            act.wait_ge(S["const_in"], 16)
            keep_projections(0, 0, 0)
            act.wait_ge(S["w_rest_in"], 16)
            act.copy(w_hi[:, W_EARLY:W_COLS], wraw[:, W_EARLY:W_COLS]).then_inc(S["w_hi_ready"], 1)
            steps(act, 1, 2, NPAIR - 2, NPAIR, keep_projections)

            def keep_turned(t, s):
                for half in range(2):
                    act.wait_ge(S["probT_done"], 2 * t + half + 1)
                    if half == 0 and after(t, 2):
                        act.wait_ge(S["pv_done"], t - 1)
                    act.copy(probT[:, s, 4 * half:4 * half + 4].rearrange("p c n -> p (c n)"),
                             ps[:, 4 + half, :]).then_inc(S["probT_kept"], 1)

            def exps(t, s):
                act.wait_ge(S["diff_ready"], t + 1)
                act.activation(prob[:, s], prob[:, s], ACT.Exp, scale=SCALE0).then_inc(S["exp_done"], 1)

            def split_high(t):
                n, m = UNITS * UW // NT, HC * P // NT
                act.copy(gu_hi[:, bass.ds(t * n, n)], gu_raw[:, bass.ds(t * n, n)])
                act.copy(down_hi[:, bass.ds(t * m, m)], down_raw[:, bass.ds(t * m, m)]).then_inc(S["w_high"], 1)

            def stage_q(t, s):
                if after(t, 2):
                    act.wait_ge(S["scores_done"], t - 1)
                act.copy(q_st[:, s], q0T[:, bass.ds(t * P, P)]).then_inc(S["q_staged"], 1)

            act.wait_ge(S["q_kept"], NPAIR + 1)
            stage_q(0, 0)
            stage_q(1, 1)
            act.wait_ge(S["gu_in"], 16)
            act.wait_ge(S["down_in"], 16)
            def attend(t, s, _):
                if inside(t - 1, NT):
                    keep_turned(t - 1, 1 - s)
                if inside(t, NT):
                    exps(t, s)
                if inside(t + 2, NT):
                    stage_q(t + 2, s)
                if inside(t, NT):
                    split_high(t)

            steps(act, 0, 4, NT - 2, NT + 1, attend)

            def route_high(g, s):
                act.wait_ge(S["gxT_done"], g + 1)
                act.copy(xT_hi[:, s], ps[:, 7, 0:PW]).then_inc(S["gxT_hi"], 1)

            def route_keep(g):
                act.wait_ge(S["glT_done"], g + 1)
                act.copy(lgT[0:NGATE, :], ps[0:NGATE, 7, PW:2 * PW]).then_inc(S["glT_kept"], 1)

            def route_exp(g):
                act.wait_ge(S["gl_diff"], 2 * g + 2)
                act.activation(ge[:, :, 0:10], gd[:, :, 0:10], ACT.Exp).then_inc(S["gexp_done"], 1)

            def silus(t, i, v):
                act.wait_ge(S["unit_done"], t * UNITS + 2 * v + 2)
                m = t * (UNITS // 2) + v
                if after(t, 1) or v >= 2:
                    act.wait_ge(S["hid_ready"], 2 * m - 2)
                b = bank_of(i, 2 * v)
                act.activation(silu[:, silu_of(i, v)], ps[:, b:b + 2, 0:INTER], ACT.Silu).then_inc(S["silu_done"], 1)

            def keep_high(t, i, q):
                act.wait_ge(S["hT_done"], t * 4 + q + 1)
                n = min(4, HC - 4 * q)
                act.copy(hT_hi[:, 4 * q:4 * q + n, i * P:(i + 1) * P],
                         ps[:, 4 + q % 2, 0:n * P].rearrange("p (c n) -> p c n", c=n)).then_inc(S["hT_hi_ready"], 1)

            def keep_y(g):
                act.wait_ge(S["down_done"], g + 1)
                act.copy(yT, ps[:, 6, 0:PW]).then_inc(S["yT_kept"], 1)

            def moe(g, s, _):
                last = not inside(g + 1, NPAIR)
                for v in range(UNITS // 2):
                    silus(g * 2, 0, v)
                    if v < 4 and after(g, 1):
                        keep_high(g * 2 - 1, 1, v)
                    if v == 0 and not last:
                        route_high(g + 1, 1 - s)
                    if v == 4 and not last:
                        route_keep(g + 1)
                if not last:
                    route_exp(g + 1)
                if after(g, 1):
                    keep_y(g - 1)
                for v in range(UNITS // 2):
                    silus(g * 2 + 1, 1, v)
                    if v < 4:
                        if v == 0 and after(g, 1):
                            act.wait_ge(S["down_done"], g)
                        keep_high(g * 2, 0, v)

            route_high(0, 0)
            route_keep(0)
            route_exp(0)
            steps(act, 0, 2, NPAIR - 2, NPAIR, moe)
            for q in range(4):
                keep_high(NT - 1, 1, q)
            keep_y(NPAIR - 1)

            def q1_high(g, s):
                act.wait_ge(S["axT_done"], g + 1)
                act.copy(xT_hi[:, s], ps[:, s, 0:PW]).then_inc(S["axT_hi"], 1)

            def q1_keep(g, s):
                act.wait_ge(S["aq_done"], g + 1)
                act.activation(q1T[:, s], ps[:, 4, 0:PW], ACT.Identity,
                               bias=const[:, C_BQ:C_BQ + 1]).then_inc(S["aq_kept"], 1)

            def exps1(g, s):
                act.wait_ge(S["adiff"], g + 1)
                act.wait_ge(S["pblk_zero"], 1)
                for b in range(2):
                    rows = slice(b * SEQ, (b + 1) * SEQ)
                    e = act.activation(pblk[rows, s, :, b * SEQ:(b + 1) * SEQ], pdiff[rows, s], ACT.Exp)
                e.then_inc(S["aexp_done"], 1)

            def keep_p1T(g, s):
                act.wait_ge(S["apT_done"], g + 1)
                act.copy(p1T[:, s].rearrange("p t k -> p (t k)"), ps[:, 5, 0:PW]).then_inc(S["apT_kept"], 1)

            def attend1(g, s, _):
                if inside(g + 2, NPAIR):
                    q1_high(g + 2, s)
                if inside(g, NPAIR):
                    keep_p1T(g, s)
                if inside(g + 1, NPAIR):
                    exps1(g + 1, 1 - s)
                if inside(g + 2, NPAIR):
                    q1_keep(g + 2, s)

            steps(act, -2, 2, NPAIR - 2, NPAIR, attend1)

            act.wait_ge(S["b_scaled"], 1)

            def ff_high(g, s):
                act.wait_ge(S["fxT_done"], g + 1)
                act.copy(xT_hi[:, s], ps[:, 4, 0:PW]).then_inc(S["fxT_hi"], 1)

            def ff_n(g, s):
                for c in range(FC):
                    if c % 2 == 0:
                        act.wait_ge(S["up_done"], g * 4 + c + 2)
                    if c == 0 and after(g, 2):
                        act.wait_ge(S["frac_ready"], g - 1)
                    act.activation(n_i[:, s, c * PW:(c + 1) * PW], ps[:, 2 * s + c // 2, (c % 2) * PW:(c % 2 + 1) * PW],
                                   ACT.Identity, bias=b_q[:, c:c + 1], scale=QUANT).then_inc(S["n_ready"], 1)

            def ff_gelu(g, s):
                act.wait_ge(S["base_ready"], g + 1)
                if after(g, 2):
                    act.wait_ge(S["y_ready"], g - 1)
                act.activation(g_lo[:, s], base_i[:, s], ACT.Gelu, scale=1 / QUANT).then_inc(S["glo_done"], 1)
                act.activation(g_hi[:, s], base_i[:, s], ACT.Gelu, scale=1 / QUANT,
                               bias=quarter[:]).then_inc(S["ghi_done"], 1)

            def ff_yhigh(g, s):
                act.wait_ge(S["y_ready"], g + 1)
                if after(g, 2):
                    act.wait_ge(S["fd_done"], g - 1)
                act.copy(yq_hi[:, s].rearrange("p c n -> p (c n)"), y_i[:, s]).then_inc(S["yq_hi_ready"], 1)

            def ff_out(g, s):
                act.wait_ge(S["fd_done"], g + 1)
                act.wait_ge(S["fo_done"], g + 1)
                act.activation(oq_i[:, s], ps[:, 5 + s, 0:PW], ACT.Identity,
                               bias=b_q[:, FC:FC + 1]).then_inc(S["oq_int"], 1)

            def feed(g, s, _):
                if inside(g - 2, NPAIR):
                    ff_out(g - 2, s)
                if inside(g + 2, NPAIR):
                    ff_high(g + 2, s)
                if inside(g + 1, NPAIR):
                    ff_gelu(g + 1, 1 - s)
                if inside(g + 2, NPAIR):
                    ff_n(g + 2, s)
                if inside(g, NPAIR):
                    ff_yhigh(g, s)

            steps(act, -2, 2, NPAIR - 2, NPAIR + 2, feed)

        @block.vector
        def _(dve):
            dve.sem_inc(S["xT_lo_ready"], 1)
            dve.sem_inc(S["v1_kept"], 4)
            dve.memset(quarter[:], 0.25)
            dve.memset(minus_half[:], -0.5).then_inc(S["consts_set"], 1)
            dve.sem_inc(S["x4_ready"], 4)

            def split_weights_low(cols, n):
                dve.wait_ge(S["w_hi_ready"], n)
                dve.tensor_tensor(w_lo[:, cols], wraw[:, cols], w_hi[:, cols].bitcast(F32),
                                  ALU.subtract).then_inc(S["w_lo_ready"], 1)

            def stats(t, g, i, norm):
                dve.bn_stats(moments[:, i], x[:, t, :]).then_inc(S[f"moments{norm}"], 1)
                hold(dve, f"rstd{norm}", g + 1)
                hold(dve, f"moments{norm}", t + 1)
                dve.bn_aggr(meanvar[:, i], moments[:, i]).then_inc(S[f"stats{norm}"], 1)

            def normalise(g, s, ready, rstd_name):
                dve.wait_ge(S[rstd_name], g + 2)
                for i in range(2):
                    t = g * 2 + i
                    n = dve.tensor_scalar(xn[:, s, i], x[:, t, :], mean[:, one(t)], rstd[:, one(t)],
                                          ALU.subtract, ALU.mult)
                n.then_inc(S[ready], 1)

            def low_part(out, src, high, done):
                return dve.tensor_tensor(out, src, high.bitcast(F32), ALU.subtract).then_inc(S[done], 1)

            def keep_projections(g, s, _):
                if inside(g, NPAIR):
                    dve.wait_ge(S["xT_hi_ready"], g + 2)
                    if after(g, 2):
                        dve.wait_ge(S["q_done"], g - 1)
                    low_part(xT_lo[:, s], ps[:, 0, 0:PW], xT_hi[:, s], "xT_lo_ready")
                if inside(g + 1, NPAIR):
                    if after(g + 1, 2):
                        dve.wait_ge(S["xT_done"], g)
                    normalise(g + 1, 1 - s, "xn_ready", "rstd0")
                if inside(g + 2, NPAIR):
                    for i in range(2):
                        stats(g * 2 + 4 + i, g + 2, i, 0)
                if inside(g, NPAIR):
                    keep_values(g, s)

            def keep_values(g, s):
                for i in range(2):
                    dve.wait_ge(S["v0_kept"], 2 * g + i + 5)
                    for b in range(2):
                        rows = slice(b * SEQ, (b + 1) * SEQ)
                        o = dve.tensor_tensor(v1[rows, g * 2 + i, :],
                                              ps[rows, 4 + 2 * s + i, b * PW + P:(b + 1) * PW],
                                              bv_rows[rows], ALU.add)
                    o.then_inc(S["v1_kept"], 1)

            dve.wait_ge(S["x_in"], 16)
            keep_projections(-2, 0, -1)
            split_weights_low(slice(0, W_EARLY), 1)
            dve.wait_ge(S["const_in"], 16)
            dve.tensor_scalar(b_q[:], const[:, C_B1:C_B1 + FC + 1], QUANT, None, ALU.mult).then_inc(S["b_scaled"], 1)
            keep_projections(-1, 1, -1)
            dve.wait_ge(S["x_rest_in"], 16)
            keep_projections(0, 0, 0)
            split_weights_low(slice(W_EARLY, W_COLS), 2)
            steps(dve, 1, 2, NPAIR - 2, NPAIR, keep_projections)

            def diffs(t, s):
                dve.wait_ge(S["scores_done"], t + 1)
                sc = ps[:, 0:4, 0:256].rearrange("p a (j k) -> p a j k", k=SEQ)
                dve.tensor_reduce(rowmax[:, s], sc, AX_X, ALU.max).then_inc(S["rowmax_ready"], 1)
                dve.wait_ge(S["rowmax_ready"], t + 1)
                if after(t, 2):
                    dve.wait_ge(S["probT_done"], 2 * t - 2)
                m = rowmax[:, s].unsqueeze(3).broadcast_to([P, 4, 4, SEQ])
                d = prob[:, s].rearrange("p (a j k) -> p a j k", a=4, j=4)
                dve.tensor_tensor(d, sc, m, ALU.subtract).then_inc(S["diff_ready"], 1)

            def heads_out(t, s):
                dve.wait_ge(S["pv_done"], t + 1)
                dve.reciprocal(rden, ps[:, 6, P:2 * P]).then_inc(S["rden_ready"], 1)
                dve.wait_ge(S["rden_ready"], t + 1)
                if after(t, 2):
                    dve.wait_ge(S["wo_done"], t - 1)
                dve.scalar_tensor_tensor(out=oT[:, s], in0=ps[:, 6, 0:P], scalar=float(REPEAT0),
                                         in1=rden, op0=ALU.mult, op1=ALU.mult).then_inc(S["oT_ready"], 1)

            def add_x(t, g, i):
                dve.wait_ge(S["wo_done"], t + 1)
                dve.tensor_tensor(x[:, t, :], ps[:, 7, 0:P], x[:, t, :], ALU.add).then_inc(S["x1_ready"], 1)
                hold(dve, "x1_ready", t + 1)
                stats(t, g, i, 1)

            def attend(t, s, half):
                if inside(t, NT):
                    diffs(t, s)
                if inside(t - 2, NT):
                    heads_out(t - 2, s)
                if inside(t - 3, NT):
                    add_x(t - 3, half - 2 + s, 1 - s)

            steps(dve, 0, 4, NT, NT + 3, attend)

            own = Steps(dve, S["route_steps"])

            def route_norm(g, s):
                normalise(g, s, "gxn_ready", "rstd1")

            def route_low(g, s):
                dve.wait_ge(S["gxT_hi"], g + 1)
                low_part(xT_lo[:, s], ps[:, 7, 0:PW], xT_hi[:, s], "gxT_lo")

            def route_diff(g):
                own.n = g * ROUTE_STEPS
                dve.wait_ge(S["gl_done"], g + 1)
                lg = ps[:, 7, 0:32].rearrange("p (t n) -> p t n", t=2)
                own.did(dve.tensor_reduce(gl[:, :, 0], lg[:, :, 0:NEXP], AX_X, ALU.max))
                dve.tensor_scalar(gd[:, :, 8:10], lg[:, :, 8:10], -1.0, None, ALU.mult).then_inc(S["gl_diff"], 1)
                own.wait()
                dve.tensor_tensor(gd[:, :, 0:NEXP], lg[:, :, 0:NEXP],
                                  gl[:, :, 0:1].broadcast_to([P, 2, NEXP]), ALU.subtract).then_inc(S["gl_diff"], 1)

            def route_weights(g, s):
                own.n = g * ROUTE_STEPS + 1
                dve.wait_ge(S["gexp_done"], g + 1)
                own.did(dve.tensor_reduce(gl[:, :, 1], ge[:, :, 0:NEXP], AX_X, ALU.add))
                own.did(dve.tensor_scalar(gl[:, :, 2:3], ge[:, :, 8:9], 1.0, None, ALU.add))
                own.wait()
                own.did(dve.reciprocal(gl[:, :, 4:6], gl[:, :, 1:3]))
                own.wait()
                own.did(dve.tensor_tensor(gp[:], ge[:, :, 0:NEXP], gl[:, :, 4:5].broadcast_to([P, 2, NEXP]), ALU.mult))
                own.wait()
                for i in range(2):
                    mine = gp[:, i].unsqueeze(2).broadcast_to([P, NEXP, NEXP])
                    other = gp[:, i].unsqueeze(1).broadcast_to([P, NEXP, NEXP])
                    own.did(dve.tensor_tensor(beats[:, i], other, mine, ALU.is_gt))
                    own.did(dve.tensor_tensor(ties[:, i], other, mine, ALU.is_equal))
                own.wait()
                own.did(dve.tensor_tensor(ties[:], ties[:], tri.unsqueeze(1).broadcast_to([P, 2, 8, 8]), ALU.mult))
                own.wait()
                own.did(dve.tensor_tensor(beats[:], beats[:], ties[:], ALU.add))
                own.wait()
                own.did(dve.tensor_reduce(rank[:], beats[:], AX_X, ALU.add))
                own.wait()
                own.did(dve.scalar_tensor_tensor(out=wexp[:, s, :, 0:NEXP], in0=rank[:], scalar=float(TOPK) - 0.5,
                                                 in1=gp[:], op0=ALU.is_lt, op1=ALU.mult))
                own.did(dve.tensor_copy(wexp[:, s, :, NEXP:UNITS], gl[:, :, 5:6].broadcast_to([P, 2, 2])))
                own.wait()

            def products(t, s, i, u):
                if u % 2 == 0:
                    dve.wait_ge(S["silu_done"], t * (UNITS // 2) + u // 2 + 1)
                if u == 0 and after(t, 2):
                    dve.wait_ge(S["hT_done"], (t - 1) * 4)
                dve.scalar_tensor_tensor(out=hid[:, i, u * INTER:(u + 1) * INTER], in0=silu[:, silu_of(i, u // 2), u % 2],
                                         scalar=wexp[:, s, i, u:u + 1], in1=ps[:, bank_of(i, u), INTER:UW],
                                         op0=ALU.mult, op1=ALU.mult).then_inc(S["hid_ready"], 1)

            def keep_low(t, i, q):
                dve.wait_ge(S["hT_hi_ready"], t * 4 + q + 1)
                n = min(4, HC - 4 * q)
                dve.tensor_tensor(hT_lo[:, 4 * q:4 * q + n, i * P:(i + 1) * P],
                                  ps[:, 4 + q % 2, 0:n * P].rearrange("p (c n) -> p c n", c=n),
                                  hT_hi[:, 4 * q:4 * q + n, i * P:(i + 1) * P].bitcast(F32),
                                  ALU.subtract).then_inc(S["hT_lo_ready"], 1)

            def add_y(g, i):
                t = g * 2 + i
                dve.wait_ge(S["y_done"], g + 1)
                dve.tensor_tensor(x[:, t, :], ps[:, 6, PW + i * P:PW + (i + 1) * P], x[:, t, :],
                                  ALU.add).then_inc(S["x2_ready"], 1)
                hold(dve, "x2_ready", t + 1)
                stats(t, g, i, 2)

            def moe(g, s, _):
                for u in range(UNITS):
                    products(g * 2, s, 0, u)
                    if u % 2 == 1 and u < 9 and after(g, 1):
                        keep_low(g * 2 - 1, 1, u // 2)
                    if u == 2 and inside(g + 1, NPAIR):
                        route_low(g + 1, 1 - s)
                if inside(g + 1, NPAIR):
                    route_diff(g + 1)
                    if inside(g + 2, NPAIR):
                        route_norm(g + 2, s)
                    route_weights(g + 1, 1 - s)
                for u in range(UNITS):
                    products(g * 2 + 1, s, 1, u)
                    if u % 2 == 1 and u < 9:
                        keep_low(g * 2, 0, u // 2)
                    if u == 4 and after(g, 1):
                        add_y(g - 1, 0)
                    if u == 6 and after(g, 1):
                        add_y(g - 1, 1)

            dve.wait_ge(S["k_staged"], NT)
            dve.wait_ge(S["q_staged"], NT)
            dve.wait_ge(S["vblk_staged"], 2 * NT)
            dve.memset(hid[:, :, UNITS * INTER:HPAD], 0.0).then_inc(S["hid_zero"], 1)
            dve.wait_ge(S["hid_zero"], 1)
            route_norm(0, 0)
            route_low(0, 0)
            route_diff(0)
            route_norm(1, 1)
            route_weights(0, 0)
            steps(dve, 0, 2, NPAIR - 2, NPAIR, moe)
            for q in range(4):
                keep_low(NT - 1, 1, q)
            add_y(NPAIR - 1, 0)
            add_y(NPAIR - 1, 1)

            def q1_norm(g, s):
                if after(g, 2):
                    dve.wait_ge(S["axT_done"], g - 1)
                normalise(g, s, "axn_ready", "rstd2")

            def q1_low(g, s):
                dve.wait_ge(S["axT_hi"], g + 1)
                if after(g, 2):
                    dve.wait_ge(S["aq_done"], g - 1)
                low_part(xT_lo[:, s], ps[:, s, 0:PW], xT_hi[:, s], "axT_lo")

            def diffs1(g, s):
                dve.wait_ge(S["as_done"], g + 1)
                sc = ps[:, 2 + s, 0:2 * SEQ].rearrange("p (t k) -> p t k", t=2)
                dve.tensor_reduce(stat1[:, s, 0, :], sc, AX_X, ALU.max).then_inc(S["amax"], 1)
                dve.wait_ge(S["amax"], g + 1)
                dve.tensor_tensor(pdiff[:, s], sc, stat1[:, s, 0, :].unsqueeze(2).broadcast_to([P, 2, SEQ]),
                                  ALU.subtract).then_inc(S["adiff"], 1)

            def sums1(g, s):
                dve.wait_ge(S["aexp_done"], g + 1)
                dve.tensor_reduce(stat1[:, s, 1, :], pblk[:, s], AX_X, ALU.add).then_inc(S["astat"], 1)
                dve.wait_ge(S["astat"], 2 * g + 1)
                dve.reciprocal(stat1[:, s, 2, :], stat1[:, s, 1, :]).then_inc(S["astat"], 1)
                dve.wait_ge(S["astat"], 2 * g + 2)

            def add_v(g, s):
                dve.wait_ge(S["ao_done"], g + 1)
                for i in range(2):
                    t = g * 2 + i
                    dve.scalar_tensor_tensor(out=x[:, t, :], in0=ps[:, 6 + s, i * P:(i + 1) * P],
                                             scalar=stat1[:, s, 2, i:i + 1], in1=x[:, t, :],
                                             op0=ALU.mult, op1=ALU.add).then_inc(S["x3_ready"], 1)
                    hold(dve, "x3_ready", t + 1)
                    stats(t, g, i, 3)

            dve.memset(pblk_, 0.0).then_inc(S["pblk_zero"], 1)
            def attend1(g, s, _):
                if inside(g + 2, NPAIR):
                    q1_norm(g + 2, s)
                if inside(g + 1, NPAIR):
                    diffs1(g + 1, 1 - s)
                if inside(g + 2, NPAIR):
                    q1_low(g + 2, s)
                if inside(g, NPAIR):
                    sums1(g, s)
                    add_v(g, s)

            steps(dve, -2, 2, NPAIR - 2, NPAIR, attend1)

            def ff_norm(g, s):
                if after(g, 2):
                    dve.wait_ge(S["fxT_done"], g - 1)
                normalise(g, s, "fxn_ready", "rstd3")

            def ff_low(g, s):
                dve.wait_ge(S["fxT_hi"], g + 1)
                low_part(xT_lo[:, s], ps[:, 4, 0:PW], xT_hi[:, s], "fxT_lo")

            def ff_knots(g, s):
                dve.wait_ge(S["n_ready"], 4 * g + 4)
                if after(g, 2):
                    dve.wait_ge(S["ghi_done"], g - 1)
                dve.tensor_scalar(base_i[:, s], n_i[:, s], -KNOT, None, ALU.bitwise_and).then_inc(S["base_ready"], 1)
                dve.tensor_scalar(frac_i[:, s], n_i[:, s], KNOT - 1, None, ALU.bitwise_and).then_inc(S["frac_ready"], 1)

            def ff_lerp(g, s):
                dve.wait_ge(S["slope_ready"], g + 1)
                dve.scalar_tensor_tensor(out=g_hi[:, s], in0=frac_i[:, s], scalar=QUANT / KNOT, in1=g_hi[:, s],
                                         op0=ALU.mult, op1=ALU.mult).then_inc(S["rise_ready"], 1)
                dve.wait_ge(S["rise_ready"], g + 1)
                if after(g, 2):
                    dve.wait_ge(S["yq_lo_ready"], g - 1)
                dve.scalar_tensor_tensor(out=y_i[:, s], in0=g_lo[:, s], scalar=QUANT, in1=g_hi[:, s],
                                         op0=ALU.mult, op1=ALU.add).then_inc(S["y_ready"], 1)

            def ff_ylow(g, s):
                dve.wait_ge(S["yq_hi_ready"], g + 1)
                dve.tensor_tensor(yq_lo[:, s].rearrange("p c n -> p (c n)"), y_i[:, s],
                                  yq_hi[:, s].rearrange("p c n -> p (c n)").bitcast(F32),
                                  ALU.subtract).then_inc(S["yq_lo_ready"], 1)

            def ff_scale(g, s):
                dve.wait_ge(S["oq_int"], g + 3)
                dve.tensor_scalar(oq[:, s], oq_i[:, s], 1 / QUANT, None, ALU.mult).then_inc(S["oq_ready"], 1)

            def ff_add(g, s):
                dve.wait_ge(S["fo_done"], g + 3)
                for i in range(2):
                    t = g * 2 + i
                    dve.tensor_tensor(x[:, t, :], ps[:, 5 + s, PW + i * P:PW + (i + 1) * P], x[:, t, :],
                                      ALU.add).then_inc(S["x4_ready"], 1)

            def feed(g, s, _):
                if inside(g + 2, NPAIR):
                    ff_norm(g + 2, s)
                if inside(g - 2, NPAIR):
                    ff_scale(g - 2, s)
                if inside(g + 1, NPAIR):
                    ff_knots(g + 1, 1 - s)
                if inside(g - 1, NPAIR):
                    ff_ylow(g - 1, 1 - s)
                if inside(g + 2, NPAIR):
                    ff_low(g + 2, s)
                if inside(g - 2, NPAIR):
                    ff_add(g - 2, s)
                if inside(g, NPAIR):
                    ff_lerp(g, s)

            steps(dve, -2, 2, NPAIR - 2, NPAIR + 2, feed)

        @block.gpsimd
        def _(pool):
            pool.wait_ge(S["consts_set"], 1)
            pool.sem_inc(S["rstd0"], 1)

            def free_meanvar(norm):
                pool.wait_ge(S[f"rstd{norm - 1}"], NPAIR + 1)
                pool.sem_inc(S[f"rstd{norm}"], 1)

            def rstds(g, norm):
                hold(pool, f"stats{norm}", 2 * g + 2)
                cols = bass.ds(g * 2, 2)
                pool.tensor_copy(mean[:, cols], meanvar[:, :, 0]).then_inc(S[f"veps{norm}"], 1)
                pool.tensor_scalar(veps[:], meanvar[:, :, 1], EPS, 1.0, ALU.add, ALU.mult).then_inc(S[f"veps{norm}"], 1)
                hold(pool, f"veps{norm}", 2 * g + 2)
                pool.tensor_tensor(rstd[:, cols], veps[:], minus_half[:], ALU.pow).then_inc(S[f"rstd{norm}"], 1)

            def context_low(g, s):
                hold(pool, "ctx_hi_ready", g + 1)
                src = ctxT[:, s].rearrange("p (b n) -> p b n", b=4).unsqueeze(2).broadcast_to([P, 4, 2, SEQ])
                pool.tensor_tensor(ctx_lo[:, s], src, ctx_hi[:, s].bitcast(F32), ALU.subtract).then_inc(S["ctx_lo_ready"], 1)

            rstds(0, 0)
            rstds(1, 0)
            context_low(0, 0)

            def project(g, s, _):
                if inside(g + 1, NPAIR):
                    context_low(g + 1, 1 - s)
                if inside(g + 2, NPAIR):
                    rstds(g + 2, 0)

            steps(pool, 0, 2, NPAIR - 2, NPAIR, project)
            pool.memset(vblk_, 0.0).then_inc(S["vblk_zero"], 1)
            pool.wait_ge(S["vblk_zero"], 1)

            def stage_k(t, s):
                if after(t, 2):
                    hold(pool, "scores_done", t - 1)
                src = k0T[:, bass.ds(t * P, P)].rearrange("p (b k) -> p b k", b=2)
                msk = const[:, C_MASK:C_MASK + 4]
                pool.tensor_tensor(kexp[:, s], src.unsqueeze(2).broadcast_to([P, 2, 4, SEQ]),
                                   msk.unsqueeze(1).unsqueeze(3).broadcast_to([P, 2, 4, SEQ]),
                                   ALU.mult).then_inc(S["k_staged"], 1)

            def stage_v(t, s):
                if after(t, 2):
                    hold(pool, "pv_done", t - 1)
                src = v0dup[:, bass.ds(t * 2, 2), :].rearrange("p b (j a m) -> p (b j) a m", j=4, a=2)
                dst = vblk[:, s].rearrange("p b (j a) n -> p (b j) a n", a=2)
                for par in range(2):
                    cols = slice(par * 16, par * 16 + 16)
                    own = ones32[:, par, cols].unsqueeze(1).broadcast_to([P, 8, 16])
                    pool.tensor_tensor(dst[:, :, par, cols], src[:, :, par], own,
                                       ALU.mult).then_inc(S["vblk_staged"], 1)

            def split_low(t):
                n, m = UNITS * UW // NT, HC * P // NT
                hold(pool, "w_high", t + 1)
                pool.tensor_tensor(gu_lo[:, bass.ds(t * n, n)], gu_raw[:, bass.ds(t * n, n)],
                                   gu_hi[:, bass.ds(t * n, n)].bitcast(F32), ALU.subtract).then_inc(S["w_low"], 1)
                pool.tensor_tensor(down_lo[:, bass.ds(t * m, m)], down_raw[:, bass.ds(t * m, m)],
                                   down_hi[:, bass.ds(t * m, m)].bitcast(F32), ALU.subtract).then_inc(S["w_low"], 1)

            def attend(t, s, half):
                if inside(t, NT):
                    stage_k(t, s)
                if inside(t - 1, NT):
                    stage_v(t - 1, 1 - s)
                if inside(t - 2, NT):
                    split_low(t - 2)
                if s == 1 and inside(half - 2, NPAIR):
                    rstds(half - 2, 1)

            free_meanvar(1)
            pool.wait_ge(S["k0_kept"], NPAIR + 1)
            pool.wait_ge(S["v0_kept"], NT + 4)
            steps(pool, 0, 4, NT, NT + 4, attend)

            free_meanvar(2)
            with pool.Fori(0, NPAIR) as g:
                rstds(g, 2)

            def stage_k1(g, s):
                if after(g, 2):
                    hold(pool, "as_done", g - 1)
                pool.tensor_copy(k1s[:, s], k1T[:, pair(g)]).then_inc(S["ak_staged"], 1)

            def attend1(g, s, _):
                if inside(g, NPAIR):
                    stage_k1(g, s)
                if inside(g - 3, NPAIR):
                    rstds(g - 3, 3)

            free_meanvar(3)
            steps(pool, 0, 4, NPAIR, NPAIR + 3, attend1)

            def ff_slope(g, s):
                pool.wait_ge(S["glo_done"], g + 1)
                pool.wait_ge(S["ghi_done"], g + 1)
                pool.tensor_tensor(g_hi[:, s], g_hi[:, s], g_lo[:, s], ALU.subtract).then_inc(S["slope_ready"], 1)

            steps(pool, 0, 2, NPAIR, NPAIR, lambda g, s, _: ff_slope(g, s))


def kernel(**inputs):
    import concourse.bacc as bacc
    from concourse.bass_utils import run_bass_kernel_spmd

    a = {k: np.asarray(v) for k, v in inputs.items()}

    def tokens_on_partitions(v):
        return v.reshape(NT, P, P).transpose(1, 0, 2)

    def chunks(v):
        return v.reshape(-1, P, v.shape[1]).transpose(1, 0, 2).reshape(P, -1)

    gate = np.concatenate([a["L0_ffn_gate_w"], a["L0_ffn_shared_expert_gate_w"],
                           np.zeros((NGATE - NEXP - 1, P), np.float32)])
    w = np.concatenate([a["L0_xattn_Wq"].T, a["L0_xattn_Wk"].T, a["L1_xattn_Wk"].T, a["L1_xattn_Wq"].T,
                        a["L0_xattn_Wv"].T, a["L1_xattn_Wv"].T, a["L1_ffn_w1"], chunks(a["L1_ffn_w2"]), gate.T], axis=1)
    sg, su = (a[f"L0_ffn_shared_{n}_w"].reshape(-1, INTER, P) for n in ("gate", "up"))
    gu = np.concatenate([a["L0_ffn_experts_gate_up"], np.concatenate([sg, su], axis=1)]).reshape(UNITS * UW, P).T
    down = np.concatenate([a["L0_ffn_experts_down"].transpose(0, 2, 1).reshape(NEXP * INTER, P),
                           a["L0_ffn_shared_down_w"].T, np.zeros((HPAD - UNITS * INTER, P), np.float32)])
    p = np.arange(P)
    mask = (p[:, None] // HD % 4 == np.arange(4)).astype(np.float32)
    tri = np.broadcast_to((np.arange(8)[None, :] < np.arange(8)[:, None]).astype(np.float32).reshape(1, 64), (P, 64))
    ones = (np.arange(64)[None, :] % 32 // HD == 2 * (np.arange(64)[None, :] // 32) + p[:, None] // SEQ).astype(np.float32)
    const = np.concatenate([np.eye(P, dtype=np.float32), a["L0_xattn_Wo"].T,
                            np.broadcast_to(a["L1_xattn_bv"], (P, P)), mask, tri, ones,
                            a["L1_xattn_bq"][:, None], a["L1_xattn_bk"][:, None],
                            a["L1_ffn_b1"].reshape(FC, P).T, a["L1_ffn_b2"][:, None]], axis=1)
    arrays = {
        "in_x": tokens_on_partitions(a["x"]), "in_ctx": a["ctx_1024"].reshape(NT * P, P).T, "in_w": w, "in_gu": gu,
        "in_down": chunks(down), "in_const": const,
    }
    arrays = {k: np.ascontiguousarray(v) for k, v in arrays.items()}
    nc = bacc.Bacc("TRN2", target_bir_lowering=False, num_devices=1)
    args = [nc.dram_tensor(k, v.shape, F32, kind="ExternalInput").ap() for k, v in arrays.items()]
    out = nc.dram_tensor("out_0", (P, NT, P), F32, kind="ExternalOutput").ap()
    two_layers(nc, *args, out)
    r = run_bass_kernel_spmd(nc, [arrays], core_ids=[0])
    return np.ascontiguousarray(r.results[0]["out_0"].transpose(1, 0, 2)).reshape(BATCH, SEQ, P)
```

```python
from contextlib import ExitStack

import numpy as np

import concourse.bass as bass
from concourse import mybir

F32 = mybir.dt.float32
F32R = mybir.dt.float32r
I32 = mybir.dt.int32
ALU = mybir.AluOpType
ACT = mybir.ActivationFunctionType
AX_X = mybir.AxisListType.X

P = 128
BATCH, SEQ = 32, 64
NT = BATCH * SEQ // P
NPAIR = NT // 2
PW = 2 * P
HEADS, HD = 16, 8
NEXP, TOPK = 8, 2
INTER = 176
SHARED = 352
UNITS = NEXP + SHARED // INTER
UW = 2 * INTER
HC = -(-UNITS * INTER // P)
HPAD = HC * P
FF = 512
FC = FF // P
EPS = 1e-5
SCALE0 = HD ** -0.5
REPEAT0 = 3
QUANT = 256.0
KNOT = 64

W_Q0, W_K0, W_K1, W_Q1, W_V, W_UP = 0, 128, 256, 384, 512, 768
W_DOWN = W_UP + FF
W_GATE = W_DOWN + FF
W_EARLY = W_UP
NGATE = 10
W_COLS = W_GATE + NGATE
C_ID, C_WO, C_BV, C_MASK, C_TRI, C_ONES = 0, 128, 256, 384, 388, 452
C_BQ = C_ONES + 64
C_BK, C_B1 = C_BQ + 1, C_BQ + 2
C_COLS = C_B1 + FC + 1
WARM_UP = 7
DOWN_PARTS = (0, 3, 6, 9, 12, HC)
ROUTE_STEPS = 14


def pair(g):
    return bass.ds(g * PW, PW)


def one(t):
    return bass.ds(t, 1)


def after(step, n):
    return not isinstance(step, int) or step >= n


def inside(step, n):
    return not isinstance(step, int) or 0 <= step < n


def is_last_pair(g):
    return isinstance(g, int) and g == NPAIR - 1


def steps(eng, first, lo, hi, stop, step, unroll=2):
    for k in range(first, lo):
        step(k, k % 2, k // 2)
    with eng.Fori(lo // unroll, hi // unroll) as r:
        for i in range(unroll):
            step(r * unroll + i, i % 2, r * (unroll // 2) + i // 2)
    for k in range(hi, stop):
        step(k, k % 2, k // 2)


def values_bank(t):
    return 2 if isinstance(t, int) and t == NT - 1 else 6


def bank_of(i, u):
    return (i * UNITS + u) % 4


def scores_bank(t):
    return 4 if isinstance(t, int) and t == 1 else 0


def part_of_down(i):
    return range(DOWN_PARTS[i], DOWN_PARTS[i + 1])


class Steps:

    def __init__(self, eng, sem, base=0):
        self.eng, self.sem, self.n = eng, sem, base

    def did(self, ins):
        ins.then_inc(self.sem, 1)
        self.n = self.n + 1

    def wait(self):
        self.eng.wait_ge(self.sem, self.n)


def two_layers(nc, x_d, ctx_d, w_d, gu_d, down_d, const_d, out_d):
    with ExitStack() as ctx:
        def sb(name, shape, dt=F32):
            return ctx.enter_context(nc.sbuf_tensor(name, shape, dt))

        def sem(name):
            return ctx.enter_context(nc.semaphore(name))

        x = sb("x", [P, NT, P])
        const = sb("const", [P, C_COLS])
        w_hi = sb("w_hi", [P, W_COLS], F32R)
        w_lo = sb("w_lo", [P, W_COLS], F32R)
        gu_hi = sb("gu_hi", [P, UNITS * UW], F32R)
        gu_lo = sb("gu_lo", [P, UNITS * UW], F32R)
        down_hi = sb("down_hi", [P, HC * P], F32R)
        down_lo = sb("down_lo", [P, HC * P], F32R)
        k1T = sb("k1T", [P, NT * P])
        v1 = sb("v1", [P, NT, P])
        moments = sb("moments", [P, 2, 6])
        meanvar = sb("meanvar", [P, 2, 2])
        veps = sb("veps", [P, 2])
        mean = sb("mean", [P, NT])
        rstd = sb("rstd", [P, NT])
        minus_half = sb("minus_half", [P, 2])
        xn = sb("xn", [P, 2, 2, P])
        xT_hi = sb("xT_hi", [P, 2, PW], F32R)
        xT_lo = sb("xT_lo", [P, 2, PW], F32R)

        AR = 2 * HC * PW
        arena_r = sb("arena_r", [P, AR], F32R)
        AF = 20864
        arena_f = sb("arena_f", [P, AF])

        def carve(arena, sizes):
            at, out = 0, []
            for n in sizes:
                out.append(arena[:, at:at + n])
                at += n
            assert at <= arena.shape[1]
            return out

        (k0T, q0T, v0dup, gu_raw, down_raw, kexp_, q_st_, vblk_, prob_, probT_, rden, oT_, ctxT_) = carve(
            arena_f, [NT * P, NT * P, 2 * NT * P, UNITS * UW, HC * P, 2 * 512, 2 * P, 2 * 512, 2 * 1024,
                      2 * 1024, P, 2 * P, 2 * PW])
        v0dup = v0dup.rearrange("p (b f) -> p b f", f=P)
        kexp = kexp_.rearrange("p (s b j k) -> p s b j k", s=2, b=2, j=4)
        q_st = q_st_.rearrange("p (s n) -> p s n", s=2)
        vblk = vblk_.rearrange("p (s b c n) -> p s b c n", s=2, b=2, c=8)
        prob = prob_.rearrange("p (s n) -> p s n", s=2)
        probT = probT_.rearrange("p (s c n) -> p s c n", s=2, c=8)
        oT = oT_.rearrange("p (s n) -> p s n", s=2)
        ctxT = ctxT_.rearrange("p (s n) -> p s n", s=2)
        wraw = prob_[:, 0:W_COLS]
        ctx_hi_, ctx_lo_ = carve(arena_r, [4 * PW, 4 * PW])
        ctx_hi = ctx_hi_.rearrange("p (s b r n) -> p s b r n", s=2, b=4, r=2)
        ctx_lo = ctx_lo_.rearrange("p (s b r n) -> p s b r n", s=2, b=4, r=2)
        rowmax = sb("rowmax", [P, 2, 4, 4])

        hT_hi, hT_lo = (a.rearrange("p (c n) -> p c n", c=HC) for a in carve(arena_r, [HC * PW] * 2))
        hid_, act_, yT, lgT = carve(arena_f, [2 * HPAD, 2 * 2 * INTER, PW, PW])
        hid = hid_.rearrange("p (s n) -> p s n", s=2)
        silu = act_.rearrange("p (s n) -> p s n", s=4)
        gl = sb("gl", [P, 2, 16])
        gd = sb("gd", [P, 2, 12])
        ge = sb("ge", [P, 2, 12])
        gp = sb("gp", [P, 2, 8])
        beats = sb("beats", [P, 2, 8, 8])
        ties = sb("ties", [P, 2, 8, 8])
        rank = sb("rank", [P, 2, 8])
        wexp = sb("wexp", [P, 2, 2, UNITS])

        q1T_, k1s_, pd_, pblk_, pT_ = carve(arena_f[:, 5504:], [2 * PW, 2 * PW, 2 * P, 2 * PW, 2 * PW])
        q1T = q1T_.rearrange("p (s n) -> p s n", s=2)
        k1s = k1s_.rearrange("p (s n) -> p s n", s=2)
        pdiff = pd_.rearrange("p (s t k) -> p s t k", s=2, t=2)
        pblk = pblk_.rearrange("p (s t k) -> p s t k", s=2, t=2)
        p1T = pT_.rearrange("p (s t k) -> p s t k", s=2, t=2)
        stat1 = sb("stat1", [P, 2, 3, 2])

        n_, base_, frac_, g0_, g1_, y_, oq_ = carve(arena_f[:, 7808:], [2 * 1024] * 6 + [2 * PW])
        (n_i, base_i, frac_i) = (a.bitcast(I32).rearrange("p (s n) -> p s n", s=2) for a in (n_, base_, frac_))
        g_lo = g0_.rearrange("p (s n) -> p s n", s=2)
        g_hi = g1_.rearrange("p (s n) -> p s n", s=2)
        y_i = y_.bitcast(I32).rearrange("p (s n) -> p s n", s=2)
        oq = oq_.rearrange("p (s n) -> p s n", s=2)
        oq_i = oq_.bitcast(I32).rearrange("p (s n) -> p s n", s=2)
        yq_hi_, yq_lo_ = carve(arena_r, [2 * 1024] * 2)
        yq_hi = yq_hi_.rearrange("p (s c n) -> p s c n", s=2, c=FC)
        yq_lo = yq_lo_.rearrange("p (s c n) -> p s c n", s=2, c=FC)
        b_q = sb("b_q", [P, FC + 1])
        quarter = sb("quarter", [P, 1])

        ident = const[:, C_ID:C_ID + P]
        woT = const[:, C_WO:C_WO + P]
        bv_rows = const[:, C_BV:C_BV + P]
        tri = const[:, C_TRI:C_TRI + 64].rearrange("p (i j) -> p i j", i=8)
        ones32 = const[:, C_ONES:C_ONES + 64].rearrange("p (a n) -> p a n", a=2)

        ps = ctx.enter_context(nc.psum_tensor("ps", [P, 8, 512], F32))

        S = {}
        for name in """
            ctx_in0 ctx_in1 w_in w_rest_in const_in x_in x_rest_in gu_in down_in out_done
            held zeros_set consts_set b_scaled w_hi_ready w_lo_ready ctx_hi_ready ctx_lo_ready moments0 stats0 veps0 rstd0 xn_ready
            xT_done xT_hi_ready xT_lo_ready k0_done k0_kept k1_done k1_kept v_done v0_kept v1_kept q_done q_kept
            vblk_zero k_staged q_staged vblk_staged scores_done rowmax_ready diff_ready exp_done probT_done probT_kept
            pv_done rden_ready oT_ready wo_done x1_ready w_high w_low moments1 stats1 veps1 rstd1
            hid_zero gxn_ready gxT_done gxT_hi gxT_lo glT_done glT_kept gl_done gl_diff gexp_done route_steps
            unit_done silu_done hid_ready hT_done hT_hi_ready hT_lo_ready down_done yT_kept y_done x2_ready
            moments2 stats2 veps2 rstd2 centred1 centred2 centred3
            pblk_zero axn_ready axT_done axT_hi axT_lo aq_done aq_kept ak_staged as_done amax adiff aexp_done apT_done
            apT_kept ao_done astat x3_ready moments3 stats3 veps3 rstd3
            fxn_ready fxT_done fxT_hi fxT_lo up_done n_ready base_ready frac_ready glo_done ghi_done slope_ready
            rise_ready y_ready yq_hi_ready yq_lo_ready fd_done oq_int oq_ready fo_done x4_ready
        """.split():
            S[name] = sem(name)

        def hold(eng, name, value):
            eng.wait_ge(S[name], value)
            eng.sem_inc(S["held"], 1)

        def split3(pe, out, w, m_hi, m_lo, n=P, first=True):
            pe.matmul(out, w_hi[:, w:w + n], m_hi, start=first, stop=False)
            pe.matmul(out, w_lo[:, w:w + n], m_hi, start=False, stop=False)
            return pe.matmul(out, w_hi[:, w:w + n], m_lo, start=False, stop=True)

        block = ctx.enter_context(nc.Block())

        @block.sync
        def _(sp):
            sp.dma_start(wraw[:, 0:W_EARLY], w_d[:, 0:W_EARLY]).then_inc(S["w_in"], 16)
            sp.dma_start(x[:, 0:4], x_d[:, 0:4]).then_inc(S["x_in"], 16)
            sp.dma_start(ctxT[:, 0], ctx_d[:, pair(0)]).then_inc(S["ctx_in0"], 16)
            sp.dma_start(const[:], const_d).then_inc(S["const_in"], 16)
            sp.dma_start(ctxT[:, 1], ctx_d[:, pair(1)]).then_inc(S["ctx_in1"], 16)
            sp.dma_start(x[:, 4:NT], x_d[:, 4:NT]).then_inc(S["x_rest_in"], 16)
            sp.dma_start(wraw[:, W_EARLY:W_COLS], w_d[:, W_EARLY:W_COLS]).then_inc(S["w_rest_in"], 16)
            for g in range(2, NPAIR):
                sp.wait_ge(S["ctx_lo_ready"], g - 1)
                sp.dma_start(ctxT[:, g % 2], ctx_d[:, pair(g)]).then_inc(S[f"ctx_in{g % 2}"], 16)
                if g == 3:
                    sp.dma_start(down_raw, down_d).then_inc(S["down_in"], 16)
            sp.dma_start(gu_raw, gu_d).then_inc(S["gu_in"], 16)
            for g in range(NPAIR):
                sp.wait_ge(S["x4_ready"], 2 * g + 6)
                sp.dma_start(out_d[:, 2 * g:2 * g + 2, :], x[:, 2 * g:2 * g + 2, :]).then_inc(S["out_done"], 16)
            sp.wait_ge(S["out_done"], 16 * NPAIR)

        @block.tensor
        def _(pe):
            pe.wait_ge(S["zeros_set"], 1)
            for _ in range(WARM_UP):
                pe.matmul(ps[:, 7, 0:PW], oT[:, 0], oT_, start=True, stop=True)
            pe.wait_ge(S["w_hi_ready"], 1)
            pe.wait_ge(S["w_lo_ready"], 1)
            pe.wait_ge(S["const_in"], 16)

            def project(g, s):
                pe.wait_ge(S["xn_ready"], g + 1)
                pe.wait_ge(S["xT_lo_ready"], g + 1)
                pe.wait_ge(S["xT_hi_ready"], g + 1)
                for i in range(2):
                    mm = pe.transpose(ps[:, 0, i * P:(i + 1) * P], xn[:, s, i, :], ident)
                mm.then_inc(S["xT_done"], 1)
                pe.wait_ge(S["ctx_hi_ready"], g + 1)
                pe.wait_ge(S["ctx_lo_ready"], g + 1)
                pe.wait_ge(S["k0_kept"], g + 1)
                split3(pe, ps[:, 2, 0:PW], W_K0, ctx_hi[:, s, :, 0], ctx_lo[:, s, :, 0]).then_inc(S["k0_done"], 1)
                pe.wait_ge(S["k1_kept"], g + 1)
                split3(pe, ps[:, 3, 0:PW], W_K1, ctx_hi[:, s, :, 0], ctx_lo[:, s, :, 0]).then_inc(S["k1_done"], 1)
                pe.wait_ge(S["v0_kept"], 2 * g + 2)
                pe.wait_ge(S["v1_kept"], 2 * g + 2)
                for i in range(2):
                    for b in range(2):
                        at = (s * 4 + 2 * i + b) * P
                        hi, lo = ctx_hi_[:, at:at + P], ctx_lo_[:, at:at + P]
                        o = ps[:, 4 + 2 * s + i, b * PW:(b + 1) * PW]
                        pe.matmul(o, hi, w_hi[:, W_V:W_V + PW], start=True, stop=False)
                        pe.matmul(o, hi, w_lo[:, W_V:W_V + PW], start=False, stop=False)
                        mm = pe.matmul(o, lo, w_hi[:, W_V:W_V + PW], start=False, stop=True)
                    mm.then_inc(S["v_done"], 1)
                pe.wait_ge(S["xT_lo_ready"], g + 2)
                pe.wait_ge(S["xT_hi_ready"], g + 2)
                pe.wait_ge(S["q_kept"], g + 1)
                split3(pe, ps[:, 1, 0:PW], W_Q0, xT_hi[:, s], xT_lo[:, s]).then_inc(S["q_done"], 1)

            with pe.Fori(0, NPAIR // 2) as r:
                for s in range(2):
                    project(r * 2 + s, s)

            def scores(t, s):
                pe.wait_ge(S["k_staged"], t + 1)
                pe.wait_ge(S["q_staged"], t + 1)
                for h4 in range(4):
                    if h4 % 2 == 0 and after(t, 2):
                        pe.wait_ge(S["diff_ready"], 2 * (t - 1 if after(t, 3) else 0) + h4 // 2 + 1)
                    rows = slice(32 * h4, 32 * h4 + 32)
                    for b in range(2):
                        mm = pe.matmul(ps[b * SEQ:(b + 1) * SEQ, scores_bank(t) + h4, 0:256],
                                       q_st[rows, s, b * SEQ:(b + 1) * SEQ],
                                       kexp_[rows, (2 * s + b) * 256:(2 * s + b + 1) * 256], start=True, stop=True)
                    if h4 % 2 == 1:
                        mm.then_inc(S["scores_done"], 1)

            def turn(t, s):
                pe.wait_ge(S["exp_done"], t + 1)
                for half in range(2):
                    if after(t, 1):
                        pe.wait_ge(S["probT_kept"], 2 * t - 1 + half)
                    for c in range(4):
                        cc = 4 * half + c
                        mm = pe.transpose(ps[:, 4 + half, c * P:(c + 1) * P],
                                          prob[:, s, cc * P:(cc + 1) * P], ident)
                    mm.then_inc(S["probT_done"], 1)

            def values(t, s):
                pe.wait_ge(S["probT_kept"], 2 * t + 2)
                pe.wait_ge(S["vblk_staged"], 2 * t + 2)
                bank = values_bank(t)
                if after(t, 1) and bank == 6:
                    pe.wait_ge(S["oT_ready"], t)
                for b in range(2):
                    q = slice(b * SEQ, (b + 1) * SEQ)
                    for kind in range(2):
                        for par in range(2):
                            for j in range(4):
                                w = vblk[:, s, b, 2 * j + par] if kind == 0 else ones32[:, par]
                                at = kind * P + b * SEQ
                                mm = pe.matmul(ps[32 * j:32 * j + 32, bank, at:at + SEQ], w,
                                               probT[:, s, 2 * j + par, q], start=(par == 0), stop=(par == 1))
                mm.then_inc(S["pv_done"], 1)

            def out_proj(t, s):
                pe.wait_ge(S["oT_ready"], t + 1)
                if after(t, 1):
                    pe.wait_ge(S["x1_ready"], t)
                pe.matmul(ps[:, 7, 0:P], oT[:, s], woT, start=True, stop=True).then_inc(S["wo_done"], 1)

            def attend(t, s, _):
                scores(t, s)
                turn(t - 1, 1 - s)
                values(t - 2, s)
                if inside(t - 3, NT):
                    out_proj(t - 3, 1 - s)

            for name, n in (("xT_hi_ready", NPAIR + 1), ("xT_lo_ready", NPAIR + 1), ("k0_kept", NPAIR + 1),
                            ("k1_kept", NPAIR + 1), ("q_kept", NPAIR + 1)):
                pe.wait_ge(S[name], n)
            scores(0, 0)
            for name in ("v0_kept", "v1_kept"):
                pe.wait_ge(S[name], NT + 4)
            scores(1, 1)
            scores(2, 0)
            pe.wait_ge(S["diff_ready"], 4)
            turn(0, 0)
            turn(1, 1)
            values(0, 0)
            steps(pe, 3, 4, NT, NT, attend, 4)

            def route_turn(g, s, bank=7):
                pe.wait_ge(S["gxn_ready"], g + 1)
                if after(g, 1):
                    pe.wait_ge(S["gl_diff"], 2 * g)
                for i in range(2):
                    mm = pe.transpose(ps[:, bank, i * P:(i + 1) * P], xn[:, s, i, :], ident)
                mm.then_inc(S["gxT_done"], 1)

            def route_logits(g, s, bank=7):
                pe.wait_ge(S["gxT_hi"], g + 1)
                pe.wait_ge(S["gxT_lo"], g + 1)
                split3(pe, ps[0:NGATE, bank, PW:2 * PW], W_GATE, xT_hi[:, s], xT_lo[:, s], NGATE).then_inc(S["glT_done"], 1)

            def route_back(g, bank=7):
                hold(pe, "glT_kept", g + 1)
                for i in range(2):
                    mm = pe.transpose(ps[:, bank, i * 16:i * 16 + NGATE], lgT[0:NGATE, i * P:(i + 1) * P],
                                      const[0:NGATE, C_ID:C_ID + NGATE])
                mm.then_inc(S["gl_done"], 1)

            def unit(t, s, i, u):
                n = t * UNITS + u
                if after(t, 1) or u >= 4:
                    pe.wait_ge(S["hid_ready"], n - 3)
                for k, (a, b) in enumerate(((xT_hi, gu_hi), (xT_hi, gu_lo), (xT_lo, gu_hi))):
                    mm = pe.matmul(ps[:, bank_of(i, u), 0:UW], a[:, s, i * P:(i + 1) * P], b[:, u * UW:(u + 1) * UW],
                                   start=(k == 0), stop=(k == 2))
                mm.then_inc(S["unit_done"], 1)

            def hid_turn(t, i, q, bank=None):
                if q == 0:
                    pe.wait_ge(S["hid_ready"], (t + 1) * UNITS)
                m = t * 4 + q
                if bank is None:
                    bank = 4 + q % 2
                    if after(t, 1) or q >= 2:
                        pe.wait_ge(S["hT_lo_ready"], m - 1)
                for c in range(4 * q, min(4 * q + 4, HC)):
                    mm = pe.transpose(ps[:, bank, (c % 4) * P:(c % 4 + 1) * P], hid[:, i, c * P:(c + 1) * P], ident)
                mm.then_inc(S["hT_done"], 1)

            def down(g, chunks, bank=6):
                pe.wait_ge(S["hT_lo_ready"], (g + 1) * 8)
                pe.wait_ge(S["hT_hi_ready"], (g + 1) * 8)
                if after(g, 1):
                    pe.wait_ge(S["yT_kept"], g)
                for c in chunks:
                    cols = slice(c * P, (c + 1) * P)
                    o = ps[:, bank, 0:PW]
                    pe.matmul(o, down_hi[:, cols], hT_hi[:, c], start=(c == 0), stop=False)
                    pe.matmul(o, down_lo[:, cols], hT_hi[:, c], start=False, stop=False)
                    mm = pe.matmul(o, down_hi[:, cols], hT_lo[:, c], start=False, stop=(c == HC - 1))
                if c == HC - 1:
                    mm.then_inc(S["down_done"], 1)

            def down_back(g, bank=7):
                pe.wait_ge(S["yT_kept"], g + 1)
                for i in range(2):
                    mm = pe.transpose(ps[:, bank, PW + i * P:PW + (i + 1) * P], yT[:, i * P:(i + 1) * P], ident)
                mm.then_inc(S["y_done"], 1)

            def moe(g, s, _):
                last = not inside(g + 1, NPAIR)
                for u in range(UNITS):
                    if u == 2 and not after(g, 1):
                        out_proj(NT - 1, 1)
                        pe.wait_ge(S["gl_diff"], 2)
                    unit(g * 2, s, 0, u)
                    if u % 2 == 1 and u < 9 and after(g, 1):
                        hid_turn(g * 2 - 1, 1, u // 2)
                    if u == 3 and not after(g, 1):
                        pe.wait_ge(S["x1_ready"], NT)
                        route_turn(g + 1, 1 - s)
                    if u == 1 and not last and after(g, 1):
                        route_turn(g + 1, 1 - s)
                    if u == 5 and not last:
                        route_logits(g + 1, 1 - s)
                if after(g, 1):
                    down(g - 1, range(3))
                if not last:
                    route_back(g + 1)
                if after(g, 1):
                    down(g - 1, range(3, 9))
                if after(g, 2):
                    if not last:
                        pe.wait_ge(S["gl_diff"], 2 * g + 4)
                    down_back(g - 2)
                if after(g, 1):
                    down(g - 1, range(9, HC))
                for u in range(UNITS):
                    unit(g * 2 + 1, s, 1, u)
                    if u % 2 == 1 and u < 9:
                        hid_turn(g * 2, 0, u // 2)
                    if u == 2 and last:
                        pe.wait_ge(S["x2_ready"], 2 * (g - 1))
                        down_back(g - 1)

            pe.wait_ge(S["w_hi_ready"], 2)
            pe.wait_ge(S["w_lo_ready"], 2)
            pe.wait_ge(S["diff_ready"], 2 * NT)
            route_turn(0, 0, 3)
            turn(NT - 1, 1)
            values(NT - 2, 0)
            route_logits(0, 0, 3)
            values(NT - 1, 1)
            route_back(0, 3)
            out_proj(NT - 3, 1)
            out_proj(NT - 2, 0)
            pe.wait_ge(S["w_low"], 2 * NT)
            steps(pe, 0, 2, NPAIR - 2, NPAIR, moe)

            def q1_turn(g, s):
                pe.wait_ge(S["axn_ready"], g + 1)
                if after(g, 1):
                    pe.wait_ge(S["axT_lo"], g)
                for i in range(2):
                    mm = pe.transpose(ps[:, 0, i * P:(i + 1) * P], xn[:, s, i, :], ident)
                mm.then_inc(S["axT_done"], 1)

            def q1_proj(g, s):
                pe.wait_ge(S["axT_hi"], g + 1)
                pe.wait_ge(S["axT_lo"], g + 1)
                if after(g, 1):
                    pe.wait_ge(S["aq_kept"], g)
                split3(pe, ps[:, 7, 0:PW], W_Q1, xT_hi[:, s], xT_lo[:, s]).then_inc(S["aq_done"], 1)

            def scores1(g, s):
                pe.wait_ge(S["aq_kept"], g + 1)
                pe.wait_ge(S["ak_staged"], g + 1)
                if after(g, 2):
                    pe.wait_ge(S["adiff"], g - 1)
                for i in range(2):
                    for b in range(2):
                        tok = slice(i * P + b * SEQ, i * P + (b + 1) * SEQ)
                        mm = pe.matmul(ps[b * SEQ:(b + 1) * SEQ, 2 + s, i * SEQ:(i + 1) * SEQ],
                                       q1T[:, s, tok], k1s[:, s, tok], start=True, stop=True)
                mm.then_inc(S["as_done"], 1)

            def p1_turn(g, s):
                pe.wait_ge(S["aexp_done"], g + 1)
                if after(g, 1):
                    pe.wait_ge(S["apT_kept"], g)
                for i in range(2):
                    mm = pe.transpose(ps[:, 4, i * P:(i + 1) * P], pblk[:, s, i], ident)
                mm.then_inc(S["apT_done"], 1)

            def values1(g, s):
                pe.wait_ge(S["apT_kept"], g + 1)
                if after(g, 2):
                    pe.wait_ge(S["x3_ready"], 2 * (g - 1))
                for i in range(2):
                    mm = pe.matmul(ps[:, 5 + s, i * P:(i + 1) * P], p1T[:, s, i], v1[:, g * 2 + i], start=True, stop=True)
                mm.then_inc(S["ao_done"], 1)

            def keep_warm(n, bank):
                for _ in range(n):
                    pe.matmul(ps[:, bank, 0:PW], w_hi[:, 0:P], w_hi[:, 0:PW], start=True, stop=True)

            def attend1(g, s, _):
                if inside(g + 1, NPAIR):
                    scores1(g + 1, 1 - s)
                if inside(g + 2, NPAIR):
                    q1_turn(g + 2, s)
                if inside(g, NPAIR):
                    p1_turn(g, s)
                if not after(g, 1):
                    down(NPAIR - 1, part_of_down(3), 1)
                elif not after(g, 2):
                    down_back(NPAIR - 1, 1)
                else:
                    keep_warm(4, 1)
                if inside(g + 2, NPAIR):
                    q1_proj(g + 2, s)
                if inside(g, NPAIR):
                    values1(g, s)
                if not after(g, 1):
                    down(NPAIR - 1, part_of_down(4), 1)
                elif after(g, 2):
                    keep_warm(4, 1)

            keep_warm(13, 6)
            hid_turn(NT - 1, 1, 0)
            hid_turn(NT - 1, 1, 1)
            hid_turn(NT - 1, 1, 2, bank=2)
            hid_turn(NT - 1, 1, 3, bank=3)
            q1_turn(0, 0)
            keep_warm(12, 6)
            down(NPAIR - 1, part_of_down(0), 1)
            pe.wait_ge(S["x2_ready"], NT - 2)
            q1_proj(0, 0)
            down(NPAIR - 1, part_of_down(1), 1)
            scores1(0, 0)
            q1_turn(1, 1)
            down(NPAIR - 1, part_of_down(2), 1)
            q1_proj(1, 1)
            attend1(0, 0, 0)
            attend1(1, 1, 0)
            pe.wait_ge(S["x2_ready"], NT)
            steps(pe, 2, 2, NPAIR - 2, NPAIR - 2, attend1)

            def ff_turn(g, s):
                pe.wait_ge(S["fxn_ready"], g + 1)
                if after(g, 1):
                    pe.wait_ge(S["fxT_hi"], g)
                    pe.wait_ge(S["fxT_lo"], g)
                for i in range(2):
                    mm = pe.transpose(ps[:, 7, i * P:(i + 1) * P], xn[:, s, i, :], ident)
                mm.then_inc(S["fxT_done"], 1)

            def ff_up(g, s):
                pe.wait_ge(S["fxT_hi"], g + 1)
                pe.wait_ge(S["fxT_lo"], g + 1)
                if after(g, 2):
                    pe.wait_ge(S["n_ready"], 4 * (g - 1))
                for c in range(FC):
                    split3(pe, ps[:, 2 * s + c // 2, (c % 2) * PW:(c % 2 + 1) * PW], W_UP + c * P,
                           xT_hi[:, s], xT_lo[:, s]).then_inc(S["up_done"], 1)

            def ff_down(g, s):
                pe.wait_ge(S["yq_hi_ready"], g + 1)
                pe.wait_ge(S["yq_lo_ready"], g + 1)
                if not after(g, 2):
                    pe.wait_ge(S["x3_ready"], NT)
                pe.wait_ge(S["oq_int"], g + 1)
                pe.wait_ge(S["x4_ready"], 2 * g + 2)
                for c in range(FC):
                    if c == FC // 2 and is_last_pair(g):
                        pe.wait_ge(S["yq_hi_ready"], g + 2)
                        pe.wait_ge(S["yq_lo_ready"], g + 2)
                    w = W_DOWN + c * P
                    o = ps[:, 5 + s, 0:PW]
                    pe.matmul(o, w_hi[:, w:w + P], yq_hi[:, s, c], start=(c == 0), stop=False)
                    pe.matmul(o, w_lo[:, w:w + P], yq_hi[:, s, c], start=False, stop=False)
                    mm = pe.matmul(o, w_hi[:, w:w + P], yq_lo[:, s, c], start=False, stop=(c == FC - 1))
                mm.then_inc(S["fd_done"], 1)

            def ff_back(g, s):
                pe.wait_ge(S["oq_ready"], g + 1)
                for i in range(2):
                    mm = pe.transpose(ps[:, 5 + s, PW + i * P:PW + (i + 1) * P], oq[:, s, i * P:(i + 1) * P], ident)
                mm.then_inc(S["fo_done"], 1)

            def feed(g, s, _):
                if inside(g + 2, NPAIR):
                    ff_turn(g + 2, s)
                    ff_up(g + 2, s)
                if is_last_pair(g - 1):
                    ff_down(g - 1, 1 - s)
                if inside(g - 2, NPAIR):
                    ff_back(g - 2, s)
                if inside(g, NPAIR):
                    keep_warm(8 if inside(g + 2, NPAIR) else 14, 4)
                if inside(g - 1, NPAIR) and not is_last_pair(g - 1):
                    ff_down(g - 1, 1 - s)

            pe.sem_inc(S["fo_done"], 2)
            pe.wait_ge(S["axT_lo"], NPAIR)
            pe.wait_ge(S["aq_kept"], NPAIR)
            ff_turn(0, 0)
            scores1(NPAIR - 1, 1)
            p1_turn(NPAIR - 2, 0)
            ff_up(0, 0)
            values1(NPAIR - 2, 0)
            p1_turn(NPAIR - 1, 1)
            ff_turn(1, 1)
            pe.wait_ge(S["adiff"], NPAIR)
            ff_up(1, 1)
            values1(NPAIR - 1, 1)
            steps(pe, 0, 2, NPAIR - 2, NPAIR + 2, feed)

        @block.scalar
        def _(act):
            act.sem_inc(S["xT_hi_ready"], 1)
            act.sem_inc(S["k0_kept"], 1)
            act.sem_inc(S["k1_kept"], 1)
            act.sem_inc(S["v0_kept"], 4)
            act.sem_inc(S["q_kept"], 1)
            act.sem_inc(S["oq_int"], 2)
            act.wait_ge(S["w_in"], 16)
            act.copy(w_hi[:, 0:W_EARLY], wraw[:, 0:W_EARLY]).then_inc(S["w_hi_ready"], 1)

            def context_high(g, s, half):
                act.wait_ge(S[f"ctx_in{s}"], 16 * (half + 1))
                if after(g, 2):
                    act.wait_ge(S["v_done"], 2 * (g - 1))
                src = ctxT[:, s].rearrange("p (b n) -> p b n", b=4).unsqueeze(2).broadcast_to([P, 4, 2, SEQ])
                act.copy(ctx_hi[:, s], src).then_inc(S["ctx_hi_ready"], 1)

            def keep_projections(g, s, half):
                if inside(g + 1, NPAIR):
                    context_high(g + 1, 1 - s, half + s)
                act.wait_ge(S["xT_done"], g + 1)
                act.copy(xT_hi[:, s], ps[:, 0, 0:PW]).then_inc(S["xT_hi_ready"], 1)
                act.wait_ge(S["k0_done"], g + 1)
                act.copy(k0T[:, pair(g)], ps[:, 2, 0:PW]).then_inc(S["k0_kept"], 1)
                act.wait_ge(S["k1_done"], g + 1)
                act.activation(k1T[:, pair(g)], ps[:, 3, 0:PW], ACT.Identity,
                               bias=const[:, C_BK:C_BK + 1]).then_inc(S["k1_kept"], 1)
                for i in range(2):
                    act.wait_ge(S["v_done"], 2 * g + i + 1)
                    src = ps[:, 4 + 2 * s + i, :].rearrange("p (b n) -> p b n", b=2)[:, :, 0:P]
                    act.copy(v0dup[:, bass.ds(g * 4 + 2 * i, 2), :], src).then_inc(S["v0_kept"], 1)
                act.wait_ge(S["q_done"], g + 1)
                act.copy(q0T[:, pair(g)], ps[:, 1, 0:PW]).then_inc(S["q_kept"], 1)

            context_high(0, 0, 0)
            act.wait_ge(S["const_in"], 16)
            keep_projections(0, 0, 0)
            act.wait_ge(S["w_rest_in"], 16)
            act.copy(w_hi[:, W_EARLY:W_COLS], wraw[:, W_EARLY:W_COLS]).then_inc(S["w_hi_ready"], 1)
            steps(act, 1, 2, NPAIR - 2, NPAIR, keep_projections)

            def keep_turned(t, s):
                for half in range(2):
                    act.wait_ge(S["probT_done"], 2 * t + half + 1)
                    if half == 0 and after(t, 2):
                        act.wait_ge(S["pv_done"], t - 1)
                    act.copy(probT[:, s, 4 * half:4 * half + 4].rearrange("p c n -> p (c n)"),
                             ps[:, 4 + half, :]).then_inc(S["probT_kept"], 1)

            def exps(t, s):
                act.wait_ge(S["diff_ready"], 2 * t + 2)
                act.activation(prob[:, s], prob[:, s], ACT.Exp, scale=SCALE0).then_inc(S["exp_done"], 1)

            def split_high(t):
                n, m = UNITS * UW // NT, HC * P // NT
                act.copy(gu_hi[:, bass.ds(t * n, n)], gu_raw[:, bass.ds(t * n, n)])
                act.copy(down_hi[:, bass.ds(t * m, m)], down_raw[:, bass.ds(t * m, m)]).then_inc(S["w_high"], 1)

            def stage_q(t, s):
                if after(t, 2):
                    act.wait_ge(S["scores_done"], 2 * (t - 1))
                act.copy(q_st[:, s], q0T[:, bass.ds(t * P, P)]).then_inc(S["q_staged"], 1)

            act.wait_ge(S["q_kept"], NPAIR + 1)
            stage_q(0, 0)
            stage_q(1, 1)
            act.wait_ge(S["gu_in"], 16)
            act.wait_ge(S["down_in"], 16)
            def attend(t, s, _):
                if not after(t, 3) and after(t, 2):
                    keep_turned(0, 0)
                if inside(t - 1, NT) and after(t, 2):
                    keep_turned(t - 1, 1 - s)
                if inside(t + 2, NT):
                    stage_q(t + 2, s)
                if inside(t, NT):
                    exps(t, s)
                if inside(t, NT):
                    split_high(t)

            steps(act, 0, 4, NT - 4, NT, attend, 4)

            def route_high(g, s, bank=7):
                act.wait_ge(S["gxT_done"], g + 1)
                act.copy(xT_hi[:, s], ps[:, bank, 0:PW]).then_inc(S["gxT_hi"], 1)

            def route_keep(g, bank=7):
                act.wait_ge(S["glT_done"], g + 1)
                act.copy(lgT[0:NGATE, :], ps[0:NGATE, bank, PW:2 * PW]).then_inc(S["glT_kept"], 1)

            def route_exp(g):
                act.wait_ge(S["gl_diff"], 2 * g + 2)
                act.activation(ge[:, :, 0:10], gd[:, :, 0:10], ACT.Exp).then_inc(S["gexp_done"], 1)
                act.activation(gl[:, :, 6], gd[:, :, 0], ACT.Silu)

            def silus(t, i, u):
                n = t * UNITS + u
                act.wait_ge(S["unit_done"], n + 1)
                if after(t, 1) or u >= 4:
                    act.wait_ge(S["hid_ready"], n - 3)
                b = bank_of(i, u)
                act.activation(silu[:, b], ps[:, b, 0:INTER], ACT.Silu).then_inc(S["silu_done"], 1)

            def keep_high(t, i, q, bank=None):
                act.wait_ge(S["hT_done"], t * 4 + q + 1)
                b = 4 + q % 2 if bank is None else bank
                n = min(4, HC - 4 * q)
                act.copy(hT_hi[:, 4 * q:4 * q + n, i * P:(i + 1) * P],
                         ps[:, b, 0:n * P].rearrange("p (c n) -> p c n", c=n)).then_inc(S["hT_hi_ready"], 1)

            def keep_y(g, bank=6):
                act.wait_ge(S["down_done"], g + 1)
                act.copy(yT, ps[:, bank, 0:PW]).then_inc(S["yT_kept"], 1)

            def moe(g, s, _):
                last = not inside(g + 1, NPAIR)
                for u in range(UNITS):
                    silus(g * 2, 0, u)
                    if u % 2 == 1 and u < 9 and after(g, 1):
                        keep_high(g * 2 - 1, 1, u // 2)
                    if u == (2 if after(g, 1) else 4) and not last:
                        route_high(g + 1, 1 - s)
                    if u == 8 and not last:
                        route_keep(g + 1)
                if not last:
                    route_exp(g + 1)
                for u in range(UNITS):
                    silus(g * 2 + 1, 1, u)
                    if u == 0 and after(g, 1):
                        keep_y(g - 1)
                    if u % 2 == 1 and u < 9:
                        keep_high(g * 2, 0, u // 2)

            route_high(0, 0, 3)
            attend(NT, 0, NT // 2)
            act.wait_ge(S["vblk_staged"], 2 * NT)
            route_keep(0, 3)
            route_exp(0)
            steps(act, 0, 2, NPAIR - 2, NPAIR, moe)

            def q1_high(g, s):
                act.wait_ge(S["axT_done"], g + 1)
                act.copy(xT_hi[:, s], ps[:, 0, 0:PW]).then_inc(S["axT_hi"], 1)

            def q1_keep(g, s):
                act.wait_ge(S["aq_done"], g + 1)
                act.activation(q1T[:, s], ps[:, 7, 0:PW], ACT.Identity,
                               bias=const[:, C_BQ:C_BQ + 1]).then_inc(S["aq_kept"], 1)

            def exps1(g, s):
                act.wait_ge(S["adiff"], g + 1)
                act.wait_ge(S["pblk_zero"], 1)
                for b in range(2):
                    rows = slice(b * SEQ, (b + 1) * SEQ)
                    e = act.activation(pblk[rows, s, :, b * SEQ:(b + 1) * SEQ], pdiff[rows, s], ACT.Exp)
                e.then_inc(S["aexp_done"], 1)

            def keep_p1T(g, s):
                act.wait_ge(S["apT_done"], g + 1)
                act.copy(p1T[:, s].rearrange("p t k -> p (t k)"), ps[:, 4, 0:PW]).then_inc(S["apT_kept"], 1)

            def attend1(g, s, _):
                if inside(g + 2, NPAIR):
                    q1_high(g + 2, s)
                if inside(g, NPAIR):
                    keep_p1T(g, s)
                if inside(g + 1, NPAIR):
                    exps1(g + 1, 1 - s)
                if inside(g + 2, NPAIR):
                    q1_keep(g + 2, s)

            keep_high(NT - 1, 1, 0)
            keep_high(NT - 1, 1, 1)
            keep_high(NT - 1, 1, 2, bank=2)
            keep_high(NT - 1, 1, 3, bank=3)
            q1_high(0, 0)
            q1_keep(0, 0)
            q1_high(1, 1)
            exps1(0, 0)
            q1_keep(1, 1)
            attend1(0, 0, 0)
            keep_y(NPAIR - 1, 1)
            attend1(1, 1, 0)
            steps(act, 2, 2, NPAIR - 2, NPAIR - 2, attend1)

            act.wait_ge(S["b_scaled"], 1)

            def ff_high(g, s):
                act.wait_ge(S["fxT_done"], g + 1)
                act.copy(xT_hi[:, s], ps[:, 7, 0:PW]).then_inc(S["fxT_hi"], 1)

            def ff_n(g, s):
                for c in range(FC):
                    if c % 2 == 0:
                        act.wait_ge(S["up_done"], g * 4 + c + 2)
                    if c == 0 and after(g, 2):
                        act.wait_ge(S["frac_ready"], g - 1)
                    act.activation(n_i[:, s, c * PW:(c + 1) * PW], ps[:, 2 * s + c // 2, (c % 2) * PW:(c % 2 + 1) * PW],
                                   ACT.Identity, bias=b_q[:, c:c + 1], scale=QUANT).then_inc(S["n_ready"], 1)

            def ff_gelu(g, s):
                act.wait_ge(S["base_ready"], g + 1)
                if after(g, 2):
                    act.wait_ge(S["y_ready"], g - 1)
                act.activation(g_lo[:, s], base_i[:, s], ACT.Gelu, scale=1 / QUANT).then_inc(S["glo_done"], 1)
                act.activation(g_hi[:, s], base_i[:, s], ACT.Gelu, scale=1 / QUANT,
                               bias=quarter[:]).then_inc(S["ghi_done"], 1)

            def ff_yhigh(g, s, half=0, n=FC * PW):
                act.wait_ge(S["y_ready"], g + 1 + half)
                if after(g, 2):
                    act.wait_ge(S["fd_done"], g - 1)
                cols = slice(s * FC * PW + half * n, s * FC * PW + half * n + n)
                act.copy(yq_hi_[:, cols], y_i[:, s, half * n:half * n + n]).then_inc(S["yq_hi_ready"], 1)

            def ff_out(g, s):
                act.wait_ge(S["fd_done"], g + 1)
                act.wait_ge(S["fo_done"], g + 1)
                act.activation(oq_i[:, s], ps[:, 5 + s, 0:PW], ACT.Identity,
                               bias=b_q[:, FC:FC + 1]).then_inc(S["oq_int"], 1)
                act.wait_ge(S["oq_int"], g + 3)
                act.activation(oq[:, s], oq_i[:, s], ACT.Copy, scale=1 / QUANT).then_inc(S["oq_ready"], 1)

            def feed(g, s, _):
                if inside(g + 2, NPAIR):
                    ff_high(g + 2, s)
                if inside(g - 2, NPAIR):
                    ff_out(g - 2, s)
                if inside(g + 1, NPAIR):
                    ff_gelu(g + 1, 1 - s)
                if inside(g + 2, NPAIR):
                    ff_n(g + 2, s)
                if is_last_pair(g):
                    for half in range(2):
                        ff_yhigh(g, s, half, FC * PW // 2)
                elif inside(g, NPAIR):
                    ff_yhigh(g, s)

            ff_high(0, 0)
            keep_p1T(NPAIR - 2, 0)
            exps1(NPAIR - 1, 1)
            ff_n(0, 0)
            keep_p1T(NPAIR - 1, 1)
            ff_high(1, 1)
            ff_gelu(0, 0)
            ff_n(1, 1)
            steps(act, 0, 2, NPAIR - 2, NPAIR + 2, feed)

        @block.vector
        def _(dve):
            dve.sem_inc(S["xT_lo_ready"], 1)
            dve.sem_inc(S["v1_kept"], 4)
            dve.memset(oT_, 0.0).then_inc(S["zeros_set"], 1)
            dve.memset(quarter[:], 0.25)
            dve.memset(minus_half[:], -0.5).then_inc(S["consts_set"], 1)
            dve.sem_inc(S["x4_ready"], 4)

            def split_weights_low(cols, n):
                dve.wait_ge(S["w_hi_ready"], n)
                dve.tensor_tensor(w_lo[:, cols], wraw[:, cols], w_hi[:, cols].bitcast(F32),
                                  ALU.subtract).then_inc(S["w_lo_ready"], 1)

            def pair_stats(g, norm):
                for i in range(2):
                    dve.bn_stats(moments[:, i], x[:, g * 2 + i, :]).then_inc(S[f"moments{norm}"], 1)
                hold(dve, f"rstd{norm}", g + 1)
                hold(dve, f"moments{norm}", 2 * g + 2)
                for i in range(2):
                    dve.bn_aggr(meanvar[:, i], moments[:, i]).then_inc(S[f"stats{norm}"], 1)

            def normalise(g, s, ready, rstd_name):
                dve.wait_ge(S[rstd_name], g + 2)
                for i in range(2):
                    t = g * 2 + i
                    n = dve.tensor_scalar(xn[:, s, i], x[:, t, :], mean[:, one(t)], rstd[:, one(t)],
                                          ALU.subtract, ALU.mult)
                n.then_inc(S[ready], 1)

            def low_part(out, src, high, done):
                return dve.tensor_tensor(out, src, high.bitcast(F32), ALU.subtract).then_inc(S[done], 1)

            def keep_projections(g, s, _):
                if inside(g, NPAIR):
                    dve.wait_ge(S["xT_hi_ready"], g + 2)
                    if after(g, 2):
                        dve.wait_ge(S["q_done"], g - 1)
                    low_part(xT_lo[:, s], ps[:, 0, 0:PW], xT_hi[:, s], "xT_lo_ready")
                if inside(g + 1, NPAIR):
                    if after(g + 1, 2):
                        dve.wait_ge(S["xT_done"], g)
                    normalise(g + 1, 1 - s, "xn_ready", "rstd0")
                if inside(g + 2, NPAIR):
                    pair_stats(g + 2, 0)
                if inside(g, NPAIR):
                    keep_values(g, s)

            def keep_values(g, s):
                for i in range(2):
                    dve.wait_ge(S["v0_kept"], 2 * g + i + 5)
                    for b in range(2):
                        rows = slice(b * SEQ, (b + 1) * SEQ)
                        o = dve.tensor_tensor(v1[rows, g * 2 + i, :],
                                              ps[rows, 4 + 2 * s + i, b * PW + P:(b + 1) * PW],
                                              bv_rows[rows], ALU.add)
                    o.then_inc(S["v1_kept"], 1)

            dve.wait_ge(S["x_in"], 16)
            keep_projections(-2, 0, -1)
            split_weights_low(slice(0, W_EARLY), 1)
            dve.wait_ge(S["const_in"], 16)
            dve.tensor_scalar(b_q[:], const[:, C_B1:C_B1 + FC + 1], QUANT, None, ALU.mult).then_inc(S["b_scaled"], 1)
            keep_projections(-1, 1, -1)
            dve.wait_ge(S["x_rest_in"], 16)
            keep_projections(0, 0, 0)
            split_weights_low(slice(W_EARLY, W_COLS), 2)
            steps(dve, 1, 2, NPAIR - 2, NPAIR, keep_projections)

            def maxima(t, s, half):
                dve.wait_ge(S["scores_done"], 2 * t + half + 1)
                b = scores_bank(t) + 2 * half
                sc = ps[:, b:b + 2, 0:256].rearrange("p a (j k) -> p a j k", k=SEQ)
                dve.tensor_reduce(rowmax[:, s, 2 * half:2 * half + 2], sc, AX_X, ALU.max).then_inc(S["rowmax_ready"], 1)

            def diffs(t, s, half):
                dve.wait_ge(S["rowmax_ready"], 2 * t + half + 1)
                if after(t, 2) and half == 0:
                    dve.wait_ge(S["probT_done"], 2 * t - 2)
                b = scores_bank(t) + 2 * half
                sc = ps[:, b:b + 2, 0:256].rearrange("p a (j k) -> p a j k", k=SEQ)
                m = rowmax[:, s, 2 * half:2 * half + 2].unsqueeze(3).broadcast_to([P, 2, 4, SEQ])
                d = prob[:, s, half * 512:(half + 1) * 512].rearrange("p (a j k) -> p a j k", a=2, j=4)
                dve.tensor_tensor(d, sc, m, ALU.subtract).then_inc(S["diff_ready"], 1)

            def add_x(t):
                dve.wait_ge(S["wo_done"], t + 1)
                dve.tensor_tensor(x[:, t, :], ps[:, 7, 0:P], x[:, t, :], ALU.add).then_inc(S["x1_ready"], 1)

            def x_moments(t, i):
                hold(dve, "x1_ready", t + 1)
                dve.bn_stats(moments[:, i], x[:, t, :]).then_inc(S["moments1"], 1)

            def sums_inverted(t):
                dve.wait_ge(S["pv_done"], t + 1)
                dve.reciprocal(rden, ps[:, values_bank(t), P:2 * P]).then_inc(S["rden_ready"], 1)

            def x_meanvar(t, g, i):
                hold(dve, "rstd1", g + 1)
                hold(dve, "moments1", t + 1)
                dve.bn_aggr(meanvar[:, i], moments[:, i]).then_inc(S["stats1"], 1)

            def heads_out(t, s):
                dve.wait_ge(S["rden_ready"], t + 1)
                if after(t, 2):
                    dve.wait_ge(S["wo_done"], t - 1)
                dve.scalar_tensor_tensor(out=oT[:, s], in0=ps[:, values_bank(t), 0:P], scalar=float(REPEAT0),
                                         in1=rden, op0=ALU.mult, op1=ALU.mult).then_inc(S["oT_ready"], 1)

            def attend(t, s, half):
                maxima(t, s, 0)
                maxima(t, s, 1)
                diffs(t, s, 0)
                diffs(t, s, 1)
                if inside(t - 4, NT):
                    add_x(t - 4)
                if inside(t - 2, NT):
                    sums_inverted(t - 2)
                if inside(t - 4, NT):
                    x_moments(t - 4, s)
                if inside(t - 2, NT):
                    heads_out(t - 2, s)
                if inside(t - 4, NT):
                    x_meanvar(t - 4, half - 2, s)

            steps(dve, 0, 4, NT, NT, attend, 4)

            own = Steps(dve, S["route_steps"])

            def route_low(g, s, bank=7):
                dve.wait_ge(S["gxT_hi"], g + 1)
                low_part(xT_lo[:, s], ps[:, bank, 0:PW], xT_hi[:, s], "gxT_lo")

            def route_diff(g, bank=7):
                own.n = g * ROUTE_STEPS
                dve.wait_ge(S["gl_done"], g + 1)
                lg = ps[:, bank, 0:32].rearrange("p (t n) -> p t n", t=2)
                own.did(dve.tensor_reduce(gl[:, :, 0], lg[:, :, 0:NEXP], AX_X, ALU.max))
                dve.tensor_scalar(gd[:, :, 8:10], lg[:, :, 8:10], -1.0, None, ALU.mult).then_inc(S["gl_diff"], 1)
                own.wait()
                dve.tensor_tensor(gd[:, :, 0:NEXP], lg[:, :, 0:NEXP],
                                  gl[:, :, 0:1].broadcast_to([P, 2, NEXP]), ALU.subtract).then_inc(S["gl_diff"], 1)

            def route_weights(g, s):
                own.n = g * ROUTE_STEPS + 1
                dve.wait_ge(S["gexp_done"], g + 1)
                own.did(dve.tensor_reduce(gl[:, :, 1], ge[:, :, 0:NEXP], AX_X, ALU.add))
                own.did(dve.tensor_scalar(gl[:, :, 2:3], ge[:, :, 8:9], 1.0, None, ALU.add))
                own.wait()
                own.did(dve.reciprocal(gl[:, :, 4:6], gl[:, :, 1:3]))
                own.wait()
                own.did(dve.tensor_tensor(gp[:], ge[:, :, 0:NEXP], gl[:, :, 4:5].broadcast_to([P, 2, NEXP]), ALU.mult))
                own.wait()
                for i in range(2):
                    mine = gp[:, i].unsqueeze(2).broadcast_to([P, NEXP, NEXP])
                    other = gp[:, i].unsqueeze(1).broadcast_to([P, NEXP, NEXP])
                    own.did(dve.tensor_tensor(beats[:, i], other, mine, ALU.is_gt))
                    own.did(dve.tensor_tensor(ties[:, i], other, mine, ALU.is_equal))
                own.wait()
                own.did(dve.tensor_tensor(ties[:], ties[:], tri.unsqueeze(1).broadcast_to([P, 2, 8, 8]), ALU.mult))
                own.wait()
                own.did(dve.tensor_tensor(beats[:], beats[:], ties[:], ALU.add))
                own.wait()
                own.did(dve.tensor_reduce(rank[:], beats[:], AX_X, ALU.add))
                own.wait()
                own.did(dve.scalar_tensor_tensor(out=wexp[:, s, :, 0:NEXP], in0=rank[:], scalar=float(TOPK) - 0.5,
                                                 in1=gp[:], op0=ALU.is_lt, op1=ALU.mult))
                own.did(dve.tensor_copy(wexp[:, s, :, NEXP:UNITS], gl[:, :, 5:6].broadcast_to([P, 2, 2])))
                own.wait()

            def products(t, s, i, u):
                dve.wait_ge(S["silu_done"], t * UNITS + u + 1)
                if u == 0 and after(t, 2):
                    dve.wait_ge(S["hT_done"], (t - 1) * 4)
                dve.scalar_tensor_tensor(out=hid[:, i, u * INTER:(u + 1) * INTER], in0=silu[:, bank_of(i, u)],
                                         scalar=wexp[:, s, i, u:u + 1], in1=ps[:, bank_of(i, u), INTER:UW],
                                         op0=ALU.mult, op1=ALU.mult).then_inc(S["hid_ready"], 1)

            def keep_low(t, i, q, bank=None):
                dve.wait_ge(S["hT_hi_ready"], t * 4 + q + 1)
                b = 4 + q % 2 if bank is None else bank
                n = min(4, HC - 4 * q)
                dve.tensor_tensor(hT_lo[:, 4 * q:4 * q + n, i * P:(i + 1) * P],
                                  ps[:, b, 0:n * P].rearrange("p (c n) -> p c n", c=n),
                                  hT_hi[:, 4 * q:4 * q + n, i * P:(i + 1) * P].bitcast(F32),
                                  ALU.subtract).then_inc(S["hT_lo_ready"], 1)

            def add_y(g, bank=7):
                dve.wait_ge(S["y_done"], g + 1)
                for i in range(2):
                    t = g * 2 + i
                    dve.tensor_tensor(x[:, t, :], ps[:, bank, PW + i * P:PW + (i + 1) * P], x[:, t, :],
                                      ALU.add).then_inc(S["x2_ready"], 1)

            def moe(g, s, _):
                for u in range(UNITS):
                    products(g * 2, s, 0, u)
                    if u % 2 == 1 and u < 9 and after(g, 1):
                        keep_low(g * 2 - 1, 1, u // 2)
                    if u == (2 if after(g, 1) else 4) and inside(g + 1, NPAIR):
                        route_low(g + 1, 1 - s)
                    if u in (4, 6) and not after(g, 1):
                        i = u // 2 - 2
                        x_moments(NT - 2 + i, i)
                        x_meanvar(NT - 2 + i, NPAIR - 1, i)
                if inside(g + 1, NPAIR):
                    route_diff(g + 1)
                    route_weights(g + 1, 1 - s)
                if after(g, 2):
                    add_y(g - 2)
                    hold(dve, "x2_ready", 2 * (g - 1))
                    pair_stats(g - 2, 2)
                for u in range(UNITS):
                    products(g * 2 + 1, s, 1, u)
                    if u % 2 == 1 and u < 9:
                        keep_low(g * 2, 0, u // 2)
                    if u == 6 and not inside(g + 1, NPAIR):
                        add_y(g - 1)

            add_x(NT - 4)
            x_moments(NT - 4, 0)
            route_low(0, 0, 3)
            x_meanvar(NT - 4, NPAIR - 2, 0)
            sums_inverted(NT - 2)
            route_diff(0, 3)
            heads_out(NT - 2, 0)
            dve.wait_ge(S["oT_ready"], NT - 1)
            sums_inverted(NT - 1)
            heads_out(NT - 1, 1)
            add_x(NT - 3)
            x_moments(NT - 3, 1)
            add_x(NT - 2)
            x_meanvar(NT - 3, NPAIR - 2, 1)
            dve.wait_ge(S["k_staged"], NT)
            dve.wait_ge(S["q_staged"], NT)
            dve.wait_ge(S["vblk_staged"], 2 * NT)
            dve.memset(hid[:, :, UNITS * INTER:HPAD], 0.0).then_inc(S["hid_zero"], 1)
            dve.wait_ge(S["hid_zero"], 1)
            add_x(NT - 1)
            route_weights(0, 0)
            steps(dve, 0, 2, NPAIR - 2, NPAIR, moe)

            def q1_low(g, s):
                dve.wait_ge(S["axT_hi"], g + 1)
                if after(g, 2):
                    dve.wait_ge(S["aq_done"], g - 1)
                low_part(xT_lo[:, s], ps[:, 0, 0:PW], xT_hi[:, s], "axT_lo")

            def diffs1(g, s):
                dve.wait_ge(S["as_done"], g + 1)
                sc = ps[:, 2 + s, 0:2 * SEQ].rearrange("p (t k) -> p t k", t=2)
                dve.tensor_reduce(stat1[:, s, 0, :], sc, AX_X, ALU.max).then_inc(S["amax"], 1)
                dve.wait_ge(S["amax"], g + 1)
                dve.tensor_tensor(pdiff[:, s], sc, stat1[:, s, 0, :].unsqueeze(2).broadcast_to([P, 2, SEQ]),
                                  ALU.subtract).then_inc(S["adiff"], 1)

            def sums1(g, s):
                dve.wait_ge(S["aexp_done"], g + 1)
                dve.tensor_reduce(stat1[:, s, 1, :], pblk[:, s], AX_X, ALU.add).then_inc(S["astat"], 1)
                dve.wait_ge(S["astat"], 2 * g + 1)
                dve.reciprocal(stat1[:, s, 2, :], stat1[:, s, 1, :]).then_inc(S["astat"], 1)
                dve.wait_ge(S["astat"], 2 * g + 2)

            def add_v(g, s):
                dve.wait_ge(S["ao_done"], g + 1)
                for i in range(2):
                    t = g * 2 + i
                    dve.scalar_tensor_tensor(out=x[:, t, :], in0=ps[:, 5 + s, i * P:(i + 1) * P],
                                             scalar=stat1[:, s, 2, i:i + 1], in1=x[:, t, :],
                                             op0=ALU.mult, op1=ALU.add).then_inc(S["x3_ready"], 1)
                hold(dve, "x3_ready", 2 * g + 2)
                pair_stats(g, 3)

            dve.memset(pblk_, 0.0).then_inc(S["pblk_zero"], 1)
            def attend1(g, s, _):
                if inside(g + 1, NPAIR):
                    diffs1(g + 1, 1 - s)
                if inside(g, NPAIR):
                    sums1(g, s)
                if inside(g + 2, NPAIR):
                    q1_low(g + 2, s)
                if after(g, 1) and not after(g, 2):
                    add_y(NPAIR - 1, 1)
                    hold(dve, "x2_ready", NT)
                    pair_stats(NPAIR - 1, 2)
                if inside(g - 1, NPAIR):
                    add_v(g - 1, 1 - s)

            hold(dve, "x2_ready", NT - 2)
            pair_stats(NPAIR - 2, 2)
            keep_low(NT - 1, 1, 0)
            keep_low(NT - 1, 1, 1)
            keep_low(NT - 1, 1, 2, bank=2)
            keep_low(NT - 1, 1, 3, bank=3)
            q1_low(0, 0)
            diffs1(0, 0)
            q1_low(1, 1)
            attend1(0, 0, 0)
            steps(dve, 1, 2, NPAIR - 2, NPAIR - 2, attend1)

            def ff_low(g, s):
                dve.wait_ge(S["fxT_hi"], g + 1)
                low_part(xT_lo[:, s], ps[:, 7, 0:PW], xT_hi[:, s], "fxT_lo")

            def ff_knots(g, s):
                dve.wait_ge(S["n_ready"], 4 * g + 4)
                if after(g, 2):
                    dve.wait_ge(S["ghi_done"], g - 1)
                dve.tensor_scalar(base_i[:, s], n_i[:, s], -KNOT, None, ALU.bitwise_and).then_inc(S["base_ready"], 1)
                dve.tensor_scalar(frac_i[:, s], n_i[:, s], KNOT - 1, None, ALU.bitwise_and).then_inc(S["frac_ready"], 1)

            def ff_rise(g, s, half=0, n=FC * PW):
                dve.wait_ge(S["slope_ready"], g + 1)
                cols = slice(half * n, half * n + n)
                dve.scalar_tensor_tensor(out=g_hi[:, s, cols], in0=frac_i[:, s, cols], scalar=QUANT / KNOT,
                                         in1=g_hi[:, s, cols], op0=ALU.mult, op1=ALU.mult).then_inc(S["rise_ready"], 1)

            def ff_y(g, s, half=0, n=FC * PW):
                cols = slice(half * n, half * n + n)
                dve.wait_ge(S["rise_ready"], g + 1 + half)
                if after(g, 2):
                    dve.wait_ge(S["yq_lo_ready"], g - 1)
                dve.scalar_tensor_tensor(out=y_i[:, s, cols], in0=g_lo[:, s, cols], scalar=QUANT, in1=g_hi[:, s, cols],
                                         op0=ALU.mult, op1=ALU.add).then_inc(S["y_ready"], 1)

            def ff_ylow(g, s, half=0, n=FC * PW):
                dve.wait_ge(S["yq_hi_ready"], g + 1 + half)
                cols = slice(s * FC * PW + half * n, s * FC * PW + half * n + n)
                dve.tensor_tensor(yq_lo_[:, cols], y_i[:, s, half * n:half * n + n], yq_hi_[:, cols].bitcast(F32),
                                  ALU.subtract).then_inc(S["yq_lo_ready"], 1)

            def ff_add(g, s):
                dve.wait_ge(S["fo_done"], g + 3)
                for i in range(2):
                    t = g * 2 + i
                    dve.tensor_tensor(x[:, t, :], ps[:, 5 + s, PW + i * P:PW + (i + 1) * P], x[:, t, :],
                                      ALU.add).then_inc(S["x4_ready"], 1)

            def feed(g, s, _):
                if inside(g + 1, NPAIR):
                    ff_knots(g + 1, 1 - s)
                if inside(g + 2, NPAIR):
                    ff_low(g + 2, s)
                if is_last_pair(g - 1):
                    for half in range(2):
                        ff_ylow(g - 1, 1 - s, half, FC * PW // 2)
                elif inside(g - 1, NPAIR):
                    ff_ylow(g - 1, 1 - s)
                if is_last_pair(g):
                    for half in range(2):
                        ff_rise(g, s, half, FC * PW // 2)
                        ff_y(g, s, half, FC * PW // 2)
                elif inside(g, NPAIR):
                    ff_rise(g, s)
                if inside(g - 2, NPAIR):
                    ff_add(g - 2, s)
                if inside(g, NPAIR) and not is_last_pair(g):
                    ff_y(g, s)

            ff_low(0, 0)
            attend1(NPAIR - 2, 0, NPAIR // 2 - 1)
            ff_knots(0, 0)
            ff_low(1, 1)
            attend1(NPAIR - 1, 1, NPAIR // 2 - 1)
            feed(0, 0, 0)
            attend1(NPAIR, 0, NPAIR // 2)
            steps(dve, 1, 2, NPAIR - 2, NPAIR + 2, feed)

        @block.gpsimd
        def _(pool):
            pool.wait_ge(S["consts_set"], 1)
            pool.sem_inc(S["rstd0"], 1)

            def free_meanvar(norm):
                pool.wait_ge(S[f"rstd{norm - 1}"], NPAIR + 1)
                pool.sem_inc(S[f"rstd{norm}"], 1)

            def rstds(g, norm):
                hold(pool, f"stats{norm}", 2 * g + 2)
                cols = bass.ds(g * 2, 2)
                pool.tensor_copy(mean[:, cols], meanvar[:, :, 0]).then_inc(S[f"veps{norm}"], 1)
                pool.tensor_scalar(veps[:], meanvar[:, :, 1], EPS, 1.0, ALU.add, ALU.mult).then_inc(S[f"veps{norm}"], 1)
                hold(pool, f"veps{norm}", 2 * g + 2)
                pool.tensor_tensor(rstd[:, cols], veps[:], minus_half[:], ALU.pow).then_inc(S[f"rstd{norm}"], 1)

            def context_low(g, s):
                hold(pool, "ctx_hi_ready", g + 1)
                src = ctxT[:, s].rearrange("p (b n) -> p b n", b=4).unsqueeze(2).broadcast_to([P, 4, 2, SEQ])
                pool.tensor_tensor(ctx_lo[:, s], src, ctx_hi[:, s].bitcast(F32), ALU.subtract).then_inc(S["ctx_lo_ready"], 1)

            def centre_and_scale(g, s, norm, ready):
                hold(pool, f"rstd{norm}", g + 2)
                cols = bass.ds(g * 2, 2)
                shape = [P, 2, P]
                pool.tensor_tensor(xn[:, s], x[:, cols, :], mean[:, cols].unsqueeze(2).broadcast_to(shape),
                                   ALU.subtract).then_inc(S[f"centred{norm}"], 1)
                hold(pool, f"centred{norm}", g + 1)
                pool.tensor_tensor(xn[:, s], xn[:, s], rstd[:, cols].unsqueeze(2).broadcast_to(shape),
                                   ALU.mult).then_inc(S[ready], 1)

            rstds(0, 0)
            context_low(0, 0)
            rstds(1, 0)

            def project(g, s, _):
                if inside(g + 1, NPAIR):
                    context_low(g + 1, 1 - s)
                if inside(g + 2, NPAIR):
                    rstds(g + 2, 0)

            steps(pool, 0, 2, NPAIR - 2, NPAIR, project)
            pool.memset(vblk_, 0.0).then_inc(S["vblk_zero"], 1)
            pool.wait_ge(S["vblk_zero"], 1)

            def stage_k(t, s, half):
                hold(pool, "k0_kept", half + 2)
                if after(t, 2):
                    hold(pool, "scores_done", 2 * (t - 1))
                src = k0T[:, bass.ds(t * P, P)].rearrange("p (b k) -> p b k", b=2)
                msk = const[:, C_MASK:C_MASK + 4]
                pool.tensor_tensor(kexp[:, s], src.unsqueeze(2).broadcast_to([P, 2, 4, SEQ]),
                                   msk.unsqueeze(1).unsqueeze(3).broadcast_to([P, 2, 4, SEQ]),
                                   ALU.mult).then_inc(S["k_staged"], 1)

            def stage_v(t, s):
                hold(pool, "v0_kept", t + 5)
                if after(t, 2):
                    hold(pool, "pv_done", t - 1)
                src = v0dup[:, bass.ds(t * 2, 2), :].rearrange("p b (j a m) -> p (b j) a m", j=4, a=2)
                dst = vblk[:, s].rearrange("p b (j a) n -> p (b j) a n", a=2)
                for par in range(2):
                    cols = slice(par * 16, par * 16 + 16)
                    own = ones32[:, par, cols].unsqueeze(1).broadcast_to([P, 8, 16])
                    pool.tensor_tensor(dst[:, :, par, cols], src[:, :, par], own,
                                       ALU.mult).then_inc(S["vblk_staged"], 1)

            def split_low(t):
                n, m = UNITS * UW // NT, HC * P // NT
                hold(pool, "w_high", t + 1)
                pool.tensor_tensor(gu_lo[:, bass.ds(t * n, n)], gu_raw[:, bass.ds(t * n, n)],
                                   gu_hi[:, bass.ds(t * n, n)].bitcast(F32), ALU.subtract).then_inc(S["w_low"], 1)
                pool.tensor_tensor(down_lo[:, bass.ds(t * m, m)], down_raw[:, bass.ds(t * m, m)],
                                   down_hi[:, bass.ds(t * m, m)].bitcast(F32), ALU.subtract).then_inc(S["w_low"], 1)

            def attend(t, s, half):
                if inside(t, NT):
                    stage_k(t, s, half)
                if s == 1 and inside(half - 3, NPAIR):
                    rstds(half - 3, 1)
                if inside(t - 1, NT):
                    stage_v(t - 1, 1 - s)
                if inside(t - 2, NT):
                    split_low(t - 2)

            free_meanvar(1)
            steps(pool, 0, 8, NT, NT, attend, 4)
            centre_and_scale(0, 0, 1, "gxn_ready")
            centre_and_scale(1, 1, 1, "gxn_ready")
            for t in range(NT, NT + 6):
                attend(t, t % 2, t // 2)

            def stage_k1(g, s):
                if after(g, 2):
                    hold(pool, "as_done", g - 1)
                pool.tensor_copy(k1s[:, s], k1T[:, pair(g)]).then_inc(S["ak_staged"], 1)

            def norms(g, s, _):
                if inside(g + 2, NPAIR):
                    hold(pool, "gxT_done", g + 1)
                    centre_and_scale(g + 2, s, 1, "gxn_ready")
                if inside(g - 2, NPAIR):
                    rstds(g - 2, 2)

            stage_k1(0, 0)
            stage_k1(1, 1)
            free_meanvar(2)
            steps(pool, 0, 2, NPAIR - 2, NPAIR, norms)
            hold(pool, "gxT_done", NPAIR)
            centre_and_scale(0, 0, 2, "axn_ready")
            centre_and_scale(1, 1, 2, "axn_ready")
            rstds(NPAIR - 2, 2)

            def attend1(g, s, _):
                hold(pool, "axT_done", g - 1)
                centre_and_scale(g, s, 2, "axn_ready")
                stage_k1(g, s)
                if after(g, 4) and not after(g, 5):
                    rstds(NPAIR - 1, 2)
                    free_meanvar(3)
                if after(g, 4):
                    rstds(g - 4, 3)

            steps(pool, 2, 6, NPAIR, NPAIR, attend1)

            def ff_slope(g, s):
                pool.wait_ge(S["glo_done"], g + 1)
                pool.wait_ge(S["ghi_done"], g + 1)
                pool.tensor_tensor(g_hi[:, s], g_hi[:, s], g_lo[:, s], ALU.subtract).then_inc(S["slope_ready"], 1)

            def feed(g, s, _):
                if inside(g, NPAIR):
                    if after(g, 2):
                        hold(pool, "fxT_done", g - 1)
                    centre_and_scale(g, s, 3, "fxn_ready")
                if inside(g - 2, NPAIR):
                    ff_slope(g - 2, s)

            feed(0, 0, 0)
            hold(pool, "axT_done", NPAIR)
            feed(1, 1, 0)
            rstds(NPAIR - 4, 3)
            rstds(NPAIR - 3, 3)
            feed(2, 0, 1)
            rstds(NPAIR - 2, 3)
            feed(3, 1, 1)
            rstds(NPAIR - 1, 3)
            steps(pool, 4, 4, NPAIR, NPAIR + 2, feed)


def kernel(**inputs):
    import concourse.bacc as bacc
    from concourse.bass_utils import run_bass_kernel_spmd

    a = {k: np.asarray(v) for k, v in inputs.items()}

    def tokens_on_partitions(v):
        return v.reshape(NT, P, P).transpose(1, 0, 2)

    def chunks(v):
        return v.reshape(-1, P, v.shape[1]).transpose(1, 0, 2).reshape(P, -1)

    gate = np.concatenate([a["L0_ffn_gate_w"], a["L0_ffn_shared_expert_gate_w"],
                           np.zeros((NGATE - NEXP - 1, P), np.float32)])
    w = np.concatenate([a["L0_xattn_Wq"].T, a["L0_xattn_Wk"].T, a["L1_xattn_Wk"].T, a["L1_xattn_Wq"].T,
                        a["L0_xattn_Wv"].T, a["L1_xattn_Wv"].T, a["L1_ffn_w1"], chunks(a["L1_ffn_w2"]), gate.T], axis=1)
    sg, su = (a[f"L0_ffn_shared_{n}_w"].reshape(-1, INTER, P) for n in ("gate", "up"))
    gu = np.concatenate([a["L0_ffn_experts_gate_up"], np.concatenate([sg, su], axis=1)]).reshape(UNITS * UW, P).T
    down = np.concatenate([a["L0_ffn_experts_down"].transpose(0, 2, 1).reshape(NEXP * INTER, P),
                           a["L0_ffn_shared_down_w"].T, np.zeros((HPAD - UNITS * INTER, P), np.float32)])
    p = np.arange(P)
    mask = (p[:, None] // HD % 4 == np.arange(4)).astype(np.float32)
    tri = np.broadcast_to((np.arange(8)[None, :] < np.arange(8)[:, None]).astype(np.float32).reshape(1, 64), (P, 64))
    ones = (np.arange(64)[None, :] % 32 // HD == 2 * (np.arange(64)[None, :] // 32) + p[:, None] // SEQ).astype(np.float32)
    const = np.concatenate([np.eye(P, dtype=np.float32), a["L0_xattn_Wo"].T,
                            np.broadcast_to(a["L1_xattn_bv"], (P, P)), mask, tri, ones,
                            a["L1_xattn_bq"][:, None], a["L1_xattn_bk"][:, None],
                            a["L1_ffn_b1"].reshape(FC, P).T, a["L1_ffn_b2"][:, None]], axis=1)
    arrays = {
        "in_x": tokens_on_partitions(a["x"]), "in_ctx": a["ctx_1024"].reshape(NT * P, P).T, "in_w": w, "in_gu": gu,
        "in_down": chunks(down), "in_const": const,
    }
    arrays = {k: np.ascontiguousarray(v) for k, v in arrays.items()}
    nc = bacc.Bacc("TRN2", target_bir_lowering=False, num_devices=1)
    args = [nc.dram_tensor(k, v.shape, F32, kind="ExternalInput").ap() for k, v in arrays.items()]
    out = nc.dram_tensor("out_0", (P, NT, P), F32, kind="ExternalOutput").ap()
    two_layers(nc, *args, out)
    r = run_bass_kernel_spmd(nc, [arrays], core_ids=[0])
    return np.ascontiguousarray(r.results[0]["out_0"].transpose(1, 0, 2)).reshape(BATCH, SEQ, P)
```
